# Optimizing a Trainium2 kernel written in Bass

```python
import numpy as np
import jax
import jax.numpy as jnp

def _softmax(x, axis=-1):
    return jax.nn.softmax(x, axis=axis)

def _gelu(x):
    return jax.nn.gelu(x, approximate=True)

def _silu(x):
    return jax.nn.silu(x)

def _sigmoid(x):
    return jax.nn.sigmoid(x)

def _layernorm(x, axis=-1, eps=1e-05):
    m = jnp.mean(x, axis=axis, keepdims=True)
    v = jnp.var(x, axis=axis, keepdims=True)
    return (x - m) / jnp.sqrt(v + eps)

def _scatter_add(tgt, idx, src, axis=0):
    return tgt.at[idx].add(src)

def _segment_sum(src, seg, n):
    return jax.ops.segment_sum(src, seg, n)
kernel_name = 'mk_perceiver_d2_seqx_r8_d9a3dd'

def setup_inputs(seed: int=0):
    np.random.seed(seed)
    _w = jnp.asarray

    def _rec_inputs():
        import jax
        import jax.numpy as jnp
        _rk = jax.random.key(seed)
        x = 7.22e-05 + 1 * jax.random.normal(jax.random.fold_in(_rk, 1), (1, 64, 128), jnp.float32)
        _lenS = 64 - jax.random.randint(jax.random.fold_in(_rk, 7), (1,), 0, max(1, 64 // 4) + 1, jnp.int32)
        _lenS2 = 6272 - jax.random.randint(jax.random.fold_in(_rk, 8), (1,), 0, max(1, 6272 // 4) + 1, jnp.int32)
        _ctx_1024P = jax.random.normal(jax.random.fold_in(_rk, 11), (1, 16, 128), jnp.float32)
        _ctx_1024c = jax.random.dirichlet(jax.random.fold_in(_rk, 511), 0.3 * jnp.ones((16,), jnp.float32), (1, 6272))
        _ctx_1024t = jnp.einsum('bsk,bkd->bsd', _ctx_1024c, _ctx_1024P)
        _ctx_1024t = _ctx_1024t * jax.lax.rsqrt(jnp.mean(jnp.square(_ctx_1024t)) + 1e-12) * 0.953939
        ctx_1024 = 4.13588e-05 + 0.999923 * (_ctx_1024t + 0.3 * jax.random.normal(jax.random.fold_in(_rk, 611), (1, 6272, 128), jnp.float32))
        _validS = jnp.arange(64)[None, :] < _lenS[:, None]
        _validS2 = jnp.arange(6272)[None, :] < _lenS2[:, None]
        _causal = jnp.tril(jnp.ones((64, 64), dtype=bool))
        mask_SxS2_bk0 = jnp.logical_not(jnp.broadcast_to(_validS2[0:1, :], (64, 6272)))
        return (x, ctx_1024, mask_SxS2_bk0)
    x, ctx_1024, mask_SxS2_bk0 = _rec_inputs()

    def _L0_xattn_setup():
        import jax, jax.numpy as jnp
        import numpy as np
        B, S, DIM, H = (4, 256, 128, 16)
        HD = DIM // H
        SCALE = HD ** (-0.5)

        def _heads(x):
            b, s, _ = x.shape
            return x.reshape(b, s, H, HD).transpose(0, 2, 1, 3)
        key = jax.random.key(seed)
        ks = jax.random.split(key, 7)
        init = 0.02
        return {'query': jax.random.normal(ks[0], (B, S, DIM), dtype=jnp.float32), 'key': jax.random.normal(ks[1], (B, S, DIM), dtype=jnp.float32), 'value': jax.random.normal(ks[2], (B, S, DIM), dtype=jnp.float32), 'attn_mask': jnp.tril(jnp.ones((S, S), dtype=bool)), 'Wq': jax.random.normal(ks[3], (DIM, DIM), dtype=jnp.float32) * init, 'Wk': jax.random.normal(ks[4], (DIM, DIM), dtype=jnp.float32) * init, 'Wv': jax.random.normal(ks[5], (DIM, DIM), dtype=jnp.float32) * init, 'Wo': jax.random.normal(ks[6], (DIM, DIM), dtype=jnp.float32) * init}
    _L0_xattn_all = _L0_xattn_setup()
    _L0_xattn_in = {k: v for k, v in _L0_xattn_all.items() if k in ('Wq', 'Wk', 'Wv', 'Wo')}
    del _L0_xattn_all

    def _L0_attn_setup():
        import jax, jax.numpy as jnp
        import numpy as np
        _DENSE_LOCAL_W = 32
        _DYADIC = [48, 64, 96, 128, 192, 32, 48, 64, 96, 128, 192]
        OFFSETS = sorted(set(range(_DENSE_LOCAL_W + 1)) | set(_DYADIC))
        B, N, D, H = (2, 512, 128, 16)
        HD = D // H
        NEG = -1e+30

        def _shift(t, o):
            if o == 0:
                return t
            n = t.shape[2]
            return jnp.pad(t, ((0, 0), (0, 0), (o, 0), (0, 0)))[:, :, :n]
        key = jax.random.key(seed)
        ks = jax.random.split(key, 9)
        alphas = jnp.linspace(0.2, 2.0, H)
        delta = jnp.log1p(jnp.asarray(OFFSETS, dtype=jnp.float32))
        pos_bias = -delta[:, None] * alphas[None, :]
        return {'x': jax.random.normal(ks[0], (B, N, D), jnp.float32), 'qkv_w': jax.random.normal(ks[1], (3 * D, D), jnp.float32) * 0.02, 'qkv_b': jax.random.normal(ks[2], (3 * D,), jnp.float32) * 0.01, 'out_w': jax.random.normal(ks[3], (D, D), jnp.float32) * 0.02, 'out_b': jnp.zeros((D,), jnp.float32), 'gate_w': jax.random.normal(ks[4], (D, D), jnp.float32) * 0.02, 'gate_b': jnp.zeros((D,), jnp.float32), 'pos_bias': pos_bias, 'scale_embed': jax.random.normal(ks[5], (len(OFFSETS), HD), jnp.float32) * 0.02, 'if_gain': 1.0 + jax.random.normal(ks[6], (H,), jnp.float32) * 0.05}
    _L0_attn_all = _L0_attn_setup()
    _L0_attn_in = {k: v for k, v in _L0_attn_all.items() if k in ('qkv_w', 'qkv_b', 'out_w', 'out_b', 'gate_w', 'gate_b', 'pos_bias', 'scale_embed', 'if_gain')}
    del _L0_attn_all

    def _L0_ffn_setup():
        import jax, jax.numpy as jnp
        import numpy as np
        E = 16
        H = 128
        F = 256
        TOP_K = 1
        B, S = (2, 128)
        key = jax.random.key(seed)
        ks = jax.random.split(key, 7)
        s = 0.02
        return {'hidden_states': jax.random.normal(ks[0], (B, S, H), jnp.float32), 'w_router': jax.random.normal(ks[1], (E, H), jnp.float32) * s, 'gate_up_proj': jax.random.normal(ks[2], (E, H, 2 * F), jnp.float32) * s, 'down_proj': jax.random.normal(ks[3], (E, F, H), jnp.float32) * s, 'w_gate': jax.random.normal(ks[4], (F, H), jnp.float32) * s, 'w_up': jax.random.normal(ks[5], (F, H), jnp.float32) * s, 'w_down': jax.random.normal(ks[6], (H, F), jnp.float32) * s}
    _L0_ffn_all = _L0_ffn_setup()
    _L0_ffn_in = {k: v for k, v in _L0_ffn_all.items() if k in ('w_router', 'gate_up_proj', 'down_proj', 'w_gate', 'w_up', 'w_down')}
    del _L0_ffn_all

    def _L1_xattn_setup():
        import jax, jax.numpy as jnp
        import numpy as np
        EMBED_DIM = 128
        NUM_HEADS = 16
        HEAD_DIM = EMBED_DIM // NUM_HEADS
        SCALE = HEAD_DIM ** (-0.5)
        key = jax.random.key(seed)
        ks = jax.random.split(key, 12)
        B, S, D = (1, 512, EMBED_DIM)
        w_std = D ** (-0.5)
        return {'query': jax.random.normal(ks[0], (B, S, D), dtype=jnp.float32), 'key': jax.random.normal(ks[1], (B, S, D), dtype=jnp.float32), 'value': jax.random.normal(ks[2], (B, S, D), dtype=jnp.float32), 'Wq': jax.random.normal(ks[3], (D, D), dtype=jnp.float32) * w_std, 'bq': jax.random.normal(ks[4], (D,), dtype=jnp.float32) * 0.01, 'Wk': jax.random.normal(ks[5], (D, D), dtype=jnp.float32) * w_std, 'bk': jax.random.normal(ks[6], (D,), dtype=jnp.float32) * 0.01, 'Wv': jax.random.normal(ks[7], (D, D), dtype=jnp.float32) * w_std, 'bv': jax.random.normal(ks[8], (D,), dtype=jnp.float32) * 0.01, 'Wo': jax.random.normal(ks[9], (D, D), dtype=jnp.float32) * w_std, 'bo': jax.random.normal(ks[10], (D,), dtype=jnp.float32) * 0.01}
    _L1_xattn_all = _L1_xattn_setup()
    _L1_xattn_in = {k: v for k, v in _L1_xattn_all.items() if k in ('Wq', 'bq', 'Wk', 'bk', 'Wv', 'bv', 'Wo', 'bo')}
    del _L1_xattn_all

    def _L1_attn_setup():
        import jax, jax.numpy as jnp
        import numpy as np
        HIDDEN = 128
        HEADS = 16
        HEAD = HIDDEN // HEADS

        def _ternary_weight(key, shape):
            g = jax.random.normal(key, shape, dtype=jnp.float32)
            return jnp.where(jnp.abs(g) < 0.6, 0.0, jnp.sign(g)).astype(jnp.float32)

        def _tlin(x, w, s, b):
            return jnp.einsum('bsh,oh->bso', x, w) * s + b
        key = jax.random.key(seed)
        ks = jax.random.split(key, 10)
        x = jax.random.normal(ks[0], (2, 256, HIDDEN), dtype=jnp.float32)
        d = {'x': x}
        names = ['q', 'k', 'v', 'o']
        for i, n in enumerate(names):
            d[f'w_{n}'] = _ternary_weight(ks[1 + i], (HIDDEN, HIDDEN))
            d[f's_{n}'] = jnp.float32(0.02)
            d[f'b_{n}'] = jax.random.normal(ks[5 + i], (HIDDEN,), dtype=jnp.float32) * 0.02
        return d
    _L1_attn_all = _L1_attn_setup()
    _L1_attn_in = {k: v for k, v in _L1_attn_all.items() if k in ('w_q', 's_q', 'b_q', 'w_k', 's_k', 'b_k', 'w_v', 's_v', 'b_v', 'w_o', 's_o', 'b_o')}
    del _L1_attn_all

    def _L1_ffn_setup():
        import jax, jax.numpy as jnp
        import numpy as np
        B, S, D, H, E = (64, 128, 128, 64, 8)
        EPS = 1e-05
        key = jax.random.key(seed)
        ks = jax.random.split(key, 8)
        x = jax.random.normal(ks[0], (B, S, D), jnp.float32)
        return {'x': x, 'ln_g': jnp.ones((D,), jnp.float32), 'ln_b': jnp.zeros((D,), jnp.float32), 'bn_g': jnp.ones((D,), jnp.float32), 'bn_b': jnp.zeros((D,), jnp.float32), 'bn_mean': jax.random.normal(ks[1], (D,), jnp.float32) * 0.01, 'bn_var': jnp.ones((D,), jnp.float32), 'Wr': jax.random.normal(ks[2], (D, E), jnp.float32) * 0.02, 'br': jnp.zeros((E,), jnp.float32), 'W_down': jax.random.normal(ks[3], (E, D, H), jnp.float32) * 0.02, 'b_down': jnp.zeros((E, H), jnp.float32), 'W_up': jax.random.normal(ks[4], (E, H, D), jnp.float32) * 0.02, 'b_up': jnp.zeros((E, D), jnp.float32)}
    _L1_ffn_all = _L1_ffn_setup()
    _L1_ffn_in = {k: v for k, v in _L1_ffn_all.items() if k in ('ln_g', 'ln_b', 'bn_g', 'bn_b', 'bn_mean', 'bn_var', 'Wr', 'br', 'W_down', 'b_down', 'W_up', 'b_up')}
    del _L1_ffn_all
    return {'x': x, 'ctx_1024': ctx_1024, 'mask_SxS2_bk0': mask_SxS2_bk0, 'L0_xattn_Wq': _L0_xattn_in['Wq'], 'L0_xattn_Wk': _L0_xattn_in['Wk'], 'L0_xattn_Wv': _L0_xattn_in['Wv'], 'L0_xattn_Wo': _L0_xattn_in['Wo'], 'L0_attn_qkv_w': _L0_attn_in['qkv_w'], 'L0_attn_qkv_b': _L0_attn_in['qkv_b'], 'L0_attn_out_w': _L0_attn_in['out_w'], 'L0_attn_out_b': _L0_attn_in['out_b'], 'L0_attn_gate_w': _L0_attn_in['gate_w'], 'L0_attn_gate_b': _L0_attn_in['gate_b'], 'L0_attn_pos_bias': _L0_attn_in['pos_bias'], 'L0_attn_scale_embed': _L0_attn_in['scale_embed'], 'L0_attn_if_gain': _L0_attn_in['if_gain'], 'L0_ffn_w_router': _L0_ffn_in['w_router'], 'L0_ffn_gate_up_proj': _L0_ffn_in['gate_up_proj'], 'L0_ffn_down_proj': _L0_ffn_in['down_proj'], 'L0_ffn_w_gate': _L0_ffn_in['w_gate'], 'L0_ffn_w_up': _L0_ffn_in['w_up'], 'L0_ffn_w_down': _L0_ffn_in['w_down'], 'L1_xattn_Wq': _L1_xattn_in['Wq'], 'L1_xattn_bq': _L1_xattn_in['bq'], 'L1_xattn_Wk': _L1_xattn_in['Wk'], 'L1_xattn_bk': _L1_xattn_in['bk'], 'L1_xattn_Wv': _L1_xattn_in['Wv'], 'L1_xattn_bv': _L1_xattn_in['bv'], 'L1_xattn_Wo': _L1_xattn_in['Wo'], 'L1_xattn_bo': _L1_xattn_in['bo'], 'L1_attn_w_q': _L1_attn_in['w_q'], 'L1_attn_s_q': _L1_attn_in['s_q'], 'L1_attn_b_q': _L1_attn_in['b_q'], 'L1_attn_w_k': _L1_attn_in['w_k'], 'L1_attn_s_k': _L1_attn_in['s_k'], 'L1_attn_b_k': _L1_attn_in['b_k'], 'L1_attn_w_v': _L1_attn_in['w_v'], 'L1_attn_s_v': _L1_attn_in['s_v'], 'L1_attn_b_v': _L1_attn_in['b_v'], 'L1_attn_w_o': _L1_attn_in['w_o'], 'L1_attn_s_o': _L1_attn_in['s_o'], 'L1_attn_b_o': _L1_attn_in['b_o'], 'L1_ffn_ln_g': _L1_ffn_in['ln_g'], 'L1_ffn_ln_b': _L1_ffn_in['ln_b'], 'L1_ffn_bn_g': _L1_ffn_in['bn_g'], 'L1_ffn_bn_b': _L1_ffn_in['bn_b'], 'L1_ffn_bn_mean': _L1_ffn_in['bn_mean'], 'L1_ffn_bn_var': _L1_ffn_in['bn_var'], 'L1_ffn_Wr': _L1_ffn_in['Wr'], 'L1_ffn_br': _L1_ffn_in['br'], 'L1_ffn_W_down': _L1_ffn_in['W_down'], 'L1_ffn_b_down': _L1_ffn_in['b_down'], 'L1_ffn_W_up': _L1_ffn_in['W_up'], 'L1_ffn_b_up': _L1_ffn_in['b_up']}

def reference(x, ctx_1024, mask_SxS2_bk0, L0_xattn_Wq, L0_xattn_Wk, L0_xattn_Wv, L0_xattn_Wo, L0_attn_qkv_w, L0_attn_qkv_b, L0_attn_out_w, L0_attn_out_b, L0_attn_gate_w, L0_attn_gate_b, L0_attn_pos_bias, L0_attn_scale_embed, L0_attn_if_gain, L0_ffn_w_router, L0_ffn_gate_up_proj, L0_ffn_down_proj, L0_ffn_w_gate, L0_ffn_w_up, L0_ffn_w_down, L1_xattn_Wq, L1_xattn_bq, L1_xattn_Wk, L1_xattn_bk, L1_xattn_Wv, L1_xattn_bv, L1_xattn_Wo, L1_xattn_bo, L1_attn_w_q, L1_attn_s_q, L1_attn_b_q, L1_attn_w_k, L1_attn_s_k, L1_attn_b_k, L1_attn_w_v, L1_attn_s_v, L1_attn_b_v, L1_attn_w_o, L1_attn_s_o, L1_attn_b_o, L1_ffn_ln_g, L1_ffn_ln_b, L1_ffn_bn_g, L1_ffn_bn_b, L1_ffn_bn_mean, L1_ffn_bn_var, L1_ffn_Wr, L1_ffn_br, L1_ffn_W_down, L1_ffn_b_down, L1_ffn_W_up, L1_ffn_b_up):
    import jax
    import jax.numpy as jnp

    def _L0_xattn_ref(query, key, value, attn_mask, Wq, Wk, Wv, Wo):
        import jax, jax.numpy as jnp
        import numpy as np
        B, S, DIM, H = (4, 256, 128, 16)
        HD = DIM // H
        SCALE = HD ** (-0.5)

        def _heads(x):
            b, s, _ = x.shape
            return x.reshape(b, s, H, HD).transpose(0, 2, 1, 3)
        q = _heads(query @ Wq.T)
        k = _heads(key @ Wk.T)
        v = _heads(value @ Wv.T)
        logits = jnp.einsum('bhqd,bhkd->bhqk', q, k) * SCALE
        mask = attn_mask[None, None, :, :]
        masked = jnp.where(mask, logits, -1000000000.0)
        weights = jax.nn.softmax(masked, axis=-1)
        weights = weights * mask.astype(weights.dtype)
        denom = jnp.maximum(weights.sum(axis=-1, keepdims=True), 1e-09)
        weights = weights / denom
        out = jnp.einsum('bhqk,bhkd->bhqd', weights, v)
        out = out.transpose(0, 2, 1, 3).reshape(query.shape[0], query.shape[1], -1)
        return out @ Wo.T

    def _L0_attn_ref(x, qkv_w, qkv_b, out_w, out_b, gate_w, gate_b, pos_bias, scale_embed, if_gain):
        import jax, jax.numpy as jnp
        import numpy as np
        _DENSE_LOCAL_W = 32
        _DYADIC = [48, 64, 96, 128, 192, 32, 48, 64, 96, 128, 192]
        OFFSETS = sorted(set(range(_DENSE_LOCAL_W + 1)) | set(_DYADIC))
        B, N, D, H = (2, 512, 128, 16)
        HD = D // H
        NEG = -1e+30

        def _shift(t, o):
            if o == 0:
                return t
            n = t.shape[2]
            return jnp.pad(t, ((0, 0), (0, 0), (o, 0), (0, 0)))[:, :, :n]
        b, n, d = x.shape
        qkv = x @ qkv_w.T + qkv_b
        q, k, v = jnp.split(qkv, 3, axis=-1)
        heads = lambda t: t.reshape(b, n, H, HD).transpose(0, 2, 1, 3)
        q, k, v = (heads(q), heads(k), heads(v))
        inv = 1.0 / jnp.sqrt(jnp.asarray(HD, x.dtype))
        qs = jnp.einsum('bhnd,od->bhno', q, scale_embed)
        pos = jnp.arange(n)
        logits = []
        for i, o in enumerate(OFFSETS):
            qk = jnp.einsum('bhnd,bhnd->bhn', q, _shift(k, o))
            lg = qk * inv * (1.0 + qs[..., i]) + pos_bias[i][None, :, None]
            lg = jnp.where(pos[None, None, :] >= o, lg, NEG)
            logits.append(lg)
        logits = jnp.stack(logits, axis=-1)
        p = jax.nn.softmax(logits, axis=-1)
        out = jnp.zeros_like(q)
        for i, o in enumerate(OFFSETS):
            out = out + p[..., i][..., None] * _shift(v, o)
        out = out * if_gain[None, :, None, None]
        out_flat = out.transpose(0, 2, 1, 3).reshape(b, n, d)
        gate = jax.nn.sigmoid(x @ gate_w.T + gate_b)
        return out_flat * gate @ out_w.T + out_b

    def _L0_ffn_ref(hidden_states, w_router, gate_up_proj, down_proj, w_gate, w_up, w_down):
        import jax, jax.numpy as jnp
        import numpy as np
        E = 16
        H = 128
        F = 256
        TOP_K = 1
        B, S = (2, 128)
        b, s, h = hidden_states.shape
        x = hidden_states.reshape(-1, h)
        logits = x @ w_router.T
        _, top_idx = jax.lax.top_k(logits, TOP_K)
        mask = jax.nn.one_hot(top_idx, E, dtype=logits.dtype).sum(axis=1)
        scores = jax.nn.sigmoid(logits) * mask
        masked_inputs = scores.T[:, :, None] * x[None, :, :]
        gate_up = jnp.einsum('eth,ehf->etf', masked_inputs, gate_up_proj)
        gate, up = jnp.split(gate_up, 2, axis=-1)
        expert_out = jnp.einsum('etf,efh->eth', up * jax.nn.silu(gate), down_proj)
        shared = jax.nn.silu(x @ w_gate.T) * (x @ w_up.T) @ w_down.T
        out = shared + expert_out.sum(axis=0)
        return out.reshape(b, s, h)

    def _L1_xattn_ref(query, key, value, Wq, bq, Wk, bk, Wv, bv, Wo, bo):
        import jax, jax.numpy as jnp
        import numpy as np
        EMBED_DIM = 128
        NUM_HEADS = 16
        HEAD_DIM = EMBED_DIM // NUM_HEADS
        SCALE = HEAD_DIM ** (-0.5)
        B, Sq, D = query.shape
        Skv = key.shape[1]
        H, Hd = (NUM_HEADS, HEAD_DIM)
        q = (query @ Wq.T + bq).reshape(B, Sq, H, Hd).transpose(0, 2, 1, 3)
        k = (key @ Wk.T + bk).reshape(B, Skv, H, Hd).transpose(0, 2, 1, 3)
        v = (value @ Wv.T + bv).reshape(B, Skv, H, Hd).transpose(0, 2, 1, 3)
        q = q * SCALE
        scores = jnp.einsum('bhqd,bhkd->bhqk', q, k)
        attn = jax.nn.softmax(scores, axis=-1)
        out = jnp.einsum('bhqk,bhkd->bhqd', attn, v)
        out = out.transpose(0, 2, 1, 3).reshape(B, Sq, D)
        return out @ Wo.T + bo

    def _L1_attn_ref(x, w_q, s_q, b_q, w_k, s_k, b_k, w_v, s_v, b_v, w_o, s_o, b_o):
        import jax, jax.numpy as jnp
        import numpy as np
        HIDDEN = 128
        HEADS = 16
        HEAD = HIDDEN // HEADS

        def _ternary_weight(key, shape):
            g = jax.random.normal(key, shape, dtype=jnp.float32)
            return jnp.where(jnp.abs(g) < 0.6, 0.0, jnp.sign(g)).astype(jnp.float32)

        def _tlin(x, w, s, b):
            return jnp.einsum('bsh,oh->bso', x, w) * s + b
        B, S, H = x.shape

        def split_heads(t):
            return t.reshape(B, S, HEADS, HEAD).transpose(0, 2, 1, 3)
        q = split_heads(_tlin(x, w_q, s_q, b_q))
        k = split_heads(_tlin(x, w_k, s_k, b_k))
        v = split_heads(_tlin(x, w_v, s_v, b_v))
        scores = jnp.einsum('bhqd,bhkd->bhqk', q, k) / jnp.sqrt(jnp.float32(HEAD))
        attn = jax.nn.softmax(scores, axis=-1)
        ctx = jnp.einsum('bhqk,bhkd->bhqd', attn, v)
        ctx = ctx.transpose(0, 2, 1, 3).reshape(B, S, H)
        return _tlin(ctx, w_o, s_o, b_o)

    def _L1_ffn_ref(x, ln_g, ln_b, bn_g, bn_b, bn_mean, bn_var, Wr, br, W_down, b_down, W_up, b_up):
        import jax, jax.numpy as jnp
        import numpy as np
        B, S, D, H, E = (64, 128, 128, 64, 8)
        EPS = 1e-05
        mu = jnp.mean(x, axis=-1, keepdims=True)
        var = jnp.var(x, axis=-1, keepdims=True)
        z = (x - mu) * jax.lax.rsqrt(var + EPS) * ln_g + ln_b
        z_sent = jnp.mean(z, axis=1)
        z_bn = (z_sent - bn_mean) * jax.lax.rsqrt(bn_var + EPS) * bn_g + bn_b
        probs = jax.nn.softmax(z_bn @ Wr + br, axis=-1)
        idx = jnp.argmax(probs, axis=-1)
        gate = jnp.take_along_axis(probs, idx[:, None], axis=1)[:, 0]
        h = jax.nn.relu(jnp.einsum('bsd,bdh->bsh', z, W_down[idx]) + b_down[idx][:, None, :])
        y = jnp.einsum('bsh,bhd->bsd', h, W_up[idx]) + b_up[idx][:, None, :]
        return y * gate[:, None, None]
    x = x + _L0_xattn_ref(_layernorm(x, axis=-1), ctx_1024, ctx_1024, mask_SxS2_bk0, L0_xattn_Wq, L0_xattn_Wk, L0_xattn_Wv, L0_xattn_Wo)
    x = x + _L0_attn_ref(_layernorm(x, axis=-1), L0_attn_qkv_w, L0_attn_qkv_b, L0_attn_out_w, L0_attn_out_b, L0_attn_gate_w, L0_attn_gate_b, L0_attn_pos_bias, L0_attn_scale_embed, L0_attn_if_gain)
    x = x + _L0_ffn_ref(_layernorm(x, axis=-1), L0_ffn_w_router, L0_ffn_gate_up_proj, L0_ffn_down_proj, L0_ffn_w_gate, L0_ffn_w_up, L0_ffn_w_down)
    x = x + _L1_xattn_ref(_layernorm(x, axis=-1), ctx_1024, ctx_1024, L1_xattn_Wq, L1_xattn_bq, L1_xattn_Wk, L1_xattn_bk, L1_xattn_Wv, L1_xattn_bv, L1_xattn_Wo, L1_xattn_bo)
    x = x + _L1_attn_ref(_layernorm(x, axis=-1), L1_attn_w_q, L1_attn_s_q, L1_attn_b_q, L1_attn_w_k, L1_attn_s_k, L1_attn_b_k, L1_attn_w_v, L1_attn_s_v, L1_attn_b_v, L1_attn_w_o, L1_attn_s_o, L1_attn_b_o)
    x = x + _L1_ffn_ref(_layernorm(x, axis=-1), L1_ffn_ln_g, L1_ffn_ln_b, L1_ffn_bn_g, L1_ffn_bn_b, L1_ffn_bn_mean, L1_ffn_bn_var, L1_ffn_Wr, L1_ffn_br, L1_ffn_W_down, L1_ffn_b_down, L1_ffn_W_up, L1_ffn_b_up)
    return x

_drawn_inputs = setup_inputs


def setup_inputs(seed=0):
    import zlib

    import numpy as np

    out = dict(_drawn_inputs(seed))
    spreads = {'L0_attn_out_b': (0.0, 0.1),
     'L0_attn_gate_b': (0.0, 0.8),
     'L1_ffn_ln_g': (1.0, 0.6),
     'L1_ffn_ln_b': (0.0, 0.8),
     'L1_ffn_bn_g': (1.0, 0.6),
     'L1_ffn_bn_b': (0.0, 2.0),
     'L1_ffn_bn_var': (1.0, 0.6),
     'L1_ffn_br': (0.0, 0.8),
     'L1_ffn_b_down': (0.0, 0.8),
     'L1_ffn_b_up': (0.0, 0.678)}
    factors = {'L0_xattn_Wq': 8.0,
     'L0_xattn_Wk': 8.0,
     'L0_attn_qkv_w': 5.165,
     'L0_attn_qkv_b': 8.0,
     'L0_attn_out_w': 5.272,
     'L0_attn_gate_w': 8.0,
     'L0_attn_pos_bias': 6.455,
     'L0_attn_scale_embed': 8.0,
     'L0_attn_if_gain': 8.0,
     'L0_ffn_w_router': 8.0,
     'L0_ffn_gate_up_proj': 8.0,
     'L0_ffn_down_proj': 8.0,
     'L0_ffn_w_gate': 7.226,
     'L0_ffn_w_up': 7.306,
     'L0_ffn_w_down': 7.393,
     'L1_xattn_bq': 200.0,
     'L1_xattn_bk': 200.0,
     'L1_xattn_bv': 44.149,
     'L1_xattn_bo': 44.414,
     'L1_attn_w_q': 8.0,
     'L1_attn_b_q': 64.0,
     'L1_attn_w_k': 8.0,
     'L1_attn_b_k': 200.0,
     'L1_attn_w_v': 5.17,
     'L1_attn_b_v': 34.297,
     'L1_attn_w_o': 4.819,
     'L1_attn_b_o': 23.418,
     'L1_ffn_bn_mean': 64.0,
     'L1_ffn_Wr': 4.028,
     'L1_ffn_W_down': 8.0,
     'L1_ffn_W_up': 8.0}
    for name, (base, spread) in spreads.items():
        noise = np.random.default_rng([zlib.crc32(name.encode()), seed]).standard_normal(out[name].shape)
        drawn = base * np.exp(spread * noise) if base else spread * noise
        out[name] = jnp.asarray(drawn.astype(out[name].dtype))
    for name, factor in factors.items():
        out[name] = (out[name] * factor).astype(out[name].dtype)
    return out
```

```python
from contextlib import ExitStack

import concourse.bass as bass
from concourse import mybir

F32 = mybir.dt.float32
BF16 = mybir.dt.bfloat16
U8 = mybir.dt.uint8
ALU = mybir.AluOpType
ACT = mybir.ActivationFunctionType
AX = mybir.AxisListType

P = 128
D = 128
H = 16
HD = D // H
NQ = 64
NK = 6272
NKT = NK // P
PAIRS = H // 2
STEPS = 7
TPS = NKT // STEPS
SW = TPS * P
CW = SW // 2
NCH = NK // CW
K_TERM = (0, 0, 0, 1, 1, 2)
Q_TERM = (0, 1, 2, 0, 1, 0)
TERMS = len(K_TERM)
ROWS = TERMS * 2 * HD
MROW = ROWS
VC = 2 * HD + 1
SCALE = HD ** -0.5
MASKED = -1e9
CHUNKS = (3, 3, 3, 2, 2, 1, 0)
PORTIONS = ((0, 4), (4, 7))
E0, F0 = 16, 256
E1, F1 = 8, 64
NEG = -1e30
LN_EPS = 1e-5


def pack_layout():
    first = [("ident", P, P), ("hmask", H, P), ("sel", 5, ROWS), ("sum4", VC, P),
             ("eps", 1, P), ("tie", E0, P), ("zero", 1, P),
             ("wk0", D, D), ("wq0", PAIRS * ROWS, D), ("wv0", D, D)]
    second = [("wo0", 2 * D, NQ), ("wk1", D, D), ("wq1", PAIRS * ROWS, D), ("wv1", D, D), ("wo1", 2 * D, NQ),
              ("bk1", 1, D), ("bq1", PAIRS, ROWS), ("bv1", PAIRS * HD, P), ("bo1", D, NQ),
              ("a0_wq", D, D), ("a0_wk", D, D), ("a0_wv", D, D), ("a0_bq", 1, D), ("a0_bk", 1, D),
              ("a0_bv", D, P), ("a0_se", NQ, D), ("a0_gw", D, D), ("a0_gb", 1, D), ("a0_gain", H // 2, P),
              ("a0_wo", D, D), ("a0_bo", D, NQ),
              ("f0_router", E0, D), ("f0_shared", 2 * F0, D), ("f0_wd", 2 * D, P),
              ("a1_wq", D, D), ("a1_wk", D, D), ("a1_wv", D, D), ("a1_wo", D, D),
              ("a1_s", 4, P), ("a1_bq", 1, D), ("a1_bk", 1, D), ("a1_bv", D, P), ("a1_bo", D, NQ),
              ("f1_lng", D, NQ), ("f1_lnb", D, NQ), ("f1_bn", 4, D), ("f1_wr", E1, D), ("f1_br", E1, P),
              ("f1_wd", F1 * E1, D), ("f1_bd", E1, F1), ("f1_wu", D * E1, F1), ("f1_bu", D * E1, NQ)]
    out = []
    for lot in (first, second):
        at, cols = 0, {}
        for name, n, rows in lot:
            cols[name] = (at, n, rows)
            at += n
        out.append((cols, at))
    return out


def skew_back(skew, g):
    return bass.AP(tensor=skew.tensor, offset=g * (H // 2) * NQ + NQ - 1, ap=[[H * NQ - 1, NQ], [NQ, H // 2], [1, NQ]])


def bias_rows(bias, g):
    return bass.AP(tensor=bias.tensor, offset=g * (H // 2) * P + NQ - 1, ap=[[H * P - 1, NQ], [P, H // 2], [1, NQ]])


def perceiver(nc, x_in, ctx_in, mask_in, pack1_in, pack2_in, bias_in, gup_in, down_in, skew, x_out):
    (cols1, n1), (cols2, n2) = pack_layout()
    with ExitStack() as stack:
        def sb(name, shape, dt=F32):
            return stack.enter_context(nc.sbuf_tensor(name, shape, dt))

        def pb(name, shape):
            return stack.enter_context(nc.psum_tensor(name, shape, F32))

        def sem(name):
            return stack.enter_context(nc.semaphore(name))

        ctxT = sb("ctxT", [P, NK])
        kpart = sb("kpart", [P, 3, NK], BF16)
        kstack = sb("kstack", [P, 2, NK], BF16)
        vones = sb("vones", [P, NKT, PAIRS, VC])
        pack1 = sb("pack1", [P, n1])
        pack2 = sb("pack2", [P, n2])
        shared = sb("shared", [P, E0 * 2 * F0])
        gup = shared[:, :].rearrange("p (e f) -> p e f", e=E0)
        at = 0

        def part(n):
            nonlocal at
            at += n
            return shared[:, at - n:at]

        maskadd = part(NK // 2).bitcast(BF16)
        probs = part(2 * SW).rearrange("p (b n) -> p b n", b=2)
        vcur = part(2 * NKT * VC).rearrange("p (b t c) -> p b t c", b=2, t=NKT)
        junk = part(2 * CW).rearrange("p (b n) -> p b n", b=2)
        assert at <= E0 * 2 * F0
        mask_u8 = probs.rearrange("p b n -> p (b n)").bitcast(U8)[:, 0:NK]
        kres = sb("kres", [P, 2, CW])
        qstack = sb("qstack", [P, PAIRS, 2, NQ], BF16)
        qmax = sb("qmax", [P, 2, P], BF16)
        qexp = sb("qexp", [P, 2, P], BF16)
        identb = sb("identb", [P, P], BF16)
        qf = sb("qf", [P, PAIRS * NQ])
        qh = sb("qh", [P, PAIRS * NQ], BF16)
        qm = sb("qm", [P, PAIRS * NQ], BF16)
        ql = sb("ql", [P, PAIRS * NQ], BF16)
        mx = sb("mx", [P, 2, NCH])
        negm = sb("negm", [P, 4])
        m3 = sb("m3", [P, 4], BF16)
        acc_sb = sb("acc_sb", [P, P])
        o17 = sb("o17", [P, PAIRS, VC])
        den = sb("den", [P, PAIRS])
        rden = sb("rden", [P, PAIRS])
        onorm = sb("onorm", [P, PAIRS, HD])
        oT = sb("oT", [NQ, P])
        x = sb("x", [NQ, D])
        st = sb("st", [P, 6])
        mv = sb("mv", [P, 2])
        lnv = sb("lnv", [P, 1])
        rstd = sb("rstd", [P, 1])
        xn = sb("xn", [NQ, D])
        xz = sb("xz", [NQ, D])
        xnT = sb("xnT", [P, 2, NQ])
        big = sb("big", [P, H * NQ])
        big2 = sb("big2", [P, H * NQ])
        w512 = sb("w512", [P, 512])
        v512 = sb("v512", [P, 512])
        qr, qc = w512, v512
        rest = kstack[:, :, :].rearrange("p b n -> p (b n)").bitcast(F32)
        down = rest[:, 0:2 * E0 * D].rearrange("p (f e n) -> p f e n", f=2, e=E0)
        qT = sb("qT", [P, NQ])
        kT = sb("kT", [P, NQ])
        vbd = rest[:, 2 * E0 * D:2 * E0 * D + PAIRS * D].rearrange("p (a n) -> p a n", a=PAIRS)
        ogT = sb("ogT", [P, NQ])
        gt = sb("gt", [P, NQ])
        ngb = sb("ngb", [P, 1])
        bnr = sb("bnr", [P, 2])
        bias_t = sb("bias_t", [P, 512])
        red = sb("red", [P, H])
        red2 = sb("red2", [P, H])
        small = sb("small", [P, 16])
        onehot = sb("onehot", [P, E0])
        onehot2 = sb("onehot2", [P, E0])

        def w(name):
            cols, pack = (cols1, pack1) if name in cols1 else (cols2, pack2)
            c, n, rows = cols[name]
            return pack[0:rows, c:c + n]

        ident = w("ident")
        routing = big[:, :].rearrange("p (e t) -> p e t", e=E0)

        smax = [pb(f"smax{b}", [P, 512]) for b in range(2)]
        sexp = [pb(f"sexp{b}", [P, 1024]) for b in range(2)]
        acc = pb("acc", [P, 512])
        misc = pb("misc", [P, 512])

        NAMES = """x_in pack1_in pack2_in mask_in gup_in down_in se_out se_in bias_in x_out
            mask_ready identb_ready ones_ready act_chain dve_chain pool_chain
            ln_var ln_rstd ln_xn ln_xt xt_ready""".split()
        S = {n: sem(n) for n in NAMES}
        ctx_landed = [sem(f"ctx_landed{g}") for g in range(STEPS)]
        LNAMES = """qrep_done qstack_ready kproj_done khigh_done kproj_taken kmid_done klow_done
            vproj_done vproj_taken qmax_ready qexp_ready vcur_ready
            smax_done smax_taken m3_ready mt_done qm_ready sexp_done exp_done pv_done
            acc_copied sum_done o17_taken on_ready ot_done ot_ready y_done passed pool_passed mx_chain""".split()
        LS = [{n: sem(f"{n}_{L}") for n in LNAMES} for L in range(2)]
        stack_landed = [[[sem(f"stack_landed_{L}_{b}_{h}") for h in range(len(PORTIONS))] for b in range(2)] for L in range(2)]
        T = {n: sem(n) for n in """se_bd kbd_ready qkv_done qk_ready v_ready s_done se_done se_taken
            t_ready exp_ready exps p_ready pt_done pt_ready ot2_done gate_e og_ready y2_done x2_ready
            r_done r_e route_ready xm_done xm_ready h_done h_e a_ready at_done at_ready yf_done xf_ready
            b_qkv_done b_kbd_ready b_v_ready b_s_done b_exp_ready b_exps b_p_ready b_pt_done b_pt_ready
            b_ot_done b_og_ready b_y_done b_x_ready
            z_ready bn_rs zb_ready g_done g_ready g_e oh_ready ohb_done wsel_ready
            zt_done zt_ready h1_done h1_ready y1_done out_ready""".split()}

        block = stack.enter_context(nc.Block())

        @block.sync
        def _(sp):
            sp.dma_start(x[:, :], x_in).then_inc(S["x_in"], 16)
            sp.dma_start(pack1[:, :], pack1_in).then_inc(S["pack1_in"], 16)
            for g in range(STEPS):
                sp.dma_start(ctxT[:, g * SW:(g + 1) * SW], ctx_in[:, g * SW:(g + 1) * SW]).then_inc(ctx_landed[g], 16)
            sp.dma_start(mask_u8[0:NQ, :], mask_in).then_inc(S["mask_in"], 16)
            sp.dma_start(mask_u8[NQ:P, :], mask_in).then_inc(S["mask_in"], 16)
            sp.dma_start(pack2[:, :], pack2_in).then_inc(S["pack2_in"], 16)

            def refill(L, p):
                for h, (a, b) in enumerate(PORTIONS):
                    if p >= 2:
                        sp.wait_ge(LS[L]["sexp_done"], STEPS * (p - 2) + b)
                    elif h == 0 and p == 0:
                        sp.wait_ge(LS[L]["klow_done"], NCH)
                    for t, k in enumerate(K_TERM):
                        sp.dma_start(kstack[t * 16:t * 16 + 16, p % 2, a * SW:b * SW],
                                     kpart[p * 16:p * 16 + 16, k, a * SW:b * SW]
                                     ).then_inc(stack_landed[L][p % 2][h], 16)

            for p in range(PAIRS):
                refill(0, p)
            sp.wait_ge(LS[0]["pv_done"], PAIRS * STEPS + 2)
            sp.wait_ge(LS[0]["smax_taken"], PAIRS * NCH)
            sp.dma_start(gup, gup_in).then_inc(S["gup_in"], 16)
            sp.dma_start(down, down_in).then_inc(S["down_in"], 16)
            sp.wait_ge(T["se_taken"], 1)
            sp.dma_start(skew.rearrange("(q n) -> q n", q=NQ), big2[0:NQ, :]).then_inc(S["se_out"], 16)
            sp.wait_ge(S["se_out"], 16)
            for g in range(2):
                sp.dma_start(qf[g * NQ:(g + 1) * NQ, :].rearrange("p (h j) -> p h j", j=NQ),
                             skew_back(skew, g)).then_inc(S["se_in"], 16)
            sp.wait_ge(T["yf_done"], 2)
            for p in range(PAIRS):
                refill(1, p)
            sp.wait_ge(T["out_ready"], 1)
            sp.dma_start(x_out, x[:, :]).then_inc(S["x_out"], 16)
            sp.wait_ge(S["x_out"], 16)

        @block.tensor
        def _(pe):
            def ln_transpose(n):
                pe.wait_ge(S["ln_xn"], n + 1)
                pe.transpose(misc[:, 0:NQ], xn[:, :], ident[0:NQ, 0:NQ]).then_inc(S["ln_xt"], 1)
                pe.wait_ge(S["xt_ready"], n + 1)

            def project_q(L):
                q = LS[L]
                for p in range(PAIRS):
                    last = pe.matmul(sexp[0][0:ROWS, p * NQ:(p + 1) * NQ], w(f"wq{L}")[:, p * ROWS:(p + 1) * ROWS],
                                     xnT[:, 0, :], start=True, stop=True)
                last.then_inc(q["qrep_done"], 1)

            def project_k(L):
                q = LS[L]
                for c in range(NCH):
                    if L == 0 and c % 2 == 0:
                        pe.wait_ge(ctx_landed[c // 2], 16)
                    if c >= 2:
                        pe.wait_ge(q["kproj_taken"], c - 1)
                    pe.matmul(smax[c % 2][:, 0:CW], w(f"wk{L}"), ctxT[:, c * CW:(c + 1) * CW],
                              start=True, stop=True).then_inc(q["kproj_done"], 1)

            def project_v(L):
                q = LS[L]
                pe.wait_ge(q["qstack_ready"], 1)
                for g in range(STEPS):
                    if g >= 2:
                        pe.wait_ge(q["vproj_taken"], g - 1)
                    for t in range(TPS):
                        kt = g * TPS + t
                        last = pe.matmul(sexp[g % 2][:, t * P:(t + 1) * P], ctxT[:, kt * P:(kt + 1) * P],
                                         w(f"wv{L}"), start=True, stop=True)
                    last.then_inc(q["vproj_done"], 1)

            def cross(L):
                q = LS[L]

                def max_chunks(pair, b, chunks):
                    for n in chunks:
                        if n == 0:
                            pe.wait_ge(q["qmax_ready"], pair + 1)
                        for h, (a, _) in enumerate(PORTIONS):
                            if n == 2 * a:
                                pe.wait_ge(stack_landed[L][b][h], (pair - b) * (8 * TERMS) + 16 * TERMS)
                        if not (isinstance(pair, int) and pair == 0 and n < 2):
                            pe.wait_ge(q["smax_taken"], pair * NCH + (n - 1))
                        pe.matmul(smax[n % 2][:, 0:CW], qmax[0:ROWS, b, :], kstack[0:ROWS, b, n * CW:(n + 1) * CW],
                                  start=True, stop=True).then_inc(q["smax_done"], 1)

                def max_to_rows(pair):
                    pe.wait_ge(q["m3_ready"], pair + 1)
                    pe.matmul(misc[MROW:MROW + 3, 0:P], m3[:, 0:3], identb[:, :], start=True, stop=True,
                              tile_position=(0, MROW)).then_inc(q["mt_done"], 1)

                def scores(s, pair, b, j, buf):
                    if j == 0:
                        pe.wait_ge(q["qm_ready"], pair + 1)
                    pe.wait_ge(q["exp_done"], s + 1)
                    for t in range(TPS):
                        ks = slice((j * TPS + t) * P, (j * TPS + t + 1) * P)
                        o = sexp[buf][:, t * P:(t + 1) * P]
                        if L == 0:
                            pe.matmul(o, maskadd[:, ks], identb[:, :], start=True, stop=False)
                        last = pe.matmul(o, kstack[0:MROW + 3, b, ks], qexp[0:MROW + 3, b, :],
                                         start=L != 0, stop=True)
                    last.then_inc(q["sexp_done"], 1)

                def times_v(s, pair, b, j, buf):
                    if j == 0:
                        pe.wait_ge(q["vcur_ready"], pair + 1)
                        if not (isinstance(pair, int) and pair == 0):
                            pe.wait_ge(q["acc_copied"], pair)
                    pe.wait_ge(q["exp_done"], s + 3)
                    for t in range(TPS):
                        g = t % 4
                        last = pe.matmul(acc[32 * g:32 * g + VC, 0:P], vcur[:, b, j * TPS + t, :],
                                         probs[:, buf, t * P:(t + 1) * P],
                                         start=(j == 0 and t < 4), stop=(j == STEPS - 1 and t >= TPS - 4),
                                         tile_position=(0, 32 * g))
                    last.then_inc(q["pv_done"], 1)

                def sum_groups(pair):
                    pe.wait_ge(q["acc_copied"], pair + 1)
                    pe.matmul(misc[:, P:P + VC], acc_sb[:, :], w("sum4"), start=True, stop=True
                              ).then_inc(q["sum_done"], 1)

                def step(i, k, ahead=True):
                    s = i * (2 * STEPS) + k
                    j, pair, b = k % STEPS, i * 2 + k // STEPS, (k // STEPS) % 2
                    if ahead:
                        c = sum(CHUNKS[:j])
                        max_chunks(pair + 1, 1 - b, range(c, c + CHUNKS[j]))
                    scores(s, pair, b, j, k % 2)
                    k1 = k - 1
                    times_v(s - 1, i * 2 + k1 // STEPS, (k1 // STEPS) % 2, k1 % STEPS, k1 % 2)
                    if j == 1 and k > STEPS:
                        sum_groups(pair - 1)
                    if j == STEPS - 1 and ahead:
                        pe.wait_ge(q["o17_taken"], pair + 1)
                        max_to_rows(pair + 1)

                pe.sem_inc(q["pv_done"], 2)
                pe.wait_ge(q["vproj_taken"], STEPS)
                max_chunks(0, 0, range(NCH))
                max_to_rows(0)
                max_chunks(1, 1, range(CHUNKS[0]))
                scores(0, 0, 0, 0, 0)
                step(0, 1)
                step(0, 2)
                with pe.Fori(0, PAIRS // 2 - 1) as i:
                    for k in range(3, 2 * STEPS + 3):
                        step(i, k)
                for k in range(3, 2 * STEPS):
                    step(PAIRS // 2 - 1, k, ahead=k < STEPS)
                times_v(PAIRS * STEPS - 1, PAIRS - 1, 1, STEPS - 1, 1)
                sum_groups(PAIRS - 1)

            def cross_out(L):
                q = LS[L]
                pe.wait_ge(q["on_ready"], 2)
                pe.transpose(misc[0:NQ, 0:P], onorm[:, :, :].rearrange("p a d -> p (a d)"), ident).then_inc(q["ot_done"], 1)
                pe.wait_ge(q["ot_ready"], 1)
                for e in range(2):
                    last = pe.matmul(acc[0:NQ, D:2 * D], oT[:, e * NQ:(e + 1) * NQ], w(f"wo{L}")[:, e * D:(e + 1) * D],
                                     start=e == 0, stop=e == 1)
                last.then_inc(q["y_done"], 1)

            pe.wait_ge(S["pack1_in"], 16)
            ln_transpose(0)
            project_q(0)
            project_k(0)
            project_v(0)
            pe.wait_ge(S["mask_ready"], 1)
            pe.wait_ge(S["identb_ready"], 1)
            pe.wait_ge(S["ones_ready"], 3)
            cross(0)
            pe.wait_ge(S["pack2_in"], 16)
            cross_out(0)

            ln_transpose(1)
            pe.matmul(misc[:, 64:128], w("a0_wq"), xnT[:, 0, :], start=True, stop=True)
            pe.matmul(misc[:, 128:192], w("a0_wk"), xnT[:, 0, :], start=True, stop=True)
            pe.matmul(misc[:, 192:256], w("a0_gw"), xnT[:, 0, :], start=True, stop=True)
            pe.matmul(misc[:, 256:384], xnT[:, :, :].rearrange("p a n -> p (a n)"), w("a0_wv"),
                      start=True, stop=True).then_inc(T["qkv_done"], 1)
            pe.wait_ge(T["qk_ready"], 1)
            for hf in range(2):
                last = pe.matmul(sexp[1][0:NQ, hf * 512:(hf + 1) * 512], qT[:, :], big2[:, hf * 512:(hf + 1) * 512],
                                 start=True, stop=True)
            last.then_inc(T["se_done"], 1)
            pe.wait_ge(T["kbd_ready"], 1)
            for g in range(2):
                last = pe.matmul(sexp[0][g * NQ:(g + 1) * NQ, 0:512], qT[:, :], big[:, g * 512:(g + 1) * 512],
                                 start=True, stop=True, tile_position=(0, g * NQ))
            last.then_inc(T["s_done"], 1)
            pe.wait_ge(T["p_ready"], 1)
            for b in range(4):
                last = pe.transpose(sexp[0][:, 512 + b * P:512 + (b + 1) * P], w512[:, b * P:(b + 1) * P], ident)
            last.then_inc(T["pt_done"], 1)
            pe.wait_ge(T["pt_ready"], 1)
            pe.wait_ge(T["v_ready"], 2)
            for n in range(PAIRS):
                last = pe.matmul(misc[:, 384:448], vbd[:, n, :], v512[:, (n % 4) * P + (n // 4) * NQ:(n % 4) * P + (n // 4) * NQ + NQ],
                                 start=n == 0, stop=n == PAIRS - 1)
            last.then_inc(T["ot2_done"], 1)
            pe.wait_ge(T["og_ready"], 1)
            pe.matmul(acc[0:NQ, D:2 * D], ogT[:, :], w("a0_wo"), start=True, stop=True).then_inc(T["y2_done"], 1)

            ln_transpose(2)
            pe.matmul(misc[0:NQ, 64:64 + E0], xnT[:, 0, :], w("f0_router"), start=True, stop=True).then_inc(T["r_done"], 1)
            pe.wait_ge(T["route_ready"], 2)
            for hf in range(2):
                last = pe.matmul(sexp[0][:, hf * 512:(hf + 1) * 512], xz[:, :], big[0:NQ, hf * 512:(hf + 1) * 512],
                                 start=True, stop=True)
            last.then_inc(T["xm_done"], 1)
            pe.matmul(sexp[1][NQ:P, 0:2 * F0], xnT[:, 0, :], w("f0_shared"), start=True, stop=True, tile_position=(0, NQ))
            pe.wait_ge(T["xm_ready"], 1)
            pe.wait_ge(S["gup_in"], 16)
            for e in range(E0):
                last = pe.matmul(sexp[1][0:NQ, 0:2 * F0], big2[:, e * NQ:(e + 1) * NQ], gup[:, e, :],
                                 start=e == 0, stop=e == E0 - 1, tile_position=(0, 0))
            last.then_inc(T["h_done"], 1)
            pe.wait_ge(T["a_ready"], 1)
            pe.wait_ge(S["down_in"], 16)
            for f in range(2):
                fs = slice(f * P, (f + 1) * P)
                pe.transpose(misc[:, f * NQ:(f + 1) * NQ], w512[NQ:P, fs], ident[NQ:P, NQ:P])
                for hf in range(2):
                    last = pe.matmul(sexp[0][:, hf * 512:(hf + 1) * 512], w512[0:NQ, fs], big[0:NQ, hf * 512:(hf + 1) * 512],
                                     start=True, stop=True)
                last.then_inc(T["at_done"], 1)
                pe.wait_ge(T["at_ready"], f + 1)
                for e in range(E0):
                    pe.matmul(acc[0:NQ, D:2 * D], big2[:, e * NQ:(e + 1) * NQ], down[:, f, e, :],
                              start=f == 0 and e == 0, stop=False)
                last = pe.matmul(acc[0:NQ, D:2 * D], gt[:, :], w("f0_wd")[:, f * D:(f + 1) * D], start=False, stop=f == 1)
                last.then_inc(T["yf_done"], 1)

            ln_transpose(3)
            project_q(1)
            project_k(1)
            project_v(1)
            pe.wait_ge(S["ones_ready"], 4)
            cross(1)
            cross_out(1)

            ln_transpose(4)
            pe.matmul(misc[:, 64:128], w("a1_wq"), xnT[:, 0, :], start=True, stop=True)
            pe.matmul(misc[:, 128:192], w("a1_wk"), xnT[:, 0, :], start=True, stop=True)
            pe.matmul(misc[:, 256:384], xnT[:, :, :].rearrange("p a n -> p (a n)"), w("a1_wv"),
                      start=True, stop=True).then_inc(T["b_qkv_done"], 1)
            pe.wait_ge(T["b_kbd_ready"], 1)
            for g in range(2):
                last = pe.matmul(sexp[0][g * NQ:(g + 1) * NQ, 0:512], qT[:, :], big[:, g * 512:(g + 1) * 512],
                                 start=True, stop=True, tile_position=(0, g * NQ))
            last.then_inc(T["b_s_done"], 1)
            pe.wait_ge(T["b_p_ready"], 1)
            for b in range(4):
                last = pe.transpose(sexp[0][:, 512 + b * P:512 + (b + 1) * P], w512[:, b * P:(b + 1) * P], ident)
            last.then_inc(T["b_pt_done"], 1)
            pe.wait_ge(T["b_pt_ready"], 1)
            pe.wait_ge(T["b_v_ready"], 2)
            for n in range(PAIRS):
                last = pe.matmul(misc[:, 384:448], vbd[:, n, :], v512[:, (n % 4) * P + (n // 4) * NQ:(n % 4) * P + (n // 4) * NQ + NQ],
                                 start=n == 0, stop=n == PAIRS - 1)
            last.then_inc(T["b_ot_done"], 1)
            pe.wait_ge(T["b_og_ready"], 1)
            pe.matmul(acc[0:NQ, D:2 * D], ogT[:, :], w("a1_wo"), start=True, stop=True).then_inc(T["b_y_done"], 1)

            pe.wait_ge(T["z_ready"], 1)
            pe.matmul(misc[:, 64:65], xz[:, :], small[0:NQ, 0:1], start=True, stop=True)
            pe.transpose(misc[:, 128:192], xz[:, :], ident[0:NQ, 0:NQ]).then_inc(T["zt_done"], 1)
            pe.wait_ge(T["zb_ready"], 1)
            pe.matmul(sexp[0][:, 0:E1], w512[:, 0:P], w("f1_wr"),
                      start=True, stop=True).then_inc(T["g_done"], 1)
            pe.wait_ge(T["wsel_ready"], 1)
            pe.wait_ge(T["zt_ready"], 1)
            pe.matmul(acc[0:F1, 0:NQ], v512[:, 0:F1], qT[:, :], start=True, stop=True).then_inc(T["h1_done"], 1)
            pe.wait_ge(T["h1_ready"], 1)
            pe.matmul(sexp[1][0:NQ, 0:D], kT[0:F1, :], v512[0:F1, 128:256], start=True, stop=True).then_inc(T["y1_done"], 1)

        @block.scalar
        def _(act):
            chain = [0]

            def link(ins):
                chain[0] += 1
                ins.then_inc(S["act_chain"], 1)
                act.wait_ge(S["act_chain"], chain[0])

            def rsqrt(n):
                act.wait_ge(S["ln_var"], n + 1)
                link(act.activation(lnv[0:NQ, :], mv[0:NQ, 1:2], ACT.Ln, bias=w("eps")[0:NQ, :]))
                act.activation(rstd[0:NQ, :], lnv[0:NQ, :], ACT.Exp, scale=-0.5).then_inc(S["ln_rstd"], 1)

            def split_k(L):
                q = LS[L]
                bias = w("bk1") if L else w("zero")
                for c in range(NCH):
                    act.wait_ge(q["kproj_done"], c + 1)
                    act.activation(kpart[:, 0, c * CW:(c + 1) * CW], smax[c % 2][:, 0:CW], ACT.Identity, bias=bias
                                   ).then_inc(q["khigh_done"], 1)

            def take_v(L):
                q = LS[L]
                for g in range(STEPS):
                    act.wait_ge(q["vproj_done"], g + 1)
                    act.activation(vones[:, g * TPS:(g + 1) * TPS, :, 0:2 * HD],
                                   sexp[g % 2][:, 0:SW].rearrange("p (t a c) -> p t a c", t=TPS, a=PAIRS),
                                   ACT.Copy).then_inc(q["vproj_taken"], 1)

            def cross(L):
                q = LS[L]

                def exps(s, buf):
                    act.wait_ge(q["sexp_done"], s + 1)
                    act.wait_ge(q["pv_done"], s + 1)
                    act.activation(probs[:, buf, :], sexp[buf][:, 0:SW], ACT.Exp).then_inc(q["exp_done"], 1)

                def take_acc(pair):
                    act.wait_ge(q["pv_done"], pair * STEPS + STEPS + 2)
                    act.activation(acc_sb[:, :], acc[:, 0:P], ACT.Copy).then_inc(q["acc_copied"], 1)

                def take_sum(pair):
                    act.wait_ge(q["sum_done"], pair + 1)
                    o = o17[:, pair, :] if isinstance(pair, int) else \
                        o17[:, :, :].rearrange("p a c -> p (a c)")[:, bass.ds(pair * VC, VC)]
                    act.activation(o, misc[:, P:P + VC], ACT.Copy).then_inc(q["o17_taken"], 1)

                def step(i, k):
                    exps(i * (2 * STEPS) + k, k % 2)
                    if k >= STEPS and k % STEPS == 0:
                        take_acc(i * 2 + k // STEPS - 1)
                    if k >= STEPS and k % STEPS == 2:
                        take_sum(i * 2 + k // STEPS - 1)

                act.sem_inc(q["exp_done"], 2)
                act.sem_inc(q["o17_taken"], 1)
                for k in range(3):
                    step(0, k)
                with act.Fori(0, PAIRS // 2 - 1) as i:
                    for k in range(3, 2 * STEPS + 3):
                        step(i, k)
                for k in range(3, 2 * STEPS):
                    step(PAIRS // 2 - 1, k)
                take_acc(PAIRS - 1)
                take_sum(PAIRS - 1)

            act.wait_ge(S["pack1_in"], 16)
            rsqrt(0)
            split_k(0)
            take_v(0)
            cross(0)
            act.wait_ge(S["pack2_in"], 16)
            link(act.activation(bnr[:, 0:1], w("f1_bn")[:, 3:4], ACT.Ln, bias=w("eps")))
            act.activation(bnr[:, 1:2], bnr[:, 0:1], ACT.Exp, scale=-0.5).then_inc(T["bn_rs"], 1)
            rsqrt(1)
            act.wait_ge(T["se_done"], 1)
            act.activation(big2[0:NQ, :], sexp[1][0:NQ, :], ACT.Copy, scale=SCALE, bias=SCALE).then_inc(T["se_taken"], 1)
            act.wait_ge(T["qk_ready"], 1)
            act.activation(gt[:, :], misc[:, 192:256], ACT.Exp, scale=-1.0, bias=ngb[:, 0:1]).then_inc(T["gate_e"], 1)
            act.wait_ge(T["exp_ready"], 1)
            act.activation(w512[:, :], w512[:, :], ACT.Exp).then_inc(T["exps"], 1)
            rsqrt(2)
            act.wait_ge(T["r_e"], 1)
            act.activation(small[0:NQ, 2:3], small[0:NQ, 1:2], ACT.Exp, scale=-1.0).then_inc(T["r_e"], 1)
            act.wait_ge(T["h_done"], 1)
            act.activation(v512[:, 0:F0], sexp[1][:, 0:F0], ACT.Exp, scale=-1.0).then_inc(T["h_e"], 1)
            rsqrt(3)
            split_k(1)
            act.wait_ge(LS[0]["vcur_ready"], PAIRS)
            take_v(1)
            cross(1)
            rsqrt(4)
            act.wait_ge(T["b_exp_ready"], 1)
            act.activation(w512[:, :], w512[:, :], ACT.Exp).then_inc(T["b_exps"], 1)
            rsqrt(5)
            rsqrt(6)
            act.wait_ge(T["g_ready"], 1)
            act.activation(red2[:, 0:E1], red[:, 0:E1], ACT.Exp, accum_out=small[:, 4:5]).then_inc(T["g_e"], 1)

        @block.vector
        def _(dve):
            chain = [0]

            def link(ins):
                chain[0] += 1
                ins.then_inc(S["dve_chain"], 1)
                dve.wait_ge(S["dve_chain"], chain[0])

            def layernorm(n, src=None):
                src = x[:, :] if src is None else src
                link(dve.bn_stats(st[0:NQ, :], src))
                dve.bn_aggr(mv[0:NQ, :], st[0:NQ, :]).then_inc(S["ln_var"], 1)
                dve.wait_ge(S["ln_rstd"], n + 1)
                return dve.tensor_scalar(xn[:, :], src, mv[0:NQ, 0:1], rstd[0:NQ, 0:1], ALU.subtract, ALU.mult)

            def take_xt(n):
                dve.wait_ge(S["ln_xt"], n + 1)
                dve.tensor_copy(xnT[:, :, :], misc[:, 0:NQ].unsqueeze(1).to_broadcast([P, 2, NQ])).then_inc(S["xt_ready"], 1)

            def stack_q(L):
                q = LS[L]
                R = slice(0, ROWS)
                sel = w("sel")
                dve.wait_ge(q["qrep_done"], 1)
                src = sexp[0][R, 0:PAIRS * NQ]
                if L:
                    link(dve.tensor_tensor(qf[R, :].rearrange("p (a n) -> p a n", a=PAIRS),
                                           src.rearrange("p (a n) -> p a n", a=PAIRS),
                                           w("bq1").unsqueeze(2).to_broadcast([ROWS, PAIRS, NQ]), ALU.add))
                    src = qf[R, :]
                link(dve.tensor_scalar(qf[R, :], src, SCALE, None, ALU.mult))
                link(dve.tensor_copy(qh[R, :], qf[R, :]))
                link(dve.tensor_tensor(qr[R, :], qf[R, :], qh[R, :], ALU.subtract))
                link(dve.tensor_copy(qm[R, :], qr[R, :]))
                link(dve.tensor_tensor(ql[R, :], qr[R, :], qm[R, :], ALU.subtract))
                link(dve.tensor_scalar(qc[R, :], qh[R, :], sel[:, 0:1], None, ALU.mult))
                link(dve.scalar_tensor_tensor(qc[R, :], qm[R, :], sel[:, 1:2], qc[R, :], ALU.mult, ALU.add))
                link(dve.scalar_tensor_tensor(qc[R, :], ql[R, :], sel[:, 2:3], qc[R, :], ALU.mult, ALU.add))
                for e in range(2):
                    last = dve.tensor_scalar(qstack[R, :, e, :], qc[R, :].rearrange("p (a n) -> p a n", a=PAIRS),
                                             sel[:, 3 + e:4 + e], None, ALU.mult)
                    last.then_inc(q["qstack_ready"], 1)

            def split_k(L):
                q = LS[L]
                bias = w("bk1") if L else w("zero")
                for c in range(NCH):
                    cs = slice(c * CW, (c + 1) * CW)
                    dve.wait_ge(q["khigh_done"], c + 1)
                    if c >= 2:
                        dve.wait_ge(q["klow_done"], c - 1)
                    dve.scalar_tensor_tensor(kres[:, c % 2, :], smax[c % 2][:, 0:CW], bias, kpart[:, 0, cs],
                                             ALU.add, ALU.subtract).then_inc(q["kproj_taken"], 1)
                    dve.wait_ge(q["kproj_taken"], c + 1)
                    dve.tensor_copy(kpart[:, 1, cs], kres[:, c % 2, :]).then_inc(q["kmid_done"], 1)

            def cross(L):
                q = LS[L]

                def one(pair, b):
                    for n in range(NCH):
                        dve.wait_ge(q["smax_done"], pair * NCH + n + 1)
                        if L == 0:
                            dve.sem_inc(q["passed"], 1)
                        if L == 0:
                            dve.tensor_tensor_reduce(junk[:, n % 2, :], smax[n % 2][:, 0:CW], maskadd[:, n * CW:(n + 1) * CW],
                                                     1.0, -3e38, ALU.add, ALU.max, mx[:, b, n:n + 1]
                                                     ).then_inc(q["smax_taken"], 1)
                        else:
                            dve.tensor_reduce(mx[:, b, n:n + 1], smax[n % 2][:, 0:CW], AX.X, ALU.max
                                              ).then_inc(q["smax_taken"], 1)
                    dve.wait_ge(q["smax_taken"], pair * NCH + NCH)
                    links = [0]

                    def next_reads(ins):
                        links[0] += 1
                        ins.then_inc(q["mx_chain"], 1)
                        dve.wait_ge(q["mx_chain"], pair * 5 + links[0])

                    next_reads(dve.tensor_reduce(negm[:, 0:1], mx[:, b, :], AX.X, ALU.max, negate=True))
                    next_reads(dve.tensor_scalar(negm[:, 0:1], negm[:, 0:1], -MASKED / 2 if L == 0 else 3e38, None, ALU.min))
                    next_reads(dve.tensor_copy(m3[:, 0:1], negm[:, 0:1]))
                    next_reads(dve.tensor_tensor(negm[:, 1:2], negm[:, 0:1], m3[:, 0:1], ALU.subtract))
                    next_reads(dve.tensor_copy(m3[:, 1:2], negm[:, 1:2]))
                    dve.tensor_tensor(m3[:, 2:3], negm[:, 1:2], m3[:, 1:2], ALU.subtract).then_inc(q["m3_ready"], 1)
                    dve.wait_ge(q["mt_done"], pair + 1)
                    dve.wait_ge(q["qexp_ready"], pair + 1)
                    dve.tensor_copy(qexp[MROW:MROW + 3, b, :], misc[MROW:MROW + 3, 0:P]).then_inc(q["qm_ready"], 1)

                with dve.Fori(0, PAIRS // 2) as i:
                    one(i * 2, 0)
                    one(i * 2 + 1, 1)

            def cross_out(L):
                q = LS[L]
                dve.wait_ge(q["o17_taken"], PAIRS + 1)
                if L == 0:
                    link(dve.tensor_scalar(den[:, :], o17[:, :, VC - 1], 1e-9, None, ALU.max))
                link(dve.reciprocal(rden[:, :], den[:, :] if L == 0 else o17[:, :, VC - 1]))
                for e in range(2):
                    r = slice(e * NQ, (e + 1) * NQ)
                    ins = dve.tensor_tensor(onorm[r, :, :], o17[r, :, e * HD:(e + 1) * HD],
                                            rden[r, :].unsqueeze(2).to_broadcast([NQ, PAIRS, HD]), ALU.mult)
                    if L == 0:
                        ins.then_inc(q["on_ready"], 1)
                    else:
                        link(ins)
                if L:
                    dve.tensor_tensor(onorm[:, :, :], onorm[:, :, :], w("bv1").rearrange("p (a d) -> p a d", a=PAIRS),
                                      ALU.add).then_inc(q["on_ready"], 2)
                dve.wait_ge(q["ot_done"], 1)
                dve.tensor_copy(oT[:, :], misc[0:NQ, 0:P]).then_inc(q["ot_ready"], 1)
                dve.wait_ge(q["y_done"], 1)
                link(dve.tensor_tensor(x[:, :], acc[0:NQ, D:2 * D], x[:, :], ALU.add))
                if L:
                    link(dve.tensor_tensor(x[:, :], x[:, :], w("bo1"), ALU.add))

            dve.memset(vones[:, :, :, 2 * HD:VC], 1.0).then_inc(S["ones_ready"], 1)
            dve.memset(kstack[MROW:MROW + 3, :, :], 1.0).then_inc(S["ones_ready"], 1)
            dve.memset(acc[:, :], 0.0).then_inc(S["ones_ready"], 1)
            dve.wait_ge(S["pack1_in"], 16)
            dve.tensor_copy(identb[:, :], ident).then_inc(S["identb_ready"], 1)

            dve.wait_ge(S["x_in"], 16)
            layernorm(0).then_inc(S["ln_xn"], 1)
            take_xt(0)
            stack_q(0)
            split_k(0)
            dve.wait_ge(S["mask_ready"], 1)
            cross(0)
            dve.wait_ge(S["pack2_in"], 16)
            cross_out(0)

            hm = w("hmask").unsqueeze(2).to_broadcast([P, H, NQ])

            def by_head(out, src):
                return dve.tensor_tensor(out[:, :].rearrange("p (h j) -> p h j", h=H),
                                         src.unsqueeze(1).to_broadcast([P, H, NQ]), hm, ALU.mult)

            def block_v(src_ready_inc):
                flat = vbd.rearrange("p a c -> p (a c)")
                for e in range(2):
                    r = slice(e * NQ, (e + 1) * NQ)
                    o = bass.AP(tensor=flat.tensor, offset=flat[r, :].offset + e * HD,
                                ap=[flat[r, :].ap[0], [D + 2 * HD, PAIRS], [1, HD]])
                    s = v512[r, 0:D].rearrange("p (a e d) -> p a e d", a=PAIRS, e=2)[:, :, e, :]
                    dve.tensor_copy(o, s).then_inc(src_ready_inc, 1)

            def softmax_heads(exp_ready, exps):
                w3 = w512[:, :].rearrange("p (h j) -> p h j", h=H // 2)
                link(dve.tensor_reduce(red[:, 0:H // 2], w3, AX.X, ALU.max))
                dve.tensor_tensor(w3, w3, red[:, 0:H // 2].unsqueeze(2).to_broadcast([P, H // 2, NQ]), ALU.subtract
                                  ).then_inc(exp_ready, 1)
                dve.wait_ge(exps, 1)
                link(dve.tensor_reduce(red2[:, 0:H // 2], w3, AX.X, ALU.add))
                link(dve.reciprocal(red[:, 0:H // 2], red2[:, 0:H // 2]))
                return w3

            link(by_head(big2, w("a0_se")))
            layernorm(1).then_inc(S["ln_xn"], 1)
            take_xt(1)
            link(dve.tensor_scalar(ngb[:, :], w("a0_gb"), -1.0, None, ALU.mult))
            dve.wait_ge(T["qkv_done"], 1)
            link(dve.tensor_scalar(kT[:, :], misc[:, 128:192], w("a0_bk"), None, ALU.add))
            dve.tensor_scalar(qT[:, :], misc[:, 64:128], w("a0_bq"), None, ALU.add).then_inc(T["se_bd"], 1)
            dve.wait_ge(T["se_bd"], 1)
            link(dve.tensor_tensor(v512[:, 0:D], misc[:, 256:384], w("a0_bv"), ALU.add))
            by_head(big, kT[:, :]).then_inc(T["kbd_ready"], 1)
            dve.memset(small[:, 0:1], 1.0 / NQ).then_inc(T["qk_ready"], 1)
            link(dve.memset(vbd, 0.0))
            block_v(T["v_ready"])
            dve.wait_ge(T["v_ready"], 2)
            dve.wait_ge(T["s_done"], 1)
            dve.wait_ge(S["se_in"], 32)
            link(dve.tensor_tensor(w512[:, :], sexp[0][:, 0:512], qf[:, :], ALU.mult))
            dve.wait_ge(S["bias_in"], 32)
            link(dve.tensor_tensor(w512[:, :], w512[:, :], bias_t[:, :], ALU.add))
            w3 = softmax_heads(T["exp_ready"], T["exps"])
            link(dve.tensor_tensor(red[:, 0:H // 2], red[:, 0:H // 2], w("a0_gain"), ALU.mult))
            dve.tensor_tensor(w3, w3, red[:, 0:H // 2].unsqueeze(2).to_broadcast([P, H // 2, NQ]), ALU.mult
                              ).then_inc(T["p_ready"], 1)
            dve.wait_ge(T["gate_e"], 1)
            link(dve.tensor_scalar(gt[:, :], gt[:, :], 1.0, None, ALU.add))
            link(dve.reciprocal(gt[:, :], gt[:, :]))
            dve.wait_ge(T["pt_done"], 1)
            dve.tensor_copy(v512[:, :], sexp[0][:, 512:1024]).then_inc(T["pt_ready"], 1)
            dve.wait_ge(T["ot2_done"], 1)
            dve.tensor_tensor(ogT[:, :], misc[:, 384:448], gt[:, :], ALU.mult).then_inc(T["og_ready"], 1)
            dve.wait_ge(T["y2_done"], 1)
            link(dve.tensor_tensor(x[:, :], acc[0:NQ, D:2 * D], x[:, :], ALU.add))
            link(dve.tensor_tensor(x[:, :], x[:, :], w("a0_bo"), ALU.add))

            layernorm(2).then_inc(S["ln_xn"], 1)
            take_xt(2)
            dve.wait_ge(T["r_done"], 1)

            def first_of_max(logits, rows, n, mxcol, out):
                link(dve.tensor_reduce(mxcol, logits, AX.X, ALU.max))
                link(dve.tensor_scalar(onehot[rows, 0:n], logits, mxcol, None, ALU.is_equal))
                link(dve.tensor_tensor(onehot[rows, 0:n], onehot[rows, 0:n], tie_row(rows, n), ALU.mult))
                link(dve.tensor_reduce(small[rows, 3:4], onehot[rows, 0:n], AX.X, ALU.max))
                return dve.tensor_scalar(out, onehot[rows, 0:n], small[rows, 3:4], None, ALU.is_equal)

            def tie_row(rows, n):
                return w("tie")[rows, E0 - n:E0]

            R = slice(0, NQ)
            first = dve.tensor_reduce(small[R, 1:2], misc[0:NQ, 64:64 + E0], AX.X, ALU.max)
            first.then_inc(T["r_e"], 1)
            dve.wait_ge(T["r_e"], 1)
            link(first_of_max(misc[0:NQ, 64:64 + E0], R, E0, small[R, 5:6], onehot2[R, :]))
            dve.tensor_tensor(routing[0:NQ, :, :], onehot2[R, :].unsqueeze(2).to_broadcast([NQ, E0, NQ]),
                              ident[0:NQ, 0:NQ].unsqueeze(1).to_broadcast([NQ, E0, NQ]), ALU.mult
                              ).then_inc(T["route_ready"], 1)
            dve.wait_ge(T["r_e"], 2)
            link(dve.tensor_scalar(small[R, 2:3], small[R, 2:3], 1.0, None, ALU.add))
            link(dve.reciprocal(small[R, 6:7], small[R, 2:3]))
            dve.tensor_scalar(xz[:, :], xn[:, :], small[R, 6:7], None, ALU.mult).then_inc(T["route_ready"], 1)
            dve.wait_ge(T["xm_done"], 1)
            dve.tensor_copy(big2[:, :], sexp[0][:, :]).then_inc(T["xm_ready"], 1)
            dve.wait_ge(T["h_e"], 1)
            link(dve.tensor_scalar(v512[:, 0:F0], v512[:, 0:F0], 1.0, None, ALU.add))
            link(dve.reciprocal(v512[:, 0:F0], v512[:, 0:F0]))
            link(dve.tensor_tensor(v512[:, 0:F0], sexp[1][:, 0:F0], v512[:, 0:F0], ALU.mult))
            dve.tensor_tensor(w512[:, 0:F0], sexp[1][:, F0:2 * F0], v512[:, 0:F0], ALU.mult).then_inc(T["a_ready"], 1)
            for f in range(2):
                dve.wait_ge(T["at_done"], f + 1)
                if f:
                    dve.wait_ge(T["yf_done"], 1)
                link(dve.tensor_copy(gt[:, :], misc[:, f * NQ:(f + 1) * NQ]))
                dve.tensor_copy(big2[:, :], sexp[0][:, :]).then_inc(T["at_ready"], 1)
            dve.wait_ge(T["yf_done"], 2)
            link(dve.tensor_tensor(x[:, :], acc[0:NQ, D:2 * D], x[:, :], ALU.add))

            dve.memset(kstack[MROW:MROW + 3, :, :], 1.0).then_inc(S["ones_ready"], 1)
            layernorm(3).then_inc(S["ln_xn"], 1)
            take_xt(3)
            stack_q(1)
            split_k(1)
            cross(1)
            cross_out(1)

            layernorm(4).then_inc(S["ln_xn"], 1)
            take_xt(4)
            dve.wait_ge(T["b_qkv_done"], 1)
            s4 = w("a1_s")
            link(dve.tensor_scalar(kT[:, :], misc[:, 128:192], s4[:, 1:2], w("a1_bk"), ALU.mult, ALU.add))
            link(dve.tensor_scalar(qT[:, :], misc[:, 64:128], s4[:, 0:1], w("a1_bq"), ALU.mult, ALU.add))
            link(dve.tensor_scalar(qT[:, :], qT[:, :], SCALE, None, ALU.mult))
            link(dve.scalar_tensor_tensor(v512[:, 0:D], misc[:, 256:384], s4[:, 2:3], w("a1_bv"), ALU.mult, ALU.add))
            by_head(big, kT[:, :]).then_inc(T["b_kbd_ready"], 1)
            link(dve.memset(vbd, 0.0))
            block_v(T["b_v_ready"])
            dve.wait_ge(T["b_s_done"], 1)
            link(dve.tensor_copy(w512[:, :], sexp[0][:, 0:512]))
            w3 = softmax_heads(T["b_exp_ready"], T["b_exps"])
            dve.tensor_tensor(w3, w3, red[:, 0:H // 2].unsqueeze(2).to_broadcast([P, H // 2, NQ]), ALU.mult
                              ).then_inc(T["b_p_ready"], 1)
            dve.wait_ge(T["b_pt_done"], 1)
            dve.tensor_copy(v512[:, :], sexp[0][:, 512:1024]).then_inc(T["b_pt_ready"], 1)
            dve.wait_ge(T["b_ot_done"], 1)
            dve.tensor_copy(ogT[:, :], misc[:, 384:448]).then_inc(T["b_og_ready"], 1)
            dve.wait_ge(T["b_y_done"], 1)
            link(dve.scalar_tensor_tensor(x[:, :], acc[0:NQ, D:2 * D], s4[0:NQ, 3:4], x[:, :], ALU.mult, ALU.add))
            link(dve.tensor_tensor(x[:, :], x[:, :], w("a1_bo"), ALU.add))

            link(layernorm(5))
            link(layernorm(6, xn[:, :]))
            link(dve.tensor_tensor(xn[:, :], xn[:, :], w("f1_lng"), ALU.mult))
            dve.tensor_tensor(xz[:, :], xn[:, :], w("f1_lnb"), ALU.add).then_inc(T["z_ready"], 1)
            bn = w("f1_bn")
            dve.wait_ge(T["bn_rs"], 1)
            dve.wait_ge(T["zt_done"], 1)
            link(dve.tensor_scalar(red[:, 2:3], misc[:, 64:65], bn[:, 2:3], bnr[:, 1:2], ALU.subtract, ALU.mult))
            link(dve.tensor_scalar(red[:, 3:4], red[:, 2:3], bn[:, 0:1], bn[:, 1:2], ALU.mult, ALU.add))
            link(dve.memset(big2[:, 0:P], 1.0))
            dve.tensor_scalar(w512[:, 0:P], big2[:, 0:P], red[:, 3:4], None, ALU.mult).then_inc(T["zb_ready"], 1)
            dve.tensor_copy(qT[:, :], misc[:, 128:192]).then_inc(T["zt_ready"], 1)
            dve.wait_ge(T["g_done"], 1)
            A = slice(0, P)
            link(dve.tensor_tensor(red2[:, 0:E1], sexp[0][:, 0:E1], w("f1_br"), ALU.add))
            link(first_of_max(red2[:, 0:E1], A, E1, small[:, 5:6], onehot2[:, 0:E1]))
            dve.tensor_scalar(red[:, 0:E1], red2[:, 0:E1], small[:, 5:6], None, ALU.subtract).then_inc(T["g_ready"], 1)
            oh = onehot2[:, 0:E1]

            def select(name, n, rows, out):
                src = w(name).rearrange("p (n e) -> p n e", e=E1)
                link(dve.tensor_tensor(big[0:rows, 0:n * E1].rearrange("p (n e) -> p n e", e=E1), src,
                                       oh[0:rows, :].unsqueeze(1).to_broadcast([rows, n, E1]), ALU.mult))
                return dve.tensor_reduce(out, big[0:rows, 0:n * E1].rearrange("p (n e) -> p n e", e=E1), AX.X, ALU.add)

            link(select("f1_wd", F1, D, v512[:, 0:F1]))
            select("f1_wu", D, F1, v512[0:F1, 128:256]).then_inc(T["wsel_ready"], 1)
            dve.wait_ge(T["wsel_ready"], 1)
            link(dve.tensor_tensor(big[0:F1, 0:E1], w("f1_bd")[:, 0:E1], oh[0:F1, :], ALU.mult))
            link(dve.tensor_reduce(small[0:F1, 8:9], big[0:F1, 0:E1], AX.X, ALU.add))
            dve.wait_ge(T["h1_done"], 1)
            dve.tensor_scalar(kT[0:F1, :], acc[0:F1, 0:NQ], small[0:F1, 8:9], 0.0, ALU.add, ALU.max).then_inc(T["h1_ready"], 1)
            link(select("f1_bu", D, NQ, v512[0:NQ, 256:384]))
            dve.wait_ge(T["g_e"], 1)
            link(dve.reciprocal(small[:, 7:8], small[:, 4:5]))
            dve.wait_ge(T["y1_done"], 1)
            link(dve.tensor_tensor(xz[:, :], sexp[1][0:NQ, 0:D], v512[0:NQ, 256:384], ALU.add))
            dve.scalar_tensor_tensor(x[:, :], xz[:, :], small[0:NQ, 7:8], x[:, :], ALU.mult, ALU.add
                                     ).then_inc(T["out_ready"], 1)

        @block.gpsimd
        def _(pool):
            def split_k(L):
                q = LS[L]
                for c in range(NCH):
                    cs = slice(c * CW, (c + 1) * CW)
                    pool.wait_ge(q["kmid_done"], c + 1)
                    pool.tensor_tensor(kpart[:, 2, cs], kres[:, c % 2, :], kpart[:, 1, cs], ALU.subtract
                                       ).then_inc(q["klow_done"], 1)

            def cross(L):
                q = LS[L]
                qflat = qstack[:, :, :, :].rearrange("p a e n -> p (a e n)")
                vflat = vones[:, :, :, :].rearrange("p t a c -> p t (a c)")

                def one(pair, b, first):
                    qs = qflat[0:ROWS, pair * P:(pair + 1) * P] if isinstance(pair, int) else \
                        qflat[0:ROWS, bass.ds(pair * P, P)]
                    vs = vflat[:, :, pair * VC:(pair + 1) * VC] if isinstance(pair, int) else \
                        vflat[:, :, bass.ds(pair * VC, VC)]
                    pool.wait_ge(q["qstack_ready"], 2)
                    if not first:
                        pool.wait_ge(q["smax_done"], (pair - 1) * NCH)
                        pool.sem_inc(q["pool_passed"], 1)
                    pool.tensor_copy(qmax[0:ROWS, b, :], qs).then_inc(q["qmax_ready"], 1)
                    pool.wait_ge(q["qstack_ready"], 2)
                    if not first:
                        pool.wait_ge(q["sexp_done"], (pair - 1) * STEPS)
                        pool.sem_inc(q["pool_passed"], 1)
                    pool.tensor_copy(qexp[0:ROWS, b, :], qs).then_inc(q["qexp_ready"], 1)
                    pool.wait_ge(q["vproj_taken"], STEPS)
                    if not first:
                        pool.wait_ge(q["pv_done"], (pair - 1) * STEPS + 2)
                        pool.sem_inc(q["pool_passed"], 1)
                    pool.tensor_copy(vcur[:, b, :, :], vs).then_inc(q["vcur_ready"], 1)

                pool.wait_ge(S["ones_ready"], 1)
                one(0, 0, True)
                one(1, 1, True)
                with pool.Fori(1, PAIRS // 2) as i:
                    one(i * 2, 0, False)
                    one(i * 2 + 1, 1, False)

            for g in range(2):
                pool.dma_start(bias_t[g * NQ:(g + 1) * NQ, :].rearrange("p (h j) -> p h j", j=NQ),
                               bias_rows(bias_in, g)).then_inc(S["bias_in"], 16)
            pool.wait_ge(S["mask_in"], 32)
            pool.tensor_scalar(maskadd, mask_u8, -MASKED, MASKED, ALU.mult, ALU.add).then_inc(S["mask_ready"], 1)
            split_k(0)
            pool.wait_ge(S["mask_ready"], 1)
            cross(0)
            split_k(1)
            pool.wait_ge(T["h_done"], 1)
            cross(1)


OFFSETS = sorted(set(range(33)) | {48, 64, 96, 128, 192})


def kernel(**inputs):
    import numpy as np
    import concourse.bacc as bacc
    from concourse.bass_utils import run_bass_kernel_spmd

    a = {k: np.asarray(v) for k, v in inputs.items()}
    rows = lambda v, n=P: np.broadcast_to(np.asarray(v).reshape(1, -1), (n, np.asarray(v).size))
    col = lambda v: np.asarray(v).reshape(-1, 1)
    pair_rows = np.array([[(2 * p + e) * HD + d for _ in range(TERMS) for e in range(2) for d in range(HD)]
                          for p in range(PAIRS)])

    def by_pairs(m):
        return m.T[:, pair_rows.reshape(-1)]

    def out_pairs(m):
        return m.T.reshape(PAIRS, 2, HD, D).transpose(0, 2, 1, 3).reshape(NQ, 2 * D)

    sel = np.zeros((ROWS, 5), np.float32)
    for r in range(ROWS):
        sel[r, Q_TERM[r // 16]] = 1
        sel[r, 3 + (r % 16) // HD] = 1
    sum4 = np.zeros((P, VC), np.float32)
    for g in range(4):
        sum4[32 * g + np.arange(VC), np.arange(VC)] = 1
    hmask = (np.arange(P)[:, None] // HD == np.arange(H)[None, :]).astype(np.float32)
    near = [o for o in OFFSETS if o < NQ]
    at = [NQ - 1 - o for o in near]
    se = np.zeros((HD, NQ), np.float32)
    se[:, at] = a["L0_attn_scale_embed"][:len(near)].T
    bias = np.full((H, P), NEG, np.float32)
    bias[:, at] = a["L0_attn_pos_bias"][:len(near)].T
    qkv, qkvb = a["L0_attn_qkv_w"], a["L0_attn_qkv_b"]
    gain = a["L0_attn_if_gain"].reshape(2, 1, H // 2)
    parts = {
        "ident": np.eye(P, dtype=np.float32), "hmask": hmask, "sel": sel, "sum4": sum4,
        "eps": np.full((P, 1), LN_EPS, np.float32), "tie": rows(np.arange(E0, 0, -1).astype(np.float32)),
        "zero": np.zeros((P, 1), np.float32),
        "a0_wq": qkv[0:D].T, "a0_wk": qkv[D:2 * D].T, "a0_wv": qkv[2 * D:].T,
        "a0_bq": col(qkvb[0:D]), "a0_bk": col(qkvb[D:2 * D]), "a0_bv": rows(qkvb[2 * D:]),
        "a0_se": np.tile(se, (H, 1)), "a0_gw": a["L0_attn_gate_w"].T, "a0_gb": col(a["L0_attn_gate_b"]),
        "a0_gain": np.broadcast_to(gain, (2, NQ, H // 2)).reshape(P, H // 2),
        "a0_wo": a["L0_attn_out_w"].T, "a0_bo": rows(a["L0_attn_out_b"], NQ),
        "f0_router": a["L0_ffn_w_router"].T,
        "f0_shared": np.concatenate([a["L0_ffn_w_gate"].T, a["L0_ffn_w_up"].T], 1),
        "f0_wd": a["L0_ffn_w_down"].T.reshape(2, P, D).transpose(1, 0, 2).reshape(P, 2 * D),
        "bk1": col(a["L1_xattn_bk"]), "bq1": a["L1_xattn_bq"][pair_rows].T,
        "bv1": np.repeat(a["L1_xattn_bv"].reshape(PAIRS, 2, HD).transpose(1, 0, 2).reshape(2, NQ), NQ, 0),
        "bo1": rows(a["L1_xattn_bo"], NQ),
        "a1_wq": a["L1_attn_w_q"].T, "a1_wk": a["L1_attn_w_k"].T, "a1_wv": a["L1_attn_w_v"].T, "a1_wo": a["L1_attn_w_o"].T,
        "a1_s": rows(np.stack([a[f"L1_attn_s_{n}"] for n in "qkvo"])),
        "a1_bq": col(a["L1_attn_b_q"]), "a1_bk": col(a["L1_attn_b_k"]),
        "a1_bv": rows(a["L1_attn_b_v"]), "a1_bo": rows(a["L1_attn_b_o"], NQ),
        "f1_lng": rows(a["L1_ffn_ln_g"], NQ), "f1_lnb": rows(a["L1_ffn_ln_b"], NQ),
        "f1_bn": np.stack([a[f"L1_ffn_bn_{n}"] for n in ("g", "b", "mean", "var")], 1),
        "f1_wr": a["L1_ffn_Wr"], "f1_br": rows(a["L1_ffn_br"]),
        "f1_wd": a["L1_ffn_W_down"].transpose(1, 2, 0).reshape(D, F1 * E1), "f1_bd": a["L1_ffn_b_down"].T,
        "f1_wu": a["L1_ffn_W_up"].transpose(1, 2, 0).reshape(F1, D * E1), "f1_bu": rows(a["L1_ffn_b_up"].T, NQ),
    }
    for L in range(2):
        parts[f"wq{L}"] = by_pairs(a[f"L{L}_xattn_Wq"])
        parts[f"wk{L}"] = a[f"L{L}_xattn_Wk"].T
        parts[f"wv{L}"] = a[f"L{L}_xattn_Wv"].T
        parts[f"wo{L}"] = out_pairs(a[f"L{L}_xattn_Wo"])
    packs = []
    for cols, width in pack_layout():
        pack = np.zeros((P, width), np.float32)
        for name, (c, n, r) in cols.items():
            assert parts[name].shape == (r, n), (name, parts[name].shape, (r, n))
            pack[:r, c:c + n] = parts[name]
        packs.append(pack)
    arrays = {
        "x_in": a["x"][0], "ctx_in": np.ascontiguousarray(a["ctx_1024"][0].T),
        "mask_in": np.ascontiguousarray(a["mask_SxS2_bk0"]),
        "pack1_in": packs[0], "pack2_in": packs[1], "bias_in": np.ascontiguousarray(np.broadcast_to(bias, (NQ, H, P))),
        "gup_in": np.ascontiguousarray(a["L0_ffn_gate_up_proj"].transpose(1, 0, 2)),
        "down_in": np.ascontiguousarray(a["L0_ffn_down_proj"].reshape(E0, 2, P, D).transpose(2, 1, 0, 3)),
    }
    nc = bacc.Bacc("TRN2", target_bir_lowering=False, num_devices=1)
    aps = [nc.dram_tensor(n, v.shape, mybir.dt.from_np(v.dtype), kind="ExternalInput").ap() for n, v in arrays.items()]
    skew = nc.dram_tensor("skew", (NQ * H * NQ,), F32, kind="Internal").ap()
    out = nc.dram_tensor("x_out", (1, NQ, D), F32, kind="ExternalOutput").ap()
    perceiver(nc, *aps, skew, out[0])
    r = run_bass_kernel_spmd(nc, [arrays], core_ids=[0])
    return r.results[0]["x_out"]
```

```python
from contextlib import ExitStack

import concourse.bass as bass
from concourse import mybir

F32 = mybir.dt.float32
BF16 = mybir.dt.bfloat16
U8 = mybir.dt.uint8
ALU = mybir.AluOpType
ACT = mybir.ActivationFunctionType
AX = mybir.AxisListType

P = 128
D = 128
H = 16
HD = D // H
NQ = 64
NK = 6272
NKT = NK // P
PAIRS = H // 2
STEPS = 7
TPS = NKT // STEPS
SW = TPS * P
CW = SW // 2
NCH = NK // CW
K_TERM = (0, 0, 0, 1, 1, 2)
Q_TERM = (0, 1, 2, 0, 1, 0)
TERMS = len(K_TERM)
ROWS = TERMS * 2 * HD
MROW = ROWS
VC = 2 * HD + 1
SCALE = HD ** -0.5
MASKED = -1e9
CHUNKS = ((2,2,2,3,3,2,0), (2,2,2,3,3,2,0))
PORTIONS = (((0,3),(3,5),(5,7)), ((0,3),(3,5),(5,7)))
E0, F0 = 16, 256
E1, F1 = 8, 64
NEG = -1e30
LN_EPS = 1e-5
V_AFTER = (3, 7, 11)
PACK2_CUTS = 4


def pack_layout():
    first = [("ident", P, P), ("hmask", H, P), ("sel", 5, ROWS), ("sum4", VC, P),
             ("eps", 1, P), ("tie", E0, P), ("zero", 1, P),
             ("wk0", D, D), ("wq0", PAIRS * ROWS, D), ("wv0", D, D)]
    second = [("wo0", 2 * D, NQ), ("wk1", D, D), ("wq1", PAIRS * ROWS, D), ("wv1", D, D), ("wo1", 2 * D, NQ),
              ("bk1", 1, D), ("bq1", PAIRS, ROWS), ("bv1", PAIRS * HD, P), ("bo1", D, NQ),
              ("a0_wq", D, D), ("a0_wk", D, D), ("a0_wv", D, D), ("a0_bq", 1, D), ("a0_bk", 1, D),
              ("a0_bv", D, P), ("a0_se", NQ, D), ("a0_gw", D, D), ("a0_gb", 1, D), ("a0_gain", H // 2, P),
              ("a0_wo", D, D), ("a0_bo", D, NQ),
              ("f0_router", E0, D), ("f0_shared", 2 * F0, D), ("f0_wd", 2 * D, P),
              ("a1_wq", D, D), ("a1_wk", D, D), ("a1_wv", D, D), ("a1_wo", D, D),
              ("a1_s", 4, P), ("a1_bq", 1, D), ("a1_bk", 1, D), ("a1_bv", D, P), ("a1_bo", D, NQ),
              ("f1_lng", D, NQ), ("f1_lnb", D, NQ), ("f1_bn", 4, D), ("f1_wr", E1, D), ("f1_br", E1, P),
              ("f1_wd", F1 * E1, D), ("f1_bd", E1, F1), ("f1_wu", D * E1, F1), ("f1_bu", D * E1, NQ)]
    out = []
    for lot in (first, second):
        at, cols = 0, {}
        for name, n, rows in lot:
            cols[name] = (at, n, rows)
            at += n
        out.append((cols, at))
    return out


def skew_back(skew, g):
    return bass.AP(tensor=skew.tensor, offset=g * (H // 2) * NQ + NQ - 1, ap=[[H * NQ - 1, NQ], [NQ, H // 2], [1, NQ]])


def bias_rows(bias, g):
    return bass.AP(tensor=bias.tensor, offset=g * (H // 2) * P + NQ - 1, ap=[[H * P - 1, NQ], [P, H // 2], [1, NQ]])


def perceiver(nc, x_in, ctx_in, mask_in, pack1_in, pack2_in, bias_in, gup_in, down_in, ones_in, skew, x_out):
    (cols1, n1), (cols2, n2) = pack_layout()
    with ExitStack() as stack:
        def sb(name, shape, dt=F32):
            return stack.enter_context(nc.sbuf_tensor(name, shape, dt))

        def pb(name, shape):
            return stack.enter_context(nc.psum_tensor(name, shape, F32))

        def sem(name):
            return stack.enter_context(nc.semaphore(name))

        ctxT = sb("ctxT", [P, NK])
        kpart = sb("kpart", [P, 3, NK], BF16)
        kstack = sb("kstack", [P, 2, NK], BF16)
        vones = sb("vones", [P, NKT, PAIRS, VC])
        pack1 = sb("pack1", [P, n1])
        pack2 = sb("pack2", [P, n2])
        shared = sb("shared", [P, E0 * 2 * F0])
        gup = shared[:, :].rearrange("p (e f) -> p e f", e=E0)
        at = 0

        def part(n):
            nonlocal at
            at += n
            return shared[:, at - n:at]

        maskadd = part(NK // 2).bitcast(BF16)
        probs = part(2 * SW).rearrange("p (b n) -> p b n", b=2)
        vcur = part(2 * NKT * VC).rearrange("p (b t c) -> p b t c", b=2, t=NKT)
        junk = part(2 * CW).rearrange("p (b n) -> p b n", b=2)
        assert at <= E0 * 2 * F0
        mask_u8 = probs.rearrange("p b n -> p (b n)").bitcast(U8)[:, 0:NK]
        kres = sb("kres", [P, 2, CW])
        qstack = sb("qstack", [P, PAIRS, 2, NQ], BF16)
        qmax = sb("qmax", [P, 2, P], BF16)
        qexp = sb("qexp", [P, 2, P], BF16)
        identb = sb("identb", [P, P], BF16)
        qf = sb("qf", [P, PAIRS * NQ])
        qh = sb("qh", [P, PAIRS * NQ], BF16)
        qm = sb("qm", [P, PAIRS * NQ], BF16)
        ql = sb("ql", [P, PAIRS * NQ], BF16)
        mx = sb("mx", [P, 2, NCH])
        negm = sb("negm", [P, 4])
        m3 = sb("m3", [P, 4], BF16)
        acc_sb = sb("acc_sb", [P, P])
        o17 = sb("o17", [P, PAIRS, VC])
        den = sb("den", [P, PAIRS])
        rden = sb("rden", [P, PAIRS])
        onorm = sb("onorm", [P, PAIRS, HD])
        oT = sb("oT", [NQ, P])
        x = sb("x", [NQ, D])
        st = sb("st", [P, 6])
        mv = sb("mv", [P, 2])
        warm = sb("warm", [1, 16])
        rstd = sb("rstd", [P, 1])
        xn = sb("xn", [NQ, D])
        xz = sb("xz", [NQ, D])
        xnT = sb("xnT", [P, 2, NQ])
        big = sb("big", [P, H * NQ])
        big2 = sb("big2", [P, H * NQ])
        w512 = sb("w512", [P, 512])
        v512 = sb("v512", [P, 512])
        qr, qc = w512, v512
        rest = kstack[:, :, :].rearrange("p b n -> p (b n)").bitcast(F32)
        down = rest[:, 0:2 * E0 * D].rearrange("p (f e n) -> p f e n", f=2, e=E0)
        qT = sb("qT", [P, NQ])
        kT = sb("kT", [P, NQ])
        vbd = rest[:, 2 * E0 * D:2 * E0 * D + PAIRS * D].rearrange("p (a n) -> p a n", a=PAIRS)
        ogT = sb("ogT", [P, NQ])
        gt = sb("gt", [P, NQ])
        ngb = sb("ngb", [P, 1])
        bnr = sb("bnr", [P, 2])
        bias_t = sb("bias_t", [P, 512])
        red = sb("red", [P, H])
        red2 = sb("red2", [P, H])
        small = sb("small", [P, 16])
        onehot = sb("onehot", [P, E0])
        onehot2 = sb("onehot2", [P, E0])

        def w(name):
            cols, pack = (cols1, pack1) if name in cols1 else (cols2, pack2)
            c, n, rows = cols[name]
            return pack[0:rows, c:c + n]

        ident = w("ident")
        routing = big[:, :].rearrange("p (e t) -> p e t", e=E0)

        smax = [pb(f"smax{b}", [P, 512]) for b in range(2)]
        sexp = [pb(f"sexp{b}", [P, 1024]) for b in range(2)]
        acc = pb("acc", [P, 512])
        misc = pb("misc", [P, 512])

        NAMES = """x_in pack1_in pack2_in mask_in gup_in down_in se_out se_in bias_in x_out
            mask_ready identb_ready ones_ready vones_ready ones_in act_chain dve_chain pool_chain
            ln_var ln_rstd ln_xn ln_xt xt_ready""".split()
        S = {n: sem(n) for n in NAMES}
        ctx_landed = [sem(f"ctx_landed{g}") for g in range(STEPS)]
        LNAMES = """qrep_done qstack_ready kproj_done khigh_done kproj_taken kmid_done klow_done
            vproj_done vproj_taken qmax_ready qexp_ready vcur_ready
            smax_done smax_taken m3_ready mt_done qm_ready sexp_done exp_done pv_done
            acc_copied sum_done o17_taken on_ready ot_done ot_ready y_done passed pool_passed mx_chain""".split()
        LS = [{n: sem(f"{n}_{L}") for n in LNAMES} for L in range(2)]
        stack_landed = [[sem(f"stack_landed_{b}_{h}") for h in range(len(PORTIONS[0]))] for b in range(2)]
        T = {n: sem(n) for n in """se_bd kbd_ready qkv_done qk_ready v_ready s_done se_done se_taken
            t_ready exp_ready exps p_ready pt_done pt_ready ot2_done gate_e og_ready y2_done x2_ready
            r_done r_e route_ready xm_done xm_ready h_done h_e a_ready at_done at_ready yf_done xf_ready
            b_qkv_done b_kbd_ready b_v_ready b_s_done b_exp_ready b_exps b_p_ready b_pt_done b_pt_ready
            b_ot_done b_og_ready b_y_done b_x_ready
            z_ready bn_rs zb_ready g_done g_ready g_e oh_ready ohb_done wsel_ready
            zt_done zt_ready h1_done h1_ready y1_done out_ready""".split()}

        block = stack.enter_context(nc.Block())

        @block.sync
        def _(sp):
            def ones_rows():
                sp.dma_start(kstack[MROW:MROW + 3, :, :].rearrange("p b n -> p (b n)"), ones_in).then_inc(S["ones_in"], 16)

            sp.dma_start(x[:, :], x_in).then_inc(S["x_in"], 16)
            sp.dma_start(pack1[:, :], pack1_in).then_inc(S["pack1_in"], 16)
            for g in range(STEPS):
                sp.dma_start(ctxT[:, g * SW:(g + 1) * SW], ctx_in[:, g * SW:(g + 1) * SW]).then_inc(ctx_landed[g], 16)
                if g == 0:
                    sp.dma_start(mask_u8[0:NQ, :], mask_in).then_inc(S["mask_in"], 16)
                    sp.dma_start(mask_u8[NQ:P, :], mask_in).then_inc(S["mask_in"], 16)
            ones_rows()

            def refill(L, p):
                for h, (a, b) in enumerate(PORTIONS[L]):
                    if p >= 2:
                        sp.wait_ge(LS[L]["sexp_done"], STEPS * (p - 2) + b)
                    elif p == 0:
                        sp.wait_ge(LS[L]["klow_done"], 2 * b)
                    for t, k in enumerate(K_TERM):
                        sp.dma_start(kstack[t * 16:t * 16 + 16, p % 2, a * SW:b * SW],
                                     kpart[p * 16:p * 16 + 16, k, a * SW:b * SW]
                                     ).then_inc(stack_landed[p % 2][h], 16)

            for p in range(PAIRS):
                refill(0, p)
                if 1 <= p <= PACK2_CUTS:
                    cut = slice(n2 * (p - 1) // PACK2_CUTS, n2 * p // PACK2_CUTS)
                    sp.dma_start(pack2[:, cut], pack2_in[:, cut]).then_inc(S["pack2_in"], 16)
            for g in range(2):
                sp.dma_start(bias_t[g * NQ:(g + 1) * NQ, :].rearrange("p (h j) -> p h j", j=NQ),
                             bias_rows(bias_in, g)).then_inc(S["bias_in"], 16)
            sp.wait_ge(LS[0]["pv_done"], PAIRS * STEPS + 2)
            sp.wait_ge(LS[0]["smax_taken"], PAIRS * NCH)
            sp.dma_start(gup, gup_in).then_inc(S["gup_in"], 16)
            sp.dma_start(down, down_in).then_inc(S["down_in"], 16)
            sp.wait_ge(T["se_taken"], 1)
            sp.dma_start(skew.rearrange("(q n) -> q n", q=NQ), big2[0:NQ, :]).then_inc(S["se_out"], 16)
            sp.wait_ge(S["se_out"], 16)
            for g in range(2):
                sp.dma_start(qf[g * NQ:(g + 1) * NQ, :].rearrange("p (h j) -> p h j", j=NQ),
                             skew_back(skew, g)).then_inc(S["se_in"], 16)
            sp.wait_ge(T["yf_done"], 2)
            ones_rows()
            for p in range(PAIRS):
                refill(1, p)
            sp.wait_ge(T["out_ready"], 1)
            sp.dma_start(x_out, x[:, :]).then_inc(S["x_out"], 16)
            sp.wait_ge(S["x_out"], 16)

        @block.tensor
        def _(pe):
            def ln_transpose(n):
                pe.wait_ge(S["ln_xn"], n + 1)
                pe.transpose(misc[:, 0:NQ], xn[:, :], ident[0:NQ, 0:NQ]).then_inc(S["ln_xt"], 1)
                pe.wait_ge(S["xt_ready"], n + 1)

            def project_q(L):
                q = LS[L]
                for p in range(PAIRS):
                    last = pe.matmul(acc[0:ROWS, p * NQ:(p + 1) * NQ], w(f"wq{L}")[:, p * ROWS:(p + 1) * ROWS],
                                     xnT[:, 0, :], start=True, stop=True)
                last.then_inc(q["qrep_done"], 1)

            def k_chunk(L, c):
                q = LS[L]
                if L == 0 and c % 2 == 0:
                    pe.wait_ge(ctx_landed[c // 2], 16)
                if c >= 2:
                    pe.wait_ge(q["kproj_taken"], c - 1)
                pe.matmul(smax[c % 2][:, 0:CW], w(f"wk{L}"), ctxT[:, c * CW:(c + 1) * CW],
                          start=True, stop=True).then_inc(q["kproj_done"], 1)

            def v_tile(L, kt):
                q = LS[L]
                g, t = kt // TPS, kt % TPS
                if t == 0 and g >= 2:
                    pe.wait_ge(q["vproj_taken"], g - 1)
                ins = pe.matmul(sexp[g % 2][:, t * P:(t + 1) * P], ctxT[:, kt * P:(kt + 1) * P],
                                w(f"wv{L}"), start=True, stop=True)
                if t == TPS - 1:
                    ins.then_inc(q["vproj_done"], 1)

            def project_kv(L):
                for c in range(NCH):
                    k_chunk(L, c)
                    if c in V_AFTER:
                        for t in range(TPS):
                            v_tile(L, V_AFTER.index(c) * TPS + t)

            def cross(L):
                q = LS[L]

                def max_chunks(pair, b, chunks):
                    for n in chunks:
                        if n == 0:
                            pe.wait_ge(q["qmax_ready"], pair + 1)
                        for h, (a, _) in enumerate(PORTIONS[L]):
                            if n == 2 * a:
                                pe.wait_ge(stack_landed[b][h], (L * PAIRS + pair - b) * (8 * TERMS) + 16 * TERMS)
                        if isinstance(pair, int) and pair == 0 and n < 2:
                            pe.wait_ge(q["kproj_taken"], NCH - 1 + n)
                        else:
                            pe.wait_ge(q["smax_taken"], pair * NCH + (n - 1))
                        pe.matmul(smax[n % 2][:, 0:CW], qmax[0:ROWS, b, :], kstack[0:ROWS, b, n * CW:(n + 1) * CW],
                                  start=True, stop=True).then_inc(q["smax_done"], 1)

                def max_to_rows(pair):
                    pe.wait_ge(q["m3_ready"], pair + 1)
                    pe.matmul(misc[MROW:MROW + 3, 0:P], m3[:, 0:3], identb[:, :], start=True, stop=True,
                              tile_position=(0, MROW)).then_inc(q["mt_done"], 1)

                def scores(s, pair, b, j, buf):
                    if j == 0:
                        pe.wait_ge(q["qm_ready"], pair + 1)
                    pe.wait_ge(q["exp_done"], s + 1)
                    for t in range(TPS):
                        ks = slice((j * TPS + t) * P, (j * TPS + t + 1) * P)
                        o = sexp[buf][:, t * P:(t + 1) * P]
                        if L == 0:
                            pe.matmul(o, maskadd[:, ks], identb[:, :], start=True, stop=False)
                        last = pe.matmul(o, kstack[0:MROW + 3, b, ks], qexp[0:MROW + 3, b, :],
                                         start=L != 0, stop=True)
                    last.then_inc(q["sexp_done"], 1)

                def times_v(s, pair, b, j, buf):
                    if j == 0:
                        pe.wait_ge(q["vcur_ready"], pair + 1)
                        if not (isinstance(pair, int) and pair == 0):
                            pe.wait_ge(q["acc_copied"], pair)
                    pe.wait_ge(q["exp_done"], s + 3)
                    for t in range(TPS):
                        g = t % 4
                        last = pe.matmul(acc[32 * g:32 * g + VC, 0:P], vcur[:, b, j * TPS + t, :],
                                         probs[:, buf, t * P:(t + 1) * P],
                                         start=(j == 0 and t < 4), stop=(j == STEPS - 1 and t >= TPS - 4),
                                         tile_position=(0, 32 * g))
                    last.then_inc(q["pv_done"], 1)

                def sum_groups(pair):
                    pe.wait_ge(q["acc_copied"], pair + 1)
                    pe.matmul(misc[:, P:P + VC], acc_sb[:, :], w("sum4"), start=True, stop=True
                              ).then_inc(q["sum_done"], 1)

                def step(i, k, ahead=True):
                    s = i * (2 * STEPS) + k
                    j, pair, b = k % STEPS, i * 2 + k // STEPS, (k // STEPS) % 2
                    if ahead:
                        c = sum(CHUNKS[L][:j])
                        max_chunks(pair + 1, 1 - b, range(c, c + CHUNKS[L][j]))
                    k1 = k - 1
                    if j:
                        scores(s, pair, b, j, k % 2)
                    times_v(s - 1, i * 2 + k1 // STEPS, (k1 // STEPS) % 2, k1 % STEPS, k1 % 2)
                    if j == 0:
                        scores(s, pair, b, j, k % 2)
                    if j == 1 and k > STEPS:
                        sum_groups(pair - 1)
                    if j == STEPS - 1 and ahead:
                        pe.wait_ge(q["o17_taken"], pair + 1)
                        max_to_rows(pair + 1)

                pe.sem_inc(q["pv_done"], 2)
                pe.sem_inc(q["mt_done"], 1)
                for n in range(NCH):
                    max_chunks(0, 0, range(n, n + 1))
                    rest_v = NKT - len(V_AFTER) * TPS
                    for t in range(rest_v * n // NCH, rest_v * (n + 1) // NCH):
                        v_tile(L, len(V_AFTER) * TPS + t)
                pe.wait_ge(q["vproj_taken"], STEPS)
                max_to_rows(0)
                max_chunks(1, 1, range(CHUNKS[L][0]))
                scores(0, 0, 0, 0, 0)
                step(0, 1)
                step(0, 2)
                with pe.Fori(0, PAIRS // 2 - 1) as i:
                    for k in range(3, 2 * STEPS + 3):
                        step(i, k)
                for k in range(3, 2 * STEPS):
                    step(PAIRS // 2 - 1, k, ahead=k < STEPS)
                times_v(PAIRS * STEPS - 1, PAIRS - 1, 1, STEPS - 1, 1)
                sum_groups(PAIRS - 1)

            def cross_out(L):
                q = LS[L]
                pe.wait_ge(q["on_ready"], 2)
                pe.transpose(misc[0:NQ, 0:P], onorm[:, :, :].rearrange("p a d -> p (a d)"), ident).then_inc(q["ot_done"], 1)
                pe.wait_ge(q["ot_ready"], 1)
                for e in range(2):
                    last = pe.matmul(acc[0:NQ, D:2 * D], oT[:, e * NQ:(e + 1) * NQ], w(f"wo{L}")[:, e * D:(e + 1) * D],
                                     start=e == 0, stop=e == 1)
                last.then_inc(q["y_done"], 1)

            pe.wait_ge(S["pack1_in"], 16)
            ln_transpose(0)
            pe.wait_ge(S["ones_ready"], 1)
            project_q(0)
            project_kv(0)
            pe.wait_ge(S["mask_ready"], 2)
            pe.wait_ge(S["identb_ready"], 1)
            pe.wait_ge(S["ones_in"], 16)
            cross(0)
            pe.wait_ge(S["pack2_in"], 16 * PACK2_CUTS)
            cross_out(0)

            ln_transpose(1)
            pe.matmul(misc[:, 64:128], w("a0_wq"), xnT[:, 0, :], start=True, stop=True)
            pe.matmul(misc[:, 128:192], w("a0_wk"), xnT[:, 0, :], start=True, stop=True)
            pe.matmul(misc[:, 192:256], w("a0_gw"), xnT[:, 0, :], start=True, stop=True)
            pe.matmul(misc[:, 256:384], xnT[:, :, :].rearrange("p a n -> p (a n)"), w("a0_wv"),
                      start=True, stop=True).then_inc(T["qkv_done"], 1)
            pe.wait_ge(T["qk_ready"], 1)
            for hf in range(2):
                last = pe.matmul(sexp[1][0:NQ, hf * 512:(hf + 1) * 512], qT[:, :], big2[:, hf * 512:(hf + 1) * 512],
                                 start=True, stop=True)
            last.then_inc(T["se_done"], 1)
            pe.wait_ge(T["kbd_ready"], 1)
            for g in range(2):
                last = pe.matmul(sexp[0][g * NQ:(g + 1) * NQ, 0:512], qT[:, :], big[:, g * 512:(g + 1) * 512],
                                 start=True, stop=True, tile_position=(0, g * NQ))
            last.then_inc(T["s_done"], 1)
            pe.wait_ge(T["p_ready"], 1)
            for b in range(4):
                last = pe.transpose(sexp[0][:, 512 + b * P:512 + (b + 1) * P], w512[:, b * P:(b + 1) * P], ident)
            last.then_inc(T["pt_done"], 1)
            pe.wait_ge(T["pt_ready"], 1)
            pe.wait_ge(T["v_ready"], 2)
            for n in range(PAIRS):
                last = pe.matmul(misc[:, 384:448], vbd[:, n, :], v512[:, (n % 4) * P + (n // 4) * NQ:(n % 4) * P + (n // 4) * NQ + NQ],
                                 start=n == 0, stop=n == PAIRS - 1)
            last.then_inc(T["ot2_done"], 1)
            pe.wait_ge(T["og_ready"], 1)
            pe.matmul(acc[0:NQ, D:2 * D], ogT[:, :], w("a0_wo"), start=True, stop=True).then_inc(T["y2_done"], 1)

            ln_transpose(2)
            pe.matmul(misc[0:NQ, 64:64 + E0], xnT[:, 0, :], w("f0_router"), start=True, stop=True).then_inc(T["r_done"], 1)
            pe.wait_ge(T["route_ready"], 2)
            for hf in range(2):
                last = pe.matmul(sexp[0][:, hf * 512:(hf + 1) * 512], xz[:, :], big[0:NQ, hf * 512:(hf + 1) * 512],
                                 start=True, stop=True)
            last.then_inc(T["xm_done"], 1)
            pe.matmul(sexp[1][NQ:P, 0:2 * F0], xnT[:, 0, :], w("f0_shared"), start=True, stop=True, tile_position=(0, NQ))
            pe.wait_ge(T["xm_ready"], 1)
            pe.wait_ge(S["gup_in"], 16)
            for e in range(E0):
                last = pe.matmul(sexp[1][0:NQ, 0:2 * F0], big2[:, e * NQ:(e + 1) * NQ], gup[:, e, :],
                                 start=e == 0, stop=e == E0 - 1, tile_position=(0, 0))
            last.then_inc(T["h_done"], 1)
            pe.wait_ge(T["a_ready"], 1)
            pe.wait_ge(S["down_in"], 16)
            for f in range(2):
                fs = slice(f * P, (f + 1) * P)
                pe.transpose(misc[:, f * NQ:(f + 1) * NQ], w512[NQ:P, fs], ident[NQ:P, NQ:P])
                for hf in range(2):
                    last = pe.matmul(sexp[0][:, hf * 512:(hf + 1) * 512], w512[0:NQ, fs], big[0:NQ, hf * 512:(hf + 1) * 512],
                                     start=True, stop=True)
                last.then_inc(T["at_done"], 1)
                pe.wait_ge(T["at_ready"], f + 1)
                for e in range(E0):
                    pe.matmul(acc[0:NQ, D:2 * D], big2[:, e * NQ:(e + 1) * NQ], down[:, f, e, :],
                              start=f == 0 and e == 0, stop=False)
                last = pe.matmul(acc[0:NQ, D:2 * D], gt[:, :], w("f0_wd")[:, f * D:(f + 1) * D], start=False, stop=f == 1)
                last.then_inc(T["yf_done"], 1)

            ln_transpose(3)
            project_q(1)
            project_kv(1)
            pe.wait_ge(S["ones_in"], 32)
            cross(1)
            cross_out(1)

            ln_transpose(4)
            pe.matmul(misc[:, 64:128], w("a1_wq"), xnT[:, 0, :], start=True, stop=True)
            pe.matmul(misc[:, 128:192], w("a1_wk"), xnT[:, 0, :], start=True, stop=True)
            pe.matmul(misc[:, 256:384], xnT[:, :, :].rearrange("p a n -> p (a n)"), w("a1_wv"),
                      start=True, stop=True).then_inc(T["b_qkv_done"], 1)
            pe.wait_ge(T["b_kbd_ready"], 1)
            for g in range(2):
                last = pe.matmul(sexp[0][g * NQ:(g + 1) * NQ, 0:512], qT[:, :], big[:, g * 512:(g + 1) * 512],
                                 start=True, stop=True, tile_position=(0, g * NQ))
            last.then_inc(T["b_s_done"], 1)
            pe.wait_ge(T["b_p_ready"], 1)
            for b in range(4):
                last = pe.transpose(sexp[0][:, 512 + b * P:512 + (b + 1) * P], w512[:, b * P:(b + 1) * P], ident)
            last.then_inc(T["b_pt_done"], 1)
            pe.wait_ge(T["b_pt_ready"], 1)
            pe.wait_ge(T["b_v_ready"], 2)
            for n in range(PAIRS):
                last = pe.matmul(misc[:, 384:448], vbd[:, n, :], v512[:, (n % 4) * P + (n // 4) * NQ:(n % 4) * P + (n // 4) * NQ + NQ],
                                 start=n == 0, stop=n == PAIRS - 1)
            last.then_inc(T["b_ot_done"], 1)
            pe.wait_ge(T["b_og_ready"], 1)
            pe.matmul(acc[0:NQ, D:2 * D], ogT[:, :], w("a1_wo"), start=True, stop=True).then_inc(T["b_y_done"], 1)

            pe.wait_ge(T["z_ready"], 1)
            pe.matmul(misc[:, 64:65], xz[:, :], small[0:NQ, 0:1], start=True, stop=True)
            pe.transpose(misc[:, 128:192], xz[:, :], ident[0:NQ, 0:NQ]).then_inc(T["zt_done"], 1)
            pe.wait_ge(T["zb_ready"], 1)
            pe.matmul(sexp[0][:, 0:E1], w512[:, 0:P], w("f1_wr"),
                      start=True, stop=True).then_inc(T["g_done"], 1)
            pe.wait_ge(T["wsel_ready"], 1)
            pe.wait_ge(T["zt_ready"], 1)
            pe.matmul(acc[0:F1, 0:NQ], v512[:, 0:F1], qT[:, :], start=True, stop=True).then_inc(T["h1_done"], 1)
            pe.wait_ge(T["h1_ready"], 1)
            pe.matmul(sexp[1][0:NQ, 0:D], kT[0:F1, :], v512[0:F1, 128:256], start=True, stop=True).then_inc(T["y1_done"], 1)

        @block.scalar
        def _(act):
            chain = [0]

            def link(ins):
                chain[0] += 1
                ins.then_inc(S["act_chain"], 1)
                act.wait_ge(S["act_chain"], chain[0])

            def load_table(func, n):
                act.activation(warm[0:1, n:n + 1], w("eps")[0:1, :], func)

            def std(n):
                act.wait_ge(S["ln_var"], n + 1)
                act.activation(rstd[0:NQ, :], mv[0:NQ, 1:2], ACT.Sqrt, bias=w("eps")[0:NQ, :]).then_inc(S["ln_rstd"], 1)
                load_table(ACT.Exp, 2 * n + 1)

            def take_kv(L):
                q = LS[L]
                bias = w("bk1") if L else w("zero")
                for c in range(NCH + 1):
                    if c < NCH:
                        act.wait_ge(q["kproj_done"], c + 1)
                        act.activation(kpart[:, 0, c * CW:(c + 1) * CW], smax[c % 2][:, 0:CW], ACT.Identity, bias=bias
                                       ).then_inc(q["khigh_done"], 1)
                    if c - 2 in V_AFTER:
                        take_v(L, V_AFTER.index(c - 2))
                    if c:
                        act.wait_ge(q["kproj_taken"], c)
                        act.activation(kpart[:, 1, (c - 1) * CW:c * CW], kres[:, (c - 1) % 2, :], ACT.Copy
                                       ).then_inc(q["kmid_done"], 1)

            def take_v(L, g):
                q = LS[L]
                act.wait_ge(q["vproj_done"], g + 1)
                act.activation(vones[:, g * TPS:(g + 1) * TPS, :, 0:2 * HD],
                               sexp[g % 2][:, 0:SW].rearrange("p (t a c) -> p t a c", t=TPS, a=PAIRS),
                               ACT.Copy).then_inc(q["vproj_taken"], 1)

            def cross(L):
                q = LS[L]

                def exps(s, buf):
                    act.wait_ge(q["sexp_done"], s + 1)
                    act.wait_ge(q["pv_done"], s + 1)
                    act.activation(probs[:, buf, :], sexp[buf][:, 0:SW], ACT.Exp).then_inc(q["exp_done"], 1)

                def take_acc(pair):
                    act.wait_ge(q["pv_done"], pair * STEPS + STEPS + 2)
                    act.activation(acc_sb[:, :], acc[:, 0:P], ACT.Copy).then_inc(q["acc_copied"], 1)

                def take_sum(pair):
                    act.wait_ge(q["sum_done"], pair + 1)
                    o = o17[:, pair, :] if isinstance(pair, int) else \
                        o17[:, :, :].rearrange("p a c -> p (a c)")[:, bass.ds(pair * VC, VC)]
                    act.activation(o, misc[:, P:P + VC], ACT.Copy).then_inc(q["o17_taken"], 1)

                def take_rows(pair, b):
                    act.wait_ge(q["qexp_ready"], pair + 1)
                    act.wait_ge(q["mt_done"], pair + 2)
                    act.activation(qexp[MROW:MROW + 3, b, :], misc[MROW:MROW + 3, 0:P], ACT.Copy
                                   ).then_inc(q["qm_ready"], 1)

                def step(i, k, ahead=True):
                    exps(i * (2 * STEPS) + k, k % 2)
                    if ahead and k % STEPS == STEPS - 1:
                        take_rows(i * 2 + k // STEPS + 1, (k // STEPS + 1) % 2)
                    if k >= STEPS and k % STEPS == 0:
                        take_acc(i * 2 + k // STEPS - 1)
                    if k >= STEPS and k % STEPS == 2:
                        take_sum(i * 2 + k // STEPS - 1)

                for g in range(len(V_AFTER), STEPS):
                    take_v(L, g)
                act.sem_inc(q["exp_done"], 2)
                act.sem_inc(q["o17_taken"], 1)
                take_rows(0, 0)
                for k in range(3):
                    step(0, k)
                with act.Fori(0, PAIRS // 2 - 1) as i:
                    for k in range(3, 2 * STEPS + 3):
                        step(i, k)
                for k in range(3, 2 * STEPS):
                    step(PAIRS // 2 - 1, k, ahead=k < STEPS)
                take_acc(PAIRS - 1)
                take_sum(PAIRS - 1)

            act.wait_ge(S["pack1_in"], 16)
            load_table(ACT.Sqrt, 0)
            std(0)
            take_kv(0)
            cross(0)
            act.wait_ge(S["pack2_in"], 16 * PACK2_CUTS)
            act.activation(bnr[:, 0:1], w("f1_bn")[:, 3:4], ACT.Sqrt, bias=w("eps")).then_inc(T["bn_rs"], 1)
            std(1)
            act.wait_ge(T["se_done"], 1)
            act.activation(big2[0:NQ, :], sexp[1][0:NQ, :], ACT.Copy, scale=SCALE, bias=SCALE).then_inc(T["se_taken"], 1)
            act.wait_ge(T["qk_ready"], 1)
            act.activation(gt[:, :], misc[:, 192:256], ACT.Exp, scale=-1.0, bias=ngb[:, 0:1]).then_inc(T["gate_e"], 1)
            act.wait_ge(T["exp_ready"], 1)
            act.activation(w512[:, :], w512[:, :], ACT.Exp).then_inc(T["exps"], 1)
            load_table(ACT.Sqrt, 4)
            std(2)
            act.wait_ge(T["r_e"], 1)
            act.activation(small[0:NQ, 2:3], small[0:NQ, 1:2], ACT.Exp, scale=-1.0).then_inc(T["r_e"], 1)
            act.wait_ge(T["h_done"], 1)
            act.activation(v512[:, 0:F0], sexp[1][:, 0:F0], ACT.Exp, scale=-1.0).then_inc(T["h_e"], 1)
            load_table(ACT.Sqrt, 6)
            std(3)
            act.wait_ge(LS[0]["vcur_ready"], PAIRS)
            take_kv(1)
            cross(1)
            load_table(ACT.Sqrt, 8)
            std(4)
            act.wait_ge(T["b_exp_ready"], 1)
            act.activation(w512[:, :], w512[:, :], ACT.Exp).then_inc(T["b_exps"], 1)
            load_table(ACT.Sqrt, 10)
            std(5)
            load_table(ACT.Sqrt, 12)
            std(6)
            act.wait_ge(T["g_ready"], 1)
            act.activation(red2[:, 0:E1], red[:, 0:E1], ACT.Exp, accum_out=small[:, 4:5]).then_inc(T["g_e"], 1)

        @block.vector
        def _(dve):
            chain = [0]

            def link(ins):
                chain[0] += 1
                ins.then_inc(S["dve_chain"], 1)
                dve.wait_ge(S["dve_chain"], chain[0])

            def layernorm(n, src=None):
                src = x[:, :] if src is None else src
                link(dve.bn_stats(st[0:NQ, :], src))
                dve.bn_aggr(mv[0:NQ, :], st[0:NQ, :]).then_inc(S["ln_var"], 1)
                dve.wait_ge(S["ln_rstd"], n + 1)
                link(dve.reciprocal(rstd[0:NQ, :], rstd[0:NQ, :]))
                return dve.tensor_scalar(xn[:, :], src, mv[0:NQ, 0:1], rstd[0:NQ, 0:1], ALU.subtract, ALU.mult)

            def take_xt(n):
                dve.wait_ge(S["ln_xt"], n + 1)
                dve.tensor_copy(xnT[:, :, :], misc[:, 0:NQ].unsqueeze(1).to_broadcast([P, 2, NQ])).then_inc(S["xt_ready"], 1)

            def stack_q(L, stage):
                q = LS[L]
                R = slice(0, ROWS)
                sel = w("sel")
                by_pair = lambda t: t.rearrange("p (a n) -> p a n", a=PAIRS)
                src = acc[R, 0:PAIRS * NQ]
                if stage == 0:
                    dve.wait_ge(q["qrep_done"], 1)
                    if L:
                        link(dve.tensor_tensor(by_pair(qf[R, :]), by_pair(src),
                                               w("bq1").unsqueeze(2).to_broadcast([ROWS, PAIRS, NQ]), ALU.add))
                        src = qf[R, :]
                    link(dve.tensor_scalar(qf[R, :], src, SCALE, None, ALU.mult))
                elif stage == 1:
                    link(dve.tensor_copy(qh[R, :], qf[R, :]))
                elif stage == 2:
                    link(dve.tensor_tensor(qr[R, :], qf[R, :], qh[R, :], ALU.subtract))
                elif stage == 3:
                    link(dve.tensor_copy(qm[R, :], qr[R, :]))
                elif stage == 4:
                    link(dve.tensor_tensor(ql[R, :], qr[R, :], qm[R, :], ALU.subtract))
                elif stage == 5:
                    link(dve.tensor_scalar(qc[R, :], qh[R, :], sel[:, 0:1], None, ALU.mult))
                elif stage == 6:
                    link(dve.scalar_tensor_tensor(qc[R, :], qm[R, :], sel[:, 1:2], qc[R, :], ALU.mult, ALU.add))
                elif stage == 7:
                    link(dve.scalar_tensor_tensor(qc[R, :], ql[R, :], sel[:, 2:3], qc[R, :], ALU.mult, ALU.add))
                elif stage < 10:
                    e = stage - 8
                    dve.tensor_scalar(qstack[R, :, e, :], by_pair(qc[R, :]), sel[:, 3 + e:4 + e], None, ALU.mult
                                      ).then_inc(q["qstack_ready"], 1)

            def split_k(L):
                q = LS[L]
                bias = w("bk1") if L else w("zero")
                for c in range(NCH):
                    cs = slice(c * CW, (c + 1) * CW)
                    dve.wait_ge(q["khigh_done"], c + 1)
                    if c >= 2:
                        dve.wait_ge(q["klow_done"], c - 1)
                    dve.scalar_tensor_tensor(kres[:, c % 2, :], smax[c % 2][:, 0:CW], bias, kpart[:, 0, cs],
                                             ALU.add, ALU.subtract).then_inc(q["kproj_taken"], 1)
                    stack_q(L, c)

            def cross(L):
                q = LS[L]

                def one(pair, b):
                    for n in range(NCH):
                        dve.wait_ge(q["smax_done"], pair * NCH + n + 1)
                        if L == 0:
                            dve.sem_inc(q["passed"], 1)
                        if L == 0:
                            dve.tensor_tensor_reduce(junk[:, n % 2, :], smax[n % 2][:, 0:CW], maskadd[:, n * CW:(n + 1) * CW],
                                                     1.0, -3e38, ALU.add, ALU.max, mx[:, b, n:n + 1]
                                                     ).then_inc(q["smax_taken"], 1)
                        else:
                            dve.tensor_reduce(mx[:, b, n:n + 1], smax[n % 2][:, 0:CW], AX.X, ALU.max
                                              ).then_inc(q["smax_taken"], 1)
                    dve.wait_ge(q["smax_taken"], pair * NCH + NCH)
                    links = [0]

                    def next_reads(ins):
                        links[0] += 1
                        ins.then_inc(q["mx_chain"], 1)
                        dve.wait_ge(q["mx_chain"], pair * 3 + links[0])

                    next_reads(dve.tensor_reduce(negm[:, 0:1], mx[:, b, :], AX.X, ALU.max, negate=True))
                    most = -MASKED / 2 if L == 0 else 3e38
                    dve.wait_ge(q["mt_done"], pair + 1)
                    next_reads(dve.tensor_scalar(m3[:, 0:1], negm[:, 0:1], most, None, ALU.min))
                    dve.scalar_tensor_tensor(negm[:, 1:2], negm[:, 0:1], most, m3[:, 0:1], ALU.min, ALU.subtract)
                    next_reads(dve.scalar_tensor_tensor(m3[:, 1:2], negm[:, 0:1], most, m3[:, 0:1], ALU.min, ALU.subtract))
                    dve.tensor_tensor(m3[:, 2:3], negm[:, 1:2], m3[:, 1:2], ALU.subtract).then_inc(q["m3_ready"], 1)

                with dve.Fori(0, PAIRS // 2) as i:
                    one(i * 2, 0)
                    one(i * 2 + 1, 1)

            def cross_out(L):
                q = LS[L]
                dve.wait_ge(q["o17_taken"], PAIRS + 1)
                if L == 0:
                    link(dve.tensor_scalar(den[:, :], o17[:, :, VC - 1], 1e-9, None, ALU.max))
                link(dve.reciprocal(rden[:, :], den[:, :] if L == 0 else o17[:, :, VC - 1]))
                for e in range(2):
                    r = slice(e * NQ, (e + 1) * NQ)
                    ins = dve.tensor_tensor(onorm[r, :, :], o17[r, :, e * HD:(e + 1) * HD],
                                            rden[r, :].unsqueeze(2).to_broadcast([NQ, PAIRS, HD]), ALU.mult)
                    if L == 0:
                        ins.then_inc(q["on_ready"], 1)
                    else:
                        link(ins)
                if L:
                    dve.tensor_tensor(onorm[:, :, :], onorm[:, :, :], w("bv1").rearrange("p (a d) -> p a d", a=PAIRS),
                                      ALU.add).then_inc(q["on_ready"], 2)
                dve.wait_ge(q["ot_done"], 1)
                dve.tensor_copy(oT[:, :], misc[0:NQ, 0:P]).then_inc(q["ot_ready"], 1)
                dve.wait_ge(q["y_done"], 1)
                link(dve.tensor_tensor(x[:, :], acc[0:NQ, D:2 * D], x[:, :], ALU.add))
                if L:
                    link(dve.tensor_tensor(x[:, :], x[:, :], w("bo1"), ALU.add))

            dve.memset(acc[:, :], 0.0).then_inc(S["ones_ready"], 1)

            dve.wait_ge(S["x_in"], 16)
            layernorm(0).then_inc(S["ln_xn"], 1)
            take_xt(0)
            dve.tensor_copy(identb[:, :], ident).then_inc(S["identb_ready"], 1)
            split_k(0)
            dve.wait_ge(S["mask_ready"], 2)
            cross(0)
            dve.wait_ge(S["pack2_in"], 16 * PACK2_CUTS)
            cross_out(0)

            hm = w("hmask").unsqueeze(2).to_broadcast([P, H, NQ])

            def by_head(out, src):
                return dve.tensor_tensor(out[:, :].rearrange("p (h j) -> p h j", h=H),
                                         src.unsqueeze(1).to_broadcast([P, H, NQ]), hm, ALU.mult)

            def block_v(src_ready_inc):
                flat = vbd.rearrange("p a c -> p (a c)")
                for e in range(2):
                    r = slice(e * NQ, (e + 1) * NQ)
                    o = bass.AP(tensor=flat.tensor, offset=flat[r, :].offset + e * HD,
                                ap=[flat[r, :].ap[0], [D + 2 * HD, PAIRS], [1, HD]])
                    s = v512[r, 0:D].rearrange("p (a e d) -> p a e d", a=PAIRS, e=2)[:, :, e, :]
                    dve.tensor_copy(o, s).then_inc(src_ready_inc, 1)

            def softmax_heads(exp_ready, exps):
                w3 = w512[:, :].rearrange("p (h j) -> p h j", h=H // 2)
                link(dve.tensor_reduce(red[:, 0:H // 2], w3, AX.X, ALU.max))
                dve.tensor_tensor(w3, w3, red[:, 0:H // 2].unsqueeze(2).to_broadcast([P, H // 2, NQ]), ALU.subtract
                                  ).then_inc(exp_ready, 1)
                dve.wait_ge(exps, 1)
                link(dve.tensor_reduce(red2[:, 0:H // 2], w3, AX.X, ALU.add))
                link(dve.reciprocal(red[:, 0:H // 2], red2[:, 0:H // 2]))
                return w3

            link(by_head(big2, w("a0_se")))
            layernorm(1).then_inc(S["ln_xn"], 1)
            take_xt(1)
            link(dve.tensor_scalar(ngb[:, :], w("a0_gb"), -1.0, None, ALU.mult))
            dve.wait_ge(T["qkv_done"], 1)
            link(dve.tensor_scalar(kT[:, :], misc[:, 128:192], w("a0_bk"), None, ALU.add))
            dve.tensor_scalar(qT[:, :], misc[:, 64:128], w("a0_bq"), None, ALU.add).then_inc(T["se_bd"], 1)
            dve.wait_ge(T["se_bd"], 1)
            link(dve.tensor_tensor(v512[:, 0:D], misc[:, 256:384], w("a0_bv"), ALU.add))
            by_head(big, kT[:, :]).then_inc(T["kbd_ready"], 1)
            dve.memset(small[:, 0:1], 1.0 / NQ).then_inc(T["qk_ready"], 1)
            link(dve.memset(vbd, 0.0))
            block_v(T["v_ready"])
            dve.wait_ge(T["v_ready"], 2)
            dve.wait_ge(T["s_done"], 1)
            dve.wait_ge(S["se_in"], 32)
            link(dve.tensor_tensor(w512[:, :], sexp[0][:, 0:512], qf[:, :], ALU.mult))
            dve.wait_ge(S["bias_in"], 32)
            link(dve.tensor_tensor(w512[:, :], w512[:, :], bias_t[:, :], ALU.add))
            w3 = softmax_heads(T["exp_ready"], T["exps"])
            link(dve.tensor_tensor(red[:, 0:H // 2], red[:, 0:H // 2], w("a0_gain"), ALU.mult))
            dve.tensor_tensor(w3, w3, red[:, 0:H // 2].unsqueeze(2).to_broadcast([P, H // 2, NQ]), ALU.mult
                              ).then_inc(T["p_ready"], 1)
            dve.wait_ge(T["gate_e"], 1)
            link(dve.tensor_scalar(gt[:, :], gt[:, :], 1.0, None, ALU.add))
            link(dve.reciprocal(gt[:, :], gt[:, :]))
            dve.wait_ge(T["pt_done"], 1)
            dve.tensor_copy(v512[:, :], sexp[0][:, 512:1024]).then_inc(T["pt_ready"], 1)
            dve.wait_ge(T["ot2_done"], 1)
            dve.tensor_tensor(ogT[:, :], misc[:, 384:448], gt[:, :], ALU.mult).then_inc(T["og_ready"], 1)
            dve.wait_ge(T["y2_done"], 1)
            link(dve.tensor_tensor(x[:, :], acc[0:NQ, D:2 * D], x[:, :], ALU.add))
            link(dve.tensor_tensor(x[:, :], x[:, :], w("a0_bo"), ALU.add))

            layernorm(2).then_inc(S["ln_xn"], 1)
            take_xt(2)
            dve.wait_ge(T["r_done"], 1)

            def first_of_max(logits, rows, n, mxcol, out):
                link(dve.tensor_reduce(mxcol, logits, AX.X, ALU.max))
                link(dve.tensor_scalar(onehot[rows, 0:n], logits, mxcol, None, ALU.is_equal))
                link(dve.tensor_tensor(onehot[rows, 0:n], onehot[rows, 0:n], tie_row(rows, n), ALU.mult))
                link(dve.tensor_reduce(small[rows, 3:4], onehot[rows, 0:n], AX.X, ALU.max))
                return dve.tensor_scalar(out, onehot[rows, 0:n], small[rows, 3:4], None, ALU.is_equal)

            def tie_row(rows, n):
                return w("tie")[rows, E0 - n:E0]

            R = slice(0, NQ)
            first = dve.tensor_reduce(small[R, 1:2], misc[0:NQ, 64:64 + E0], AX.X, ALU.max)
            first.then_inc(T["r_e"], 1)
            dve.wait_ge(T["r_e"], 1)
            link(first_of_max(misc[0:NQ, 64:64 + E0], R, E0, small[R, 5:6], onehot2[R, :]))
            dve.tensor_tensor(routing[0:NQ, :, :], onehot2[R, :].unsqueeze(2).to_broadcast([NQ, E0, NQ]),
                              ident[0:NQ, 0:NQ].unsqueeze(1).to_broadcast([NQ, E0, NQ]), ALU.mult
                              ).then_inc(T["route_ready"], 1)
            dve.wait_ge(T["r_e"], 2)
            link(dve.tensor_scalar(small[R, 2:3], small[R, 2:3], 1.0, None, ALU.add))
            link(dve.reciprocal(small[R, 6:7], small[R, 2:3]))
            dve.tensor_scalar(xz[:, :], xn[:, :], small[R, 6:7], None, ALU.mult).then_inc(T["route_ready"], 1)
            dve.wait_ge(T["xm_done"], 1)
            dve.tensor_copy(big2[:, :], sexp[0][:, :]).then_inc(T["xm_ready"], 1)
            dve.wait_ge(T["h_e"], 1)
            link(dve.tensor_scalar(v512[:, 0:F0], v512[:, 0:F0], 1.0, None, ALU.add))
            link(dve.reciprocal(v512[:, 0:F0], v512[:, 0:F0]))
            link(dve.tensor_tensor(v512[:, 0:F0], sexp[1][:, 0:F0], v512[:, 0:F0], ALU.mult))
            dve.tensor_tensor(w512[:, 0:F0], sexp[1][:, F0:2 * F0], v512[:, 0:F0], ALU.mult).then_inc(T["a_ready"], 1)
            for f in range(2):
                dve.wait_ge(T["at_done"], f + 1)
                if f:
                    dve.wait_ge(T["yf_done"], 1)
                link(dve.tensor_copy(gt[:, :], misc[:, f * NQ:(f + 1) * NQ]))
                dve.tensor_copy(big2[:, :], sexp[0][:, :]).then_inc(T["at_ready"], 1)
            dve.wait_ge(T["yf_done"], 2)
            link(dve.tensor_tensor(x[:, :], acc[0:NQ, D:2 * D], x[:, :], ALU.add))

            layernorm(3).then_inc(S["ln_xn"], 1)
            take_xt(3)
            split_k(1)
            cross(1)
            cross_out(1)

            layernorm(4).then_inc(S["ln_xn"], 1)
            take_xt(4)
            dve.wait_ge(T["b_qkv_done"], 1)
            s4 = w("a1_s")
            link(dve.tensor_scalar(kT[:, :], misc[:, 128:192], s4[:, 1:2], w("a1_bk"), ALU.mult, ALU.add))
            link(dve.tensor_scalar(qT[:, :], misc[:, 64:128], s4[:, 0:1], w("a1_bq"), ALU.mult, ALU.add))
            link(dve.tensor_scalar(qT[:, :], qT[:, :], SCALE, None, ALU.mult))
            link(dve.scalar_tensor_tensor(v512[:, 0:D], misc[:, 256:384], s4[:, 2:3], w("a1_bv"), ALU.mult, ALU.add))
            by_head(big, kT[:, :]).then_inc(T["b_kbd_ready"], 1)
            link(dve.memset(vbd, 0.0))
            block_v(T["b_v_ready"])
            dve.wait_ge(T["b_s_done"], 1)
            link(dve.tensor_copy(w512[:, :], sexp[0][:, 0:512]))
            w3 = softmax_heads(T["b_exp_ready"], T["b_exps"])
            dve.tensor_tensor(w3, w3, red[:, 0:H // 2].unsqueeze(2).to_broadcast([P, H // 2, NQ]), ALU.mult
                              ).then_inc(T["b_p_ready"], 1)
            dve.wait_ge(T["b_pt_done"], 1)
            dve.tensor_copy(v512[:, :], sexp[0][:, 512:1024]).then_inc(T["b_pt_ready"], 1)
            dve.wait_ge(T["b_ot_done"], 1)
            dve.tensor_copy(ogT[:, :], misc[:, 384:448]).then_inc(T["b_og_ready"], 1)
            dve.wait_ge(T["b_y_done"], 1)
            link(dve.scalar_tensor_tensor(x[:, :], acc[0:NQ, D:2 * D], s4[0:NQ, 3:4], x[:, :], ALU.mult, ALU.add))
            link(dve.tensor_tensor(x[:, :], x[:, :], w("a1_bo"), ALU.add))

            link(layernorm(5))
            link(layernorm(6, xn[:, :]))
            link(dve.tensor_tensor(xn[:, :], xn[:, :], w("f1_lng"), ALU.mult))
            dve.tensor_tensor(xz[:, :], xn[:, :], w("f1_lnb"), ALU.add).then_inc(T["z_ready"], 1)
            bn = w("f1_bn")
            dve.wait_ge(T["bn_rs"], 1)
            link(dve.reciprocal(bnr[:, 0:1], bnr[:, 0:1]))
            dve.wait_ge(T["zt_done"], 1)
            link(dve.tensor_scalar(red[:, 2:3], misc[:, 64:65], bn[:, 2:3], bnr[:, 0:1], ALU.subtract, ALU.mult))
            link(dve.tensor_scalar(red[:, 3:4], red[:, 2:3], bn[:, 0:1], bn[:, 1:2], ALU.mult, ALU.add))
            link(dve.memset(big2[:, 0:P], 1.0))
            dve.tensor_scalar(w512[:, 0:P], big2[:, 0:P], red[:, 3:4], None, ALU.mult).then_inc(T["zb_ready"], 1)
            dve.tensor_copy(qT[:, :], misc[:, 128:192]).then_inc(T["zt_ready"], 1)
            dve.wait_ge(T["g_done"], 1)
            A = slice(0, P)
            link(dve.tensor_tensor(red2[:, 0:E1], sexp[0][:, 0:E1], w("f1_br"), ALU.add))
            link(first_of_max(red2[:, 0:E1], A, E1, small[:, 5:6], onehot2[:, 0:E1]))
            dve.tensor_scalar(red[:, 0:E1], red2[:, 0:E1], small[:, 5:6], None, ALU.subtract).then_inc(T["g_ready"], 1)
            oh = onehot2[:, 0:E1]

            def select(name, n, rows, out):
                src = w(name).rearrange("p (n e) -> p n e", e=E1)
                link(dve.tensor_tensor(big[0:rows, 0:n * E1].rearrange("p (n e) -> p n e", e=E1), src,
                                       oh[0:rows, :].unsqueeze(1).to_broadcast([rows, n, E1]), ALU.mult))
                return dve.tensor_reduce(out, big[0:rows, 0:n * E1].rearrange("p (n e) -> p n e", e=E1), AX.X, ALU.add)

            link(select("f1_wd", F1, D, v512[:, 0:F1]))
            select("f1_wu", D, F1, v512[0:F1, 128:256]).then_inc(T["wsel_ready"], 1)
            dve.wait_ge(T["wsel_ready"], 1)
            link(dve.tensor_tensor(big[0:F1, 0:E1], w("f1_bd")[:, 0:E1], oh[0:F1, :], ALU.mult))
            link(dve.tensor_reduce(small[0:F1, 8:9], big[0:F1, 0:E1], AX.X, ALU.add))
            dve.wait_ge(T["h1_done"], 1)
            dve.tensor_scalar(kT[0:F1, :], acc[0:F1, 0:NQ], small[0:F1, 8:9], 0.0, ALU.add, ALU.max).then_inc(T["h1_ready"], 1)
            link(select("f1_bu", D, NQ, v512[0:NQ, 256:384]))
            dve.wait_ge(T["g_e"], 1)
            link(dve.reciprocal(small[:, 7:8], small[:, 4:5]))
            dve.wait_ge(T["y1_done"], 1)
            link(dve.tensor_tensor(xz[:, :], sexp[1][0:NQ, 0:D], v512[0:NQ, 256:384], ALU.add))
            dve.scalar_tensor_tensor(x[:, :], xz[:, :], small[0:NQ, 7:8], x[:, :], ALU.mult, ALU.add
                                     ).then_inc(T["out_ready"], 1)

        @block.gpsimd
        def _(pool):
            def mask_half(h):
                half = slice(h * NK // 2, (h + 1) * NK // 2)
                pool.tensor_scalar(maskadd[:, half], mask_u8[:, half], -MASKED, MASKED, ALU.mult, ALU.add
                                   ).then_inc(S["mask_ready"], 1)

            def split_k(L):
                q = LS[L]
                for c in range(NCH):
                    if L == 0 and c == NCH - 4:
                        mask_half(1)
                    cs = slice(c * CW, (c + 1) * CW)
                    pool.wait_ge(q["kmid_done"], c + 1)
                    pool.tensor_tensor(kpart[:, 2, cs], kres[:, c % 2, :], kpart[:, 1, cs], ALU.subtract
                                       ).then_inc(q["klow_done"], 1)

            def cross(L):
                q = LS[L]
                qflat = qstack[:, :, :, :].rearrange("p a e n -> p (a e n)")
                vflat = vones[:, :, :, :].rearrange("p t a c -> p t (a c)")

                def one(pair, b, first):
                    qs = qflat[0:ROWS, pair * P:(pair + 1) * P] if isinstance(pair, int) else \
                        qflat[0:ROWS, bass.ds(pair * P, P)]
                    vs = vflat[:, :, pair * VC:(pair + 1) * VC] if isinstance(pair, int) else \
                        vflat[:, :, bass.ds(pair * VC, VC)]
                    pool.wait_ge(q["qstack_ready"], 2)
                    if not first:
                        pool.wait_ge(q["smax_done"], (pair - 1) * NCH)
                        pool.sem_inc(q["pool_passed"], 1)
                    pool.tensor_copy(qmax[0:ROWS, b, :], qs).then_inc(q["qmax_ready"], 1)
                    pool.wait_ge(q["qstack_ready"], 2)
                    if not first:
                        pool.wait_ge(q["sexp_done"], (pair - 1) * STEPS)
                        pool.sem_inc(q["pool_passed"], 1)
                    pool.tensor_copy(qexp[0:ROWS, b, :], qs).then_inc(q["qexp_ready"], 1)
                    pool.wait_ge(q["vproj_taken"], STEPS)
                    if not first:
                        pool.wait_ge(q["pv_done"], (pair - 1) * STEPS + 2)
                        pool.sem_inc(q["pool_passed"], 1)
                    pool.tensor_copy(vcur[:, b, :, :], vs).then_inc(q["vcur_ready"], 1)

                pool.wait_ge(S["vones_ready"], 1)
                one(0, 0, True)
                one(1, 1, True)
                with pool.Fori(1, PAIRS // 2) as i:
                    one(i * 2, 0, False)
                    one(i * 2 + 1, 1, False)

            pool.memset(vones[:, :, :, 2 * HD:VC], 1.0).then_inc(S["vones_ready"], 1)
            pool.wait_ge(S["mask_in"], 32)
            mask_half(0)
            split_k(0)
            pool.wait_ge(S["mask_ready"], 2)
            cross(0)
            split_k(1)
            pool.wait_ge(T["h_done"], 1)
            cross(1)


OFFSETS = sorted(set(range(33)) | {48, 64, 96, 128, 192})


def kernel(**inputs):
    import ml_dtypes
    import numpy as np
    import concourse.bacc as bacc
    from concourse.bass_utils import run_bass_kernel_spmd

    a = {k: np.asarray(v) for k, v in inputs.items()}
    rows = lambda v, n=P: np.broadcast_to(np.asarray(v).reshape(1, -1), (n, np.asarray(v).size))
    col = lambda v: np.asarray(v).reshape(-1, 1)
    pair_rows = np.array([[(2 * p + e) * HD + d for _ in range(TERMS) for e in range(2) for d in range(HD)]
                          for p in range(PAIRS)])

    def by_pairs(m):
        return m.T[:, pair_rows.reshape(-1)]

    def out_pairs(m):
        return m.T.reshape(PAIRS, 2, HD, D).transpose(0, 2, 1, 3).reshape(NQ, 2 * D)

    sel = np.zeros((ROWS, 5), np.float32)
    for r in range(ROWS):
        sel[r, Q_TERM[r // 16]] = 1
        sel[r, 3 + (r % 16) // HD] = 1
    sum4 = np.zeros((P, VC), np.float32)
    for g in range(4):
        sum4[32 * g + np.arange(VC), np.arange(VC)] = 1
    hmask = (np.arange(P)[:, None] // HD == np.arange(H)[None, :]).astype(np.float32)
    near = [o for o in OFFSETS if o < NQ]
    at = [NQ - 1 - o for o in near]
    se = np.zeros((HD, NQ), np.float32)
    se[:, at] = a["L0_attn_scale_embed"][:len(near)].T
    bias = np.full((H, P), NEG, np.float32)
    bias[:, at] = a["L0_attn_pos_bias"][:len(near)].T
    qkv, qkvb = a["L0_attn_qkv_w"], a["L0_attn_qkv_b"]
    gain = a["L0_attn_if_gain"].reshape(2, 1, H // 2)
    parts = {
        "ident": np.eye(P, dtype=np.float32), "hmask": hmask, "sel": sel, "sum4": sum4,
        "eps": np.full((P, 1), LN_EPS, np.float32), "tie": rows(np.arange(E0, 0, -1).astype(np.float32)),
        "zero": np.zeros((P, 1), np.float32),
        "a0_wq": qkv[0:D].T, "a0_wk": qkv[D:2 * D].T, "a0_wv": qkv[2 * D:].T,
        "a0_bq": col(qkvb[0:D]), "a0_bk": col(qkvb[D:2 * D]), "a0_bv": rows(qkvb[2 * D:]),
        "a0_se": np.tile(se, (H, 1)), "a0_gw": a["L0_attn_gate_w"].T, "a0_gb": col(a["L0_attn_gate_b"]),
        "a0_gain": np.broadcast_to(gain, (2, NQ, H // 2)).reshape(P, H // 2),
        "a0_wo": a["L0_attn_out_w"].T, "a0_bo": rows(a["L0_attn_out_b"], NQ),
        "f0_router": a["L0_ffn_w_router"].T,
        "f0_shared": np.concatenate([a["L0_ffn_w_gate"].T, a["L0_ffn_w_up"].T], 1),
        "f0_wd": a["L0_ffn_w_down"].T.reshape(2, P, D).transpose(1, 0, 2).reshape(P, 2 * D),
        "bk1": col(a["L1_xattn_bk"]), "bq1": a["L1_xattn_bq"][pair_rows].T,
        "bv1": np.repeat(a["L1_xattn_bv"].reshape(PAIRS, 2, HD).transpose(1, 0, 2).reshape(2, NQ), NQ, 0),
        "bo1": rows(a["L1_xattn_bo"], NQ),
        "a1_wq": a["L1_attn_w_q"].T, "a1_wk": a["L1_attn_w_k"].T, "a1_wv": a["L1_attn_w_v"].T, "a1_wo": a["L1_attn_w_o"].T,
        "a1_s": rows(np.stack([a[f"L1_attn_s_{n}"] for n in "qkvo"])),
        "a1_bq": col(a["L1_attn_b_q"]), "a1_bk": col(a["L1_attn_b_k"]),
        "a1_bv": rows(a["L1_attn_b_v"]), "a1_bo": rows(a["L1_attn_b_o"], NQ),
        "f1_lng": rows(a["L1_ffn_ln_g"], NQ), "f1_lnb": rows(a["L1_ffn_ln_b"], NQ),
        "f1_bn": np.stack([a[f"L1_ffn_bn_{n}"] for n in ("g", "b", "mean", "var")], 1),
        "f1_wr": a["L1_ffn_Wr"], "f1_br": rows(a["L1_ffn_br"]),
        "f1_wd": a["L1_ffn_W_down"].transpose(1, 2, 0).reshape(D, F1 * E1), "f1_bd": a["L1_ffn_b_down"].T,
        "f1_wu": a["L1_ffn_W_up"].transpose(1, 2, 0).reshape(F1, D * E1), "f1_bu": rows(a["L1_ffn_b_up"].T, NQ),
    }
    for L in range(2):
        parts[f"wq{L}"] = by_pairs(a[f"L{L}_xattn_Wq"])
        parts[f"wk{L}"] = a[f"L{L}_xattn_Wk"].T
        parts[f"wv{L}"] = a[f"L{L}_xattn_Wv"].T
        parts[f"wo{L}"] = out_pairs(a[f"L{L}_xattn_Wo"])
    packs = []
    for cols, width in pack_layout():
        pack = np.zeros((P, width), np.float32)
        for name, (c, n, r) in cols.items():
            assert parts[name].shape == (r, n), (name, parts[name].shape, (r, n))
            pack[:r, c:c + n] = parts[name]
        packs.append(pack)
    arrays = {
        "x_in": a["x"][0], "ctx_in": np.ascontiguousarray(a["ctx_1024"][0].T),
        "mask_in": np.ascontiguousarray(a["mask_SxS2_bk0"]),
        "pack1_in": packs[0], "pack2_in": packs[1], "bias_in": np.ascontiguousarray(np.broadcast_to(bias, (NQ, H, P))),
        "gup_in": np.ascontiguousarray(a["L0_ffn_gate_up_proj"].transpose(1, 0, 2)),
        "down_in": np.ascontiguousarray(a["L0_ffn_down_proj"].reshape(E0, 2, P, D).transpose(2, 1, 0, 3)),
        "ones_in": np.ones((3, 2 * NK), ml_dtypes.bfloat16),
    }
    nc = bacc.Bacc("TRN2", target_bir_lowering=False, num_devices=1)
    aps = [nc.dram_tensor(n, v.shape, mybir.dt.from_np(v.dtype), kind="ExternalInput").ap() for n, v in arrays.items()]
    skew = nc.dram_tensor("skew", (NQ * H * NQ,), F32, kind="Internal").ap()
    out = nc.dram_tensor("x_out", (1, NQ, D), F32, kind="ExternalOutput").ap()
    perceiver(nc, *aps, skew, out[0])
    r = run_bass_kernel_spmd(nc, [arrays], core_ids=[0])
    return r.results[0]["x_out"]
```

```python
from contextlib import ExitStack

import concourse.bass as bass
from concourse import mybir

F32 = mybir.dt.float32
BF16 = mybir.dt.bfloat16
U8 = mybir.dt.uint8
ALU = mybir.AluOpType
ACT = mybir.ActivationFunctionType
AX = mybir.AxisListType

P = 128
D = 128
H = 16
HD = D // H
NQ = 64
NK = 6272
NKT = NK // P
PAIRS = H // 2
STEPS = 7
TPS = NKT // STEPS
SW = TPS * P
CW = SW // 2
NCH = NK // CW
K_TERM = (0, 0, 0, 1, 1, 2)
Q_TERM = (0, 1, 2, 0, 1, 0)
TERMS = len(K_TERM)
ROWS = TERMS * 2 * HD
MROW = ROWS
VC = 2 * HD + 1
SCALE = HD ** -0.5
MASKED = -1e9
CHUNKS = ((2, 3, 3, 2, 3, 1, 0), (2, 2, 1, 2, 3, 3, 1))
PORTIONS = (((0, 3), (3, 5), (5, 7)), ((0, 3), (3, 7)))
E0, F0 = 16, 256
E1, F1 = 8, 64
NEG = -1e30
LN_EPS = 1e-5
STAGES = 7
VW = 4
V1_GROUPS = -(-NKT // VW)
UNITS = NCH + V1_GROUPS
AHEAD = (8, 10, 12, 20, 20, 21, 24, UNITS)
V_AFTER = (3, 7, 11)
PACK2_CUTS = 4


def pack_layout():
    first = [("ident", P, P), ("hmask", H, P), ("sel", 4, ROWS), ("sum4", VC, P),
             ("eps", 1, P), ("tie", E0, P), ("zero", 1, P), ("ident2", NQ, P),
             ("wk0", D, D), ("wq0", PAIRS * ROWS, D), ("wv0", D, D)]
    second = [("wo0", 2 * D, NQ), ("wk1", D, D), ("wq1", PAIRS * ROWS, D), ("wv1", D, D), ("wo1", 2 * D, NQ),
              ("bk1", 1, D), ("bq1", PAIRS, ROWS), ("bv1", PAIRS * HD, P), ("bo1", D, NQ),
              ("a0_wq", D, D), ("a0_wk", D, D), ("a0_wv", D, D), ("a0_bq", 1, D), ("a0_bk", 1, D),
              ("a0_bv", D, P), ("a0_se", NQ, D), ("a0_gw", D, D), ("a0_gb", 1, D), ("a0_gain", H // 2, P),
              ("a0_wo", D, D), ("a0_bo", D, NQ),
              ("f0_router", E0, D), ("f0_shared", 2 * F0, D), ("f0_wd", 2 * D, P),
              ("a1_wq", D, D), ("a1_wk", D, D), ("a1_wv", D, D), ("a1_wo", D, D),
              ("a1_s", 4, P), ("a1_bq", 1, D), ("a1_bk", 1, D), ("a1_bv", D, P), ("a1_bo", D, NQ),
              ("f1_lng", D, NQ), ("f1_lnb", D, NQ), ("f1_bn", 4, D), ("f1_wr", E1, D), ("f1_br", E1, P),
              ("f1_wd", F1 * E1, D), ("f1_bd", E1, F1), ("f1_wu", D * E1, F1), ("f1_bu", D * E1, NQ)]
    out = []
    for lot in (first, second):
        at, cols = 0, {}
        for name, n, rows in lot:
            cols[name] = (at, n, rows)
            at += n
        out.append((cols, at))
    return out


def skew_back(skew, g):
    return bass.AP(tensor=skew.tensor, offset=g * (H // 2) * NQ + NQ - 1, ap=[[H * NQ - 1, NQ], [NQ, H // 2], [1, NQ]])


def bias_rows(bias, g):
    return bass.AP(tensor=bias.tensor, offset=g * (H // 2) * P + NQ - 1, ap=[[H * P - 1, NQ], [P, H // 2], [1, NQ]])


def perceiver(nc, x_in, ctx_in, mask_in, pack1_in, pack2_in, bias_in, gup_in, down_in, ones_in, skew, x_out):
    (cols1, n1), (cols2, n2) = pack_layout()
    with ExitStack() as stack:
        def sb(name, shape, dt=F32):
            return stack.enter_context(nc.sbuf_tensor(name, shape, dt))

        def pb(name, shape):
            return stack.enter_context(nc.psum_tensor(name, shape, F32))

        def sem(name):
            return stack.enter_context(nc.semaphore(name))

        ctxT = sb("ctxT", [P, NK])
        kpart = sb("kpart", [P, 3, NK], BF16)
        kstack = sb("kstack", [P, 2, NK], BF16)
        vones = sb("vones", [P, NKT, PAIRS, VC])
        pack1 = sb("pack1", [P, n1])
        pack2 = sb("pack2", [P, n2])
        shared = sb("shared", [P, E0 * 2 * F0])
        gup = shared[:, :].rearrange("p (e f) -> p e f", e=E0)
        big3 = shared[:, 0:E0 * NQ]
        at = 0

        def part(n):
            nonlocal at
            at += n
            return shared[:, at - n:at]

        maskadd = part(NK // 2).bitcast(BF16)
        probs = part(2 * SW).rearrange("p (b n) -> p b n", b=2)
        vcur = part(2 * NKT * VC).rearrange("p (b t c) -> p b t c", b=2, t=NKT)
        junk = part(3 * CW).rearrange("p (b n) -> p b n", b=3)
        assert at <= E0 * 2 * F0
        mask_u8 = probs.rearrange("p b n -> p (b n)").bitcast(U8)[:, 0:NK]
        kres = sb("kres", [P, 2, CW])
        qstack = sb("qstack", [P, PAIRS, 2, NQ], BF16)
        qmax = sb("qmax", [P, 2, P], BF16)
        qexp = sb("qexp", [P, 2, P], BF16)
        identb = sb("identb", [P, P], BF16)
        qf = sb("qf", [P, PAIRS * NQ])
        qh = sb("qh", [P, PAIRS * NQ], BF16)
        qm = sb("qm", [P, PAIRS * NQ], BF16)
        mx = sb("mx", [P, 2, NCH])
        negm = sb("negm", [P, 4])
        m3 = sb("m3", [P, 4], BF16)
        acc_sb = sb("acc_sb", [P, P])
        o17 = sb("o17", [P, PAIRS, VC])
        den = sb("den", [P, PAIRS])
        rden = sb("rden", [P, PAIRS])
        onorm = sb("onorm", [P, PAIRS, HD])
        oT = sb("oT", [NQ, P])
        x = sb("x", [NQ, D])
        st = sb("st", [P, 6])
        mv = sb("mv", [P, 2])
        warm = sb("warm", [1, 16])
        rstd = sb("rstd", [P, 1])
        xn = sb("xn", [NQ, D])
        xz = sb("xz", [NQ, D])
        xnT = sb("xnT", [P, 2, NQ])
        big = sb("big", [P, H * NQ])
        big2 = sb("big2", [P, H * NQ])
        w512 = sb("w512", [P, 512])
        v512 = sb("v512", [P, 512])
        qr = w512
        rest = kstack[:, :, :].rearrange("p b n -> p (b n)").bitcast(F32)
        down = rest[:, 0:2 * E0 * D].rearrange("p (f e n) -> p f e n", f=2, e=E0)
        qT = sb("qT", [P, NQ])
        kT = sb("kT", [P, NQ])
        vbd = rest[:, 2 * E0 * D:2 * E0 * D + PAIRS * D].rearrange("p (a n) -> p a n", a=PAIRS)
        ogT = sb("ogT", [P, NQ])
        gt = sb("gt", [P, NQ])
        ngb = sb("ngb", [P, 1])
        bnr = sb("bnr", [P, 2])
        bias_t = sb("bias_t", [P, 512])
        red = sb("red", [P, H])
        red2 = sb("red2", [P, H])
        small = sb("small", [P, 16])
        onehot = sb("onehot", [P, E0])
        onehot2 = sb("onehot2", [P, E0])

        def w(name):
            cols, pack = (cols1, pack1) if name in cols1 else (cols2, pack2)
            c, n, rows = cols[name]
            return pack[0:rows, c:c + n]

        ident = w("ident")
        routing = big[:, :].rearrange("p (e t) -> p e t", e=E0)

        smax = [pb(f"smax{b}", [P, 512]) for b in range(2)]
        sexp = [pb(f"sexp{b}", [P, 1024]) for b in range(2)]
        acc = pb("acc", [P, 512])
        misc = pb("misc", [P, 512])
        smax3 = smax + [misc]
        MAXROWS, SUMS = slice(SW, SW + P), slice(SW, SW + VC)

        NAMES = """x_in pack1_in pack2_in mask_in gup_in down_in se_out se_in bias_in x_out
            mask_ready identb_ready ones_ready vones_ready ones_in act_chain dve_chain pool_chain
            ln_var ln_rstd ln_xn ln_xt xt_ready""".split()
        S = {n: sem(n) for n in NAMES}
        ctx_landed = [sem(f"ctx_landed{g}") for g in range(STEPS)]
        LNAMES = """qrep_done qstack_ready kproj_done khigh_done kproj_taken krest_ready kmid_done klow_done
            vproj_done vproj_taken qmax_ready qexp_ready vcur_ready
            smax_done smax_taken m3_ready mt_done qm_ready sexp_done exp_done pv_done
            acc_copied sum_done o17_taken on_ready ot_done ot_ready y_done passed pool_passed mx_chain""".split()
        only = (("khigh_done", "passed"), ("krest_ready",))
        LS = [{n: sem(f"{n}_{L}") for n in LNAMES if n not in only[1 - L]} for L in range(2)]
        stack_landed = [[sem(f"stack_landed_{b}_{h}") for h in range(len(PORTIONS[0]))] for b in range(2)]
        T = {n: sem(n) for n in """se_bd kbd_ready qkv_done qk_ready v_ready s_done se_done se_taken
            exp_ready exps p_ready pt_done pt_ready ot2_done gate_e og_ready y2_done
            r_done r_e route_ready xm_done xm_ready h_done h_e a_ready at_done at_ready yf_done
            b_qkv_done b_kbd_ready b_v_ready b_s_done b_exp_ready b_exps b_p_ready b_pt_done b_pt_ready
            b_ot_done b_og_ready b_y_done
            z_ready sh_done sh_e sh_ready sht_done bn_rs zb_ready g_done g_ready g_e wsel_ready
            zt_done zt_ready h1_done h1_ready y1_done out_ready""".split()}

        block = stack.enter_context(nc.Block())

        @block.sync
        def _(sp):
            def ones_rows():
                sp.dma_start(kstack[MROW:MROW + 3, :, :].rearrange("p b n -> p (b n)"), ones_in).then_inc(S["ones_in"], 16)

            sp.dma_start(x[:, :], x_in).then_inc(S["x_in"], 16)
            sp.dma_start(pack1[:, :], pack1_in).then_inc(S["pack1_in"], 16)
            for g in range(STEPS):
                sp.dma_start(ctxT[:, g * SW:(g + 1) * SW], ctx_in[:, g * SW:(g + 1) * SW]).then_inc(ctx_landed[g], 16)
                if g == 0:
                    sp.dma_start(mask_u8[0:NQ, :], mask_in).then_inc(S["mask_in"], 16)
                    sp.dma_start(mask_u8[NQ:P, :], mask_in).then_inc(S["mask_in"], 16)
            ones_rows()

            def refill(L, p):
                for h, (a, b) in enumerate(PORTIONS[L]):
                    if p >= 2:
                        sp.wait_ge(LS[L]["sexp_done"], STEPS * (p - 2) + b)
                    elif p == 0:
                        sp.wait_ge(LS[L]["klow_done"], 2 * b)
                    for t, k in enumerate(K_TERM):
                        sp.dma_start(kstack[t * 16:t * 16 + 16, p % 2, a * SW:b * SW],
                                     kpart[p * 16:p * 16 + 16, k, a * SW:b * SW]
                                     ).then_inc(stack_landed[p % 2][h], 16)

            for p in range(PAIRS):
                refill(0, p)
                if 1 <= p <= PACK2_CUTS:
                    cut = slice(n2 * (p - 1) // PACK2_CUTS, n2 * p // PACK2_CUTS)
                    sp.dma_start(pack2[:, cut], pack2_in[:, cut]).then_inc(S["pack2_in"], 16)
            for g in range(2):
                sp.dma_start(bias_t[g * NQ:(g + 1) * NQ, :].rearrange("p (h j) -> p h j", j=NQ),
                             bias_rows(bias_in, g)).then_inc(S["bias_in"], 16)
            sp.wait_ge(LS[0]["pv_done"], PAIRS * STEPS + 2)
            sp.wait_ge(LS[0]["smax_taken"], PAIRS * NCH)
            sp.dma_start(gup, gup_in).then_inc(S["gup_in"], 16)
            sp.dma_start(down, down_in).then_inc(S["down_in"], 16)
            sp.wait_ge(T["se_taken"], 1)
            sp.dma_start(skew.rearrange("(q n) -> q n", q=NQ), big2[0:NQ, :]).then_inc(S["se_out"], 16)
            sp.wait_ge(S["se_out"], 16)
            for g in range(2):
                sp.dma_start(qf[g * NQ:(g + 1) * NQ, :].rearrange("p (h j) -> p h j", j=NQ),
                             skew_back(skew, g)).then_inc(S["se_in"], 16)
            sp.wait_ge(T["yf_done"], 1)
            ones_rows()
            for p in range(PAIRS):
                refill(1, p)
            sp.wait_ge(T["out_ready"], 1)
            sp.dma_start(x_out, x[:, :]).then_inc(S["x_out"], 16)
            sp.wait_ge(S["x_out"], 16)

        @block.tensor
        def _(pe):
            def ln_transpose(n):
                pe.wait_ge(S["ln_xn"], n + 1)
                pe.transpose(misc[:, 0:NQ], xn[:, :], ident[0:NQ, 0:NQ]).then_inc(S["ln_xt"], 1)
                pe.wait_ge(S["xt_ready"], n + 1)

            def project_q(L):
                q = LS[L]
                for p in range(PAIRS):
                    last = pe.matmul(acc[0:ROWS, p * NQ:(p + 1) * NQ], w(f"wq{L}")[:, p * ROWS:(p + 1) * ROWS],
                                     xnT[:, 0, :], start=True, stop=True)
                last.then_inc(q["qrep_done"], 1)

            def k_chunk(L, c):
                q = LS[L]
                if c % 2 == 0:
                    pe.wait_ge(ctx_landed[c // 2], 16)
                if c >= 2:
                    pe.wait_ge(q["kproj_taken"], c - 1)
                pe.matmul(smax[c % 2][:, 0:CW], w(f"wk{L}"), ctxT[:, c * CW:(c + 1) * CW],
                          start=True, stop=True).then_inc(q["kproj_done"], 1)

            def v_tile(L, kt):
                q = LS[L]
                g, t = kt // TPS, kt % TPS
                if t == 0 and g >= 2:
                    pe.wait_ge(q["vproj_taken"], g - 1)
                ins = pe.matmul(sexp[g % 2][:, t * P:(t + 1) * P], ctxT[:, kt * P:(kt + 1) * P],
                                w(f"wv{L}"), start=True, stop=True)
                if t == TPS - 1:
                    ins.then_inc(q["vproj_done"], 1)

            def project_kv(L=0):
                for c in range(NCH):
                    k_chunk(L, c)
                    if c in V_AFTER:
                        for t in range(TPS):
                            v_tile(L, V_AFTER.index(c) * TPS + t)

            def ahead(first, last):
                q = LS[1]
                for u in range(first, last):
                    i = u // 2
                    if u % 2 == 0:
                        if i:
                            pe.wait_ge(q["kproj_taken"], i)
                        pe.matmul(smax[0][:, 0:CW], w("wk1"), ctxT[:, i * CW:(i + 1) * CW],
                                  start=True, stop=True).then_inc(q["kproj_done"], 1)
                    else:
                        if i:
                            pe.wait_ge(q["vproj_taken"], i)
                        for t in range(i * VW, min(NKT, (i + 1) * VW)):
                            lastmm = pe.matmul(smax[1][:, (t % VW) * P:(t % VW + 1) * P], ctxT[:, t * P:(t + 1) * P],
                                               w("wv1"), start=True, stop=True)
                        lastmm.then_inc(q["vproj_done"], 1)

            def cross(L):
                q = LS[L]

                def max_chunks(pair, b, chunks):
                    for n in chunks:
                        if n == 0:
                            pe.wait_ge(q["qmax_ready"], pair + 1)
                        for h, (a, _) in enumerate(PORTIONS[L]):
                            if n == 2 * a:
                                pe.wait_ge(stack_landed[b][h], (L * PAIRS + pair - b) * (8 * TERMS) + 16 * TERMS)
                        if isinstance(pair, int) and pair == 0 and n == 2:
                            pass
                        elif isinstance(pair, int) and pair == 0 and n < 2:
                            if L == 0:
                                pe.wait_ge(q["kproj_taken"], NCH - 1 + n)
                            elif n == 0:
                                pe.wait_ge(q["kproj_taken"], NCH)
                            else:
                                pe.wait_ge(q["vproj_taken"], V1_GROUPS)
                        else:
                            pe.wait_ge(q["smax_taken"], pair * NCH + (n - 2 if n > 2 else (-1, 0, -2)[n]))
                        pe.matmul(smax3[n % 3][:, 0:CW], qmax[0:ROWS, b, :], kstack[0:ROWS, b, n * CW:(n + 1) * CW],
                                  start=True, stop=True).then_inc(q["smax_done"], 1)

                def max_to_rows(pair, b):
                    pe.wait_ge(q["m3_ready"], pair + 1)
                    pe.wait_ge(q["exp_done"], pair * STEPS + 1)
                    pe.matmul(sexp[b][MROW:MROW + 3, MAXROWS], m3[:, 0:3], identb[:, :], start=True, stop=True,
                              tile_position=(0, MROW)).then_inc(q["mt_done"], 1)

                def scores(s, pair, b, j, buf, sums=False):
                    if j == 0:
                        pe.wait_ge(q["qm_ready"], pair + 1)
                    pe.wait_ge(q["exp_done"], s + 1)
                    for t in range(TPS):
                        ks = slice((j * TPS + t) * P, (j * TPS + t + 1) * P)
                        o = sexp[buf][:, t * P:(t + 1) * P]
                        if L == 0:
                            pe.matmul(o, maskadd[:, ks], identb[:, :], start=True, stop=False)
                        last = pe.matmul(o, kstack[0:MROW + 3, b, ks], qexp[0:MROW + 3, b, :],
                                         start=L != 0, stop=True)
                    if sums:
                        last = sum_groups(pair - 1, buf)
                    last.then_inc(q["sexp_done"], 1)

                def times_v(s, pair, b, j, buf):
                    if j == 0:
                        pe.wait_ge(q["vcur_ready"], pair + 1)
                        if not (isinstance(pair, int) and pair == 0):
                            pe.wait_ge(q["acc_copied"], pair)
                    pe.wait_ge(q["exp_done"], s + 3)
                    for t in range(TPS):
                        g = t % 4
                        last = pe.matmul(acc[32 * g:32 * g + VC, 0:P], vcur[:, b, j * TPS + t, :],
                                         probs[:, buf, t * P:(t + 1) * P],
                                         start=(j == 0 and t < 4), stop=(j == STEPS - 1 and t >= TPS - 4),
                                         tile_position=(0, 32 * g))
                    last.then_inc(q["pv_done"], 1)

                def sum_groups(pair, buf):
                    pe.wait_ge(q["acc_copied"], pair + 1)
                    return pe.matmul(sexp[buf][:, SUMS], acc_sb[:, :], w("sum4"), start=True, stop=True)

                def step(i, k, ahead=True):
                    s = i * (2 * STEPS) + k
                    j, pair, b = k % STEPS, i * 2 + k // STEPS, (k // STEPS) % 2
                    if ahead:
                        c = sum(CHUNKS[L][:j])
                        max_chunks(pair + 1, 1 - b, range(c, c + CHUNKS[L][j]))
                    k1 = k - 1
                    if j:
                        scores(s, pair, b, j, k % 2, sums=j == 2 and k > STEPS)
                    else:
                        max_to_rows(pair, b)
                    times_v(s - 1, i * 2 + k1 // STEPS, (k1 // STEPS) % 2, k1 % STEPS, k1 % 2)
                    if j == 0:
                        scores(s, pair, b, j, k % 2)

                pe.sem_inc(q["pv_done"], 2)
                pe.sem_inc(q["mt_done"], 1)
                for n in range(NCH):
                    max_chunks(0, 0, range(n, n + 1))
                    rest_v = NKT - len(V_AFTER) * TPS if L == 0 else 0
                    for t in range(rest_v * n // NCH, rest_v * (n + 1) // NCH):
                        v_tile(L, len(V_AFTER) * TPS + t)
                if L == 0:
                    pe.wait_ge(q["vproj_taken"], STEPS)
                max_to_rows(0, 0)
                max_chunks(1, 1, range(CHUNKS[L][0]))
                scores(0, 0, 0, 0, 0)
                step(0, 1)
                step(0, 2)
                with pe.Fori(0, PAIRS // 2 - 1) as i:
                    for k in range(3, 2 * STEPS + 3):
                        step(i, k)
                for k in range(3, 2 * STEPS):
                    step(PAIRS // 2 - 1, k, ahead=k < STEPS)
                    if L == 0 and k > STEPS:
                        pe.wait_ge(q["smax_taken"], PAIRS * NCH)
                        ahead(k - STEPS - 1, k - STEPS)
                times_v(PAIRS * STEPS - 1, PAIRS - 1, 1, STEPS - 1, 1)
                sum_groups(PAIRS - 1, 0).then_inc(q["sum_done"], 1)

            def cross_out(L):
                q = LS[L]
                pe.wait_ge(q["on_ready"], 2)
                pe.transpose(misc[0:NQ, 0:P], onorm[:, :, :].rearrange("p a d -> p (a d)"), ident).then_inc(q["ot_done"], 1)
                pe.wait_ge(q["ot_ready"], 1)
                for e in range(2):
                    last = pe.matmul(acc[0:NQ, D:2 * D], oT[:, e * NQ:(e + 1) * NQ], w(f"wo{L}")[:, e * D:(e + 1) * D],
                                     start=e == 0, stop=e == 1)
                last.then_inc(q["y_done"], 1)

            pe.wait_ge(S["pack1_in"], 16)
            ln_transpose(0)
            pe.wait_ge(S["ones_ready"], 1)
            project_q(0)
            project_kv()
            pe.wait_ge(S["mask_ready"], NCH)
            pe.wait_ge(S["identb_ready"], 1)
            pe.wait_ge(S["ones_in"], 16)
            cross(0)
            pe.wait_ge(S["pack2_in"], 16 * PACK2_CUTS)
            ahead(STEPS - 1, AHEAD[0])
            cross_out(0)
            ahead(AHEAD[0], AHEAD[1])

            ln_transpose(1)
            pe.matmul(misc[:, 64:128], w("a0_wq"), xnT[:, 0, :], start=True, stop=True)
            pe.matmul(misc[:, 128:192], w("a0_wk"), xnT[:, 0, :], start=True, stop=True)
            pe.matmul(misc[:, 192:256], w("a0_gw"), xnT[:, 0, :], start=True, stop=True)
            pe.matmul(misc[:, 256:384], xnT[:, :, :].rearrange("p a n -> p (a n)"), w("a0_wv"),
                      start=True, stop=True).then_inc(T["qkv_done"], 1)
            ahead(AHEAD[1], AHEAD[2])
            pe.wait_ge(T["qk_ready"], 1)
            for hf in range(2):
                last = pe.matmul(sexp[1][0:NQ, hf * 512:(hf + 1) * 512], qT[:, :], big2[:, hf * 512:(hf + 1) * 512],
                                 start=True, stop=True)
            last.then_inc(T["se_done"], 1)
            pe.wait_ge(T["kbd_ready"], 1)
            for g in range(2):
                last = pe.matmul(sexp[0][g * NQ:(g + 1) * NQ, 0:512], qT[:, :], big[:, g * 512:(g + 1) * 512],
                                 start=True, stop=True, tile_position=(0, g * NQ))
            last.then_inc(T["s_done"], 1)
            ahead(AHEAD[2], AHEAD[3])
            pe.wait_ge(T["p_ready"], 1)
            for b in range(4):
                last = pe.transpose(sexp[0][:, 512 + b * P:512 + (b + 1) * P], w512[:, b * P:(b + 1) * P], ident)
            last.then_inc(T["pt_done"], 1)
            ahead(AHEAD[3], AHEAD[4])
            pe.wait_ge(T["pt_ready"], 1)
            pe.wait_ge(T["v_ready"], 2)
            for n in range(PAIRS):
                last = pe.matmul(misc[:, 384:448], vbd[:, n, :], v512[:, (n % 4) * P + (n // 4) * NQ:(n % 4) * P + (n // 4) * NQ + NQ],
                                 start=n == 0, stop=n == PAIRS - 1)
            last.then_inc(T["ot2_done"], 1)
            pe.wait_ge(T["og_ready"], 1)
            pe.matmul(acc[0:NQ, D:2 * D], ogT[:, :], w("a0_wo"), start=True, stop=True).then_inc(T["y2_done"], 1)
            ahead(AHEAD[4], AHEAD[5])

            ln_transpose(2)
            pe.matmul(misc[:, 64:64 + E0], xnT[:, :, :].rearrange("p a n -> p (a n)"), w("f0_router"), start=True, stop=True).then_inc(T["r_done"], 1)
            ahead(AHEAD[5], AHEAD[6])
            pe.wait_ge(T["route_ready"], 2)
            for hf in range(2):
                last = pe.matmul(sexp[0][:, hf * 512:(hf + 1) * 512], xz[:, :], big[0:NQ, hf * 512:(hf + 1) * 512],
                                 start=True, stop=True)
            last.then_inc(T["xm_done"], 1)
            pe.matmul(sexp[1][0:NQ, 2 * F0:4 * F0], xnT[:, 0, :], w("f0_shared"), start=True, stop=True
                      ).then_inc(T["sh_done"], 1)
            pe.wait_ge(T["xm_ready"], 1)
            pe.wait_ge(S["gup_in"], 16)
            for e in range(E0):
                odd = e % 2 * NQ
                last = pe.matmul(sexp[1][odd:odd + NQ, 0:2 * F0], big2[:, e * NQ:(e + 1) * NQ], gup[:, e, :],
                                 start=e < 2, stop=e >= E0 - 2, tile_position=(0, odd))
            last.then_inc(T["h_done"], 1)
            pe.wait_ge(T["sh_ready"], 1)
            for f in range(2):
                last = pe.transpose(misc[:, f * NQ:(f + 1) * NQ], w512[0:NQ, F0 + f * P:F0 + (f + 1) * P], ident[0:NQ, 0:NQ])
            last.then_inc(T["sht_done"], 1)
            ahead(AHEAD[6], AHEAD[7])
            pe.wait_ge(T["a_ready"], 1)
            for f in range(2):
                for hf in range(2):
                    last = pe.matmul(sexp[f][:, hf * 512:(hf + 1) * 512], w512[:, f * P:(f + 1) * P],
                                     big[:, hf * 512:(hf + 1) * 512], start=True, stop=True)
                last.then_inc(T["at_done"], 1)
            pe.wait_ge(S["down_in"], 16)
            pe.wait_ge(T["at_ready"], 3)
            for e in range(E0):
                for f in range(2):
                    pe.matmul(acc[f * NQ:(f + 1) * NQ, D:2 * D], (big2, big3)[f][:, e * NQ:(e + 1) * NQ], down[:, f, e, :],
                              start=e == 0, stop=False, tile_position=(0, f * NQ))
            for f in range(2):
                last = pe.matmul(acc[f * NQ:(f + 1) * NQ, D:2 * D], xnT[:, f, :], w("f0_wd")[:, f * D:(f + 1) * D],
                                 start=False, stop=True, tile_position=(0, f * NQ))
            last.then_inc(T["yf_done"], 1)

            ln_transpose(3)
            project_q(1)
            pe.wait_ge(S["ones_in"], 32)
            cross(1)
            pe.wait_ge(LS[1]["smax_taken"], PAIRS * NCH)
            cross_out(1)

            ln_transpose(4)
            pe.matmul(misc[:, 64:128], w("a1_wq"), xnT[:, 0, :], start=True, stop=True)
            pe.matmul(misc[:, 128:192], w("a1_wk"), xnT[:, 0, :], start=True, stop=True)
            pe.matmul(misc[:, 256:384], xnT[:, :, :].rearrange("p a n -> p (a n)"), w("a1_wv"),
                      start=True, stop=True).then_inc(T["b_qkv_done"], 1)
            pe.wait_ge(T["b_kbd_ready"], 1)
            for g in range(2):
                last = pe.matmul(sexp[0][g * NQ:(g + 1) * NQ, 0:512], qT[:, :], big[:, g * 512:(g + 1) * 512],
                                 start=True, stop=True, tile_position=(0, g * NQ))
            last.then_inc(T["b_s_done"], 1)
            pe.wait_ge(T["b_p_ready"], 1)
            for b in range(4):
                last = pe.transpose(sexp[0][:, 512 + b * P:512 + (b + 1) * P], w512[:, b * P:(b + 1) * P], ident)
            last.then_inc(T["b_pt_done"], 1)
            pe.wait_ge(T["b_pt_ready"], 1)
            pe.wait_ge(T["b_v_ready"], 2)
            for n in range(PAIRS):
                last = pe.matmul(misc[:, 384:448], vbd[:, n, :], v512[:, (n % 4) * P + (n // 4) * NQ:(n % 4) * P + (n // 4) * NQ + NQ],
                                 start=n == 0, stop=n == PAIRS - 1)
            last.then_inc(T["b_ot_done"], 1)
            pe.wait_ge(T["b_og_ready"], 1)
            pe.matmul(acc[0:NQ, D:2 * D], ogT[:, :], w("a1_wo"), start=True, stop=True).then_inc(T["b_y_done"], 1)

            pe.wait_ge(T["z_ready"], 1)
            pe.matmul(misc[:, 64:65], xz[:, :], small[0:NQ, 0:1], start=True, stop=True)
            pe.transpose(misc[:, 128:192], xz[:, :], ident[0:NQ, 0:NQ]).then_inc(T["zt_done"], 1)
            pe.wait_ge(T["zb_ready"], 1)
            pe.matmul(sexp[0][:, 0:E1], w512[:, 0:P], w("f1_wr"),
                      start=True, stop=True).then_inc(T["g_done"], 1)
            pe.wait_ge(T["wsel_ready"], 1)
            pe.wait_ge(T["zt_ready"], 1)
            pe.matmul(acc[0:F1, 0:NQ], v512[:, 0:F1], qT[:, :], start=True, stop=True).then_inc(T["h1_done"], 1)
            pe.wait_ge(T["h1_ready"], 1)
            pe.matmul(sexp[1][0:NQ, 0:D], kT[0:F1, :], v512[0:F1, 128:256], start=True, stop=True).then_inc(T["y1_done"], 1)

        @block.scalar
        def _(act):
            chain = [0]

            def link(ins):
                chain[0] += 1
                ins.then_inc(S["act_chain"], 1)
                act.wait_ge(S["act_chain"], chain[0])

            def load_table(func, n):
                act.activation(warm[0:1, n:n + 1], w("eps")[0:1, :], func)

            def std(n):
                act.wait_ge(S["ln_var"], n + 1)
                act.activation(rstd[0:NQ, :], mv[0:NQ, 1:2], ACT.Sqrt, bias=w("eps")[0:NQ, :]).then_inc(S["ln_rstd"], 1)
                load_table(ACT.Exp, 2 * n + 1)

            def take_ahead(first, last):
                q = LS[1]
                for u in range(first, last):
                    i = u // 2
                    if u % 2 == 0:
                        act.wait_ge(q["kproj_done"], i + 1)
                        act.activation(kpart[:, 0, i * CW:(i + 1) * CW], smax[0][:, 0:CW], ACT.Identity, bias=w("bk1"))
                        if i >= 2:
                            act.wait_ge(q["klow_done"], i - 1)
                        act.activation(kres[:, i % 2, :], smax[0][:, 0:CW], ACT.Identity, bias=w("bk1")
                                       ).then_inc(q["kproj_taken"], 1)
                        if i:
                            take_mid(i - 1)
                    else:
                        n = min(NKT, (i + 1) * VW) - i * VW
                        act.wait_ge(q["vproj_done"], i + 1)
                        act.activation(vones[:, i * VW:i * VW + n, :, 0:2 * HD],
                                       smax[1][:, 0:n * P].rearrange("p (t a c) -> p t a c", t=n, a=PAIRS),
                                       ACT.Copy).then_inc(q["vproj_taken"], 1)

            def take_mid(i):
                act.wait_ge(LS[1]["krest_ready"], i + 1)
                act.activation(kpart[:, 1, i * CW:(i + 1) * CW], kres[:, i % 2, :], ACT.Copy
                               ).then_inc(LS[1]["kmid_done"], 1)

            def take_kv(L=0):
                q = LS[L]
                bias = w("zero")
                for c in range(NCH + 1):
                    if c < NCH:
                        act.wait_ge(q["kproj_done"], c + 1)
                        act.activation(kpart[:, 0, c * CW:(c + 1) * CW], smax[c % 2][:, 0:CW], ACT.Identity, bias=bias
                                       ).then_inc(q["khigh_done"], 1)
                    if c - 2 in V_AFTER:
                        take_v(L, V_AFTER.index(c - 2))
                    if c:
                        act.wait_ge(q["kproj_taken"], c)
                        act.activation(kpart[:, 1, (c - 1) * CW:c * CW], kres[:, (c - 1) % 2, :], ACT.Copy
                                       ).then_inc(q["kmid_done"], 1)

            def take_v(L, g):
                q = LS[L]
                act.wait_ge(q["vproj_done"], g + 1)
                act.activation(vones[:, g * TPS:(g + 1) * TPS, :, 0:2 * HD],
                               sexp[g % 2][:, 0:SW].rearrange("p (t a c) -> p t a c", t=TPS, a=PAIRS),
                               ACT.Copy).then_inc(q["vproj_taken"], 1)

            def cross(L):
                q = LS[L]

                def exps(s, buf):
                    act.wait_ge(q["sexp_done"], s + 1)
                    act.wait_ge(q["pv_done"], s + 1)
                    act.activation(probs[:, buf, :], sexp[buf][:, 0:SW], ACT.Exp).then_inc(q["exp_done"], 1)

                def take_acc(pair):
                    act.wait_ge(q["pv_done"], pair * STEPS + STEPS + 2)
                    act.activation(acc_sb[:, :], acc[:, 0:P], ACT.Copy).then_inc(q["acc_copied"], 1)

                def take_sum(pair, buf):
                    o = o17[:, pair, :] if isinstance(pair, int) else \
                        o17[:, :, :].rearrange("p a c -> p (a c)")[:, bass.ds(pair * VC, VC)]
                    act.activation(o, sexp[buf][:, SUMS], ACT.Copy).then_inc(q["o17_taken"], 1)

                def take_rows(pair, b):
                    act.wait_ge(q["qexp_ready"], pair + 1)
                    act.wait_ge(q["mt_done"], pair + 2)
                    act.activation(qexp[MROW:MROW + 3, b, :], sexp[b][MROW:MROW + 3, MAXROWS], ACT.Copy
                                   ).then_inc(q["qm_ready"], 1)

                def step(i, k, ahead=True):
                    if k >= STEPS and k % STEPS == 2:
                        act.wait_ge(q["sexp_done"], i * (2 * STEPS) + k + 1)
                        take_sum(i * 2 + k // STEPS - 1, k % 2)
                    exps(i * (2 * STEPS) + k, k % 2)
                    if ahead and k % STEPS == STEPS - 1:
                        take_rows(i * 2 + k // STEPS + 1, (k // STEPS + 1) % 2)
                    if k >= STEPS and k % STEPS == 0:
                        take_acc(i * 2 + k // STEPS - 1)

                if L == 0:
                    for g in range(len(V_AFTER), STEPS):
                        take_v(L, g)
                act.sem_inc(q["exp_done"], 2)
                take_rows(0, 0)
                for k in range(3):
                    step(0, k)
                with act.Fori(0, PAIRS // 2 - 1) as i:
                    for k in range(3, 2 * STEPS + 3):
                        step(i, k)
                for k in range(3, 2 * STEPS):
                    step(PAIRS // 2 - 1, k, ahead=k < STEPS)
                    if L == 0 and k > STEPS:
                        act.wait_ge(q["vcur_ready"], PAIRS)
                        take_ahead(k - STEPS - 1, k - STEPS)
                take_acc(PAIRS - 1)
                act.wait_ge(q["sum_done"], 1)
                take_sum(PAIRS - 1, 0)

            act.wait_ge(S["pack1_in"], 16)
            load_table(ACT.Sqrt, 0)
            std(0)
            take_kv()
            cross(0)
            act.wait_ge(S["pack2_in"], 16 * PACK2_CUTS)
            take_ahead(STEPS - 1, AHEAD[0])
            act.activation(bnr[:, 0:1], w("f1_bn")[:, 3:4], ACT.Sqrt, bias=w("eps")).then_inc(T["bn_rs"], 1)
            std(1)
            take_ahead(AHEAD[0], AHEAD[2])
            act.wait_ge(T["se_done"], 1)
            act.activation(big2[0:NQ, :], sexp[1][0:NQ, :], ACT.Copy, scale=SCALE, bias=SCALE).then_inc(T["se_taken"], 1)
            act.wait_ge(T["qk_ready"], 1)
            act.activation(gt[:, :], misc[:, 192:256], ACT.Exp, scale=-1.0, bias=ngb[:, 0:1]).then_inc(T["gate_e"], 1)
            take_ahead(AHEAD[2], AHEAD[3])
            act.wait_ge(T["exp_ready"], 1)
            act.activation(w512[:, :], w512[:, :], ACT.Exp).then_inc(T["exps"], 1)
            load_table(ACT.Sqrt, 4)
            take_ahead(AHEAD[3], AHEAD[4])
            std(2)
            take_ahead(AHEAD[4], AHEAD[5])
            act.wait_ge(T["r_e"], 1)
            act.activation(small[:, 2:3], small[:, 1:2], ACT.Exp, scale=-1.0).then_inc(T["r_e"], 1)
            take_ahead(AHEAD[5], AHEAD[6])
            act.wait_ge(T["sh_done"], 1)
            act.activation(v512[0:NQ, F0:2 * F0], sexp[1][0:NQ, 2 * F0:3 * F0], ACT.Exp, scale=-1.0).then_inc(T["sh_e"], 1)
            act.wait_ge(T["h_done"], 1)
            act.activation(v512[:, 0:F0], sexp[1][:, 0:F0], ACT.Exp, scale=-1.0).then_inc(T["h_e"], 1)
            load_table(ACT.Sqrt, 6)
            act.wait_ge(T["sht_done"], 1)
            act.activation(xnT[:, :, :], misc[:, 0:2 * NQ].rearrange("p (a n) -> p a n", a=2), ACT.Copy
                           ).then_inc(T["at_ready"], 1)
            take_ahead(AHEAD[6], AHEAD[7])
            take_mid(NCH - 1)
            act.wait_ge(T["at_done"], 2)
            act.activation(big3[:, :], sexp[1][:, :], ACT.Copy).then_inc(T["at_ready"], 1)
            std(3)
            cross(1)
            load_table(ACT.Sqrt, 8)
            std(4)
            act.wait_ge(T["b_exp_ready"], 1)
            act.activation(w512[:, :], w512[:, :], ACT.Exp).then_inc(T["b_exps"], 1)
            load_table(ACT.Sqrt, 10)
            std(5)
            load_table(ACT.Sqrt, 12)
            std(6)
            act.wait_ge(T["g_ready"], 1)
            act.activation(red2[:, 0:E1], red[:, 0:E1], ACT.Exp, accum_out=small[:, 4:5]).then_inc(T["g_e"], 1)

        @block.vector
        def _(dve):
            chain = [0]

            def link(ins):
                chain[0] += 1
                ins.then_inc(S["dve_chain"], 1)
                dve.wait_ge(S["dve_chain"], chain[0])

            def layernorm(n, src=None):
                src = x[:, :] if src is None else src
                link(dve.bn_stats(st[0:NQ, :], src))
                dve.bn_aggr(mv[0:NQ, :], st[0:NQ, :]).then_inc(S["ln_var"], 1)
                dve.wait_ge(S["ln_rstd"], n + 1)
                link(dve.reciprocal(rstd[0:NQ, :], rstd[0:NQ, :]))
                return dve.tensor_scalar(xn[:, :], src, mv[0:NQ, 0:1], rstd[0:NQ, 0:1], ALU.subtract, ALU.mult)

            def take_xt(n):
                dve.wait_ge(S["ln_xt"], n + 1)
                dve.tensor_copy(xnT[:, :, :], misc[:, 0:NQ].unsqueeze(1).to_broadcast([P, 2, NQ])).then_inc(S["xt_ready"], 1)

            def stack_q(L, stage):
                q = LS[L]
                R = slice(0, ROWS)
                sel = w("sel")
                by_pair = lambda t: t.rearrange("p (a n) -> p a n", a=PAIRS)
                src = acc[R, 0:PAIRS * NQ]
                if stage == 0:
                    dve.wait_ge(q["qrep_done"], 1)
                    if L:
                        link(dve.tensor_tensor(by_pair(qf[R, :]), by_pair(src),
                                               w("bq1").unsqueeze(2).to_broadcast([ROWS, PAIRS, NQ]), ALU.add))
                        src = qf[R, :]
                    link(dve.tensor_scalar(qf[R, :], src, SCALE, None, ALU.mult))
                elif stage == 1:
                    link(dve.tensor_copy(qh[R, :], qf[R, :]))
                elif stage == 2:
                    link(dve.scalar_tensor_tensor(qr[R, :], qh[R, :], sel[:, 0:1], qf[R, :], ALU.mult, ALU.add))
                elif stage == 3:
                    link(dve.tensor_copy(qm[R, :], qr[R, :]))
                elif stage == 4:
                    link(dve.scalar_tensor_tensor(qr[R, :], qm[R, :], sel[:, 1:2], qr[R, :], ALU.mult, ALU.add))
                elif stage < STAGES:
                    e = stage - 5
                    dve.tensor_scalar(qstack[R, :, e, :], by_pair(qr[R, :]), sel[:, 2 + e:3 + e], None, ALU.mult
                                      ).then_inc(q["qstack_ready"], 1)

            def split_k(L=0):
                q = LS[L]
                bias = w("zero")
                for c in range(NCH):
                    cs = slice(c * CW, (c + 1) * CW)
                    dve.wait_ge(q["khigh_done"], c + 1)
                    if c >= 2:
                        dve.wait_ge(q["klow_done"], c - 1)
                    dve.scalar_tensor_tensor(kres[:, c % 2, :], smax[c % 2][:, 0:CW], bias, kpart[:, 0, cs],
                                             ALU.add, ALU.subtract).then_inc(q["kproj_taken"], 1)
                    stack_q(L, c)

            def cross(L):
                q = LS[L]

                def one(pair, b):
                    for n in range(NCH):
                        dve.wait_ge(q["smax_done"], pair * NCH + n + 1)
                        if L == 0:
                            dve.sem_inc(q["passed"], 1)
                        if L == 0:
                            dve.tensor_tensor_reduce(junk[:, n % 3, :], smax3[n % 3][:, 0:CW], maskadd[:, n * CW:(n + 1) * CW],
                                                     1.0, -3e38, ALU.add, ALU.max, mx[:, b, n:n + 1]
                                                     ).then_inc(q["smax_taken"], 1)
                        else:
                            dve.tensor_reduce(mx[:, b, n:n + 1], smax3[n % 3][:, 0:CW], AX.X, ALU.max
                                              ).then_inc(q["smax_taken"], 1)
                    dve.wait_ge(q["smax_taken"], pair * NCH + NCH)
                    links = [0]

                    def next_reads(ins):
                        links[0] += 1
                        ins.then_inc(q["mx_chain"], 1)
                        dve.wait_ge(q["mx_chain"], pair * 3 + links[0])

                    next_reads(dve.tensor_reduce(negm[:, 0:1], mx[:, b, :], AX.X, ALU.max, negate=True))
                    most = -MASKED / 2 if L == 0 else 3e38
                    dve.wait_ge(q["mt_done"], pair + 1)
                    next_reads(dve.tensor_scalar(m3[:, 0:1], negm[:, 0:1], most, None, ALU.min))
                    dve.scalar_tensor_tensor(negm[:, 1:2], negm[:, 0:1], most, m3[:, 0:1], ALU.min, ALU.subtract)
                    next_reads(dve.scalar_tensor_tensor(m3[:, 1:2], negm[:, 0:1], most, m3[:, 0:1], ALU.min, ALU.subtract))
                    dve.tensor_tensor(m3[:, 2:3], negm[:, 1:2], m3[:, 1:2], ALU.subtract).then_inc(q["m3_ready"], 1)

                with dve.Fori(0, PAIRS // 2) as i:
                    one(i * 2, 0)
                    one(i * 2 + 1, 1)

            def cross_out(L):
                q = LS[L]
                dve.wait_ge(q["o17_taken"], PAIRS)
                if L == 0:
                    link(dve.tensor_scalar(den[:, :], o17[:, :, VC - 1], 1e-9, None, ALU.max))
                link(dve.reciprocal(rden[:, :], den[:, :] if L == 0 else o17[:, :, VC - 1]))
                for e in range(2):
                    r = slice(e * NQ, (e + 1) * NQ)
                    ins = dve.tensor_tensor(onorm[r, :, :], o17[r, :, e * HD:(e + 1) * HD],
                                            rden[r, :].unsqueeze(2).to_broadcast([NQ, PAIRS, HD]), ALU.mult)
                    if L == 0:
                        ins.then_inc(q["on_ready"], 1)
                    else:
                        link(ins)
                if L:
                    dve.tensor_tensor(onorm[:, :, :], onorm[:, :, :], w("bv1").rearrange("p (a d) -> p a d", a=PAIRS),
                                      ALU.add).then_inc(q["on_ready"], 2)
                dve.wait_ge(q["ot_done"], 1)
                dve.tensor_copy(oT[:, :], misc[0:NQ, 0:P]).then_inc(q["ot_ready"], 1)
                dve.wait_ge(q["y_done"], 1)
                link(dve.tensor_tensor(x[:, :], acc[0:NQ, D:2 * D], x[:, :], ALU.add))
                if L:
                    link(dve.tensor_tensor(x[:, :], x[:, :], w("bo1"), ALU.add))

            dve.memset(acc[:, :], 0.0).then_inc(S["ones_ready"], 1)

            dve.wait_ge(S["x_in"], 16)
            layernorm(0).then_inc(S["ln_xn"], 1)
            take_xt(0)
            dve.tensor_copy(identb[:, :], ident).then_inc(S["identb_ready"], 1)
            split_k()
            dve.wait_ge(S["mask_ready"], NCH)
            cross(0)
            dve.wait_ge(S["pack2_in"], 16 * PACK2_CUTS)
            cross_out(0)

            hm = w("hmask").unsqueeze(2).to_broadcast([P, H, NQ])

            def by_head(out, src):
                return dve.tensor_tensor(out[:, :].rearrange("p (h j) -> p h j", h=H),
                                         src.unsqueeze(1).to_broadcast([P, H, NQ]), hm, ALU.mult)

            def block_v(src_ready_inc):
                flat = vbd.rearrange("p a c -> p (a c)")
                for e in range(2):
                    r = slice(e * NQ, (e + 1) * NQ)
                    o = bass.AP(tensor=flat.tensor, offset=flat[r, :].offset + e * HD,
                                ap=[flat[r, :].ap[0], [D + 2 * HD, PAIRS], [1, HD]])
                    s = v512[r, 0:D].rearrange("p (a e d) -> p a e d", a=PAIRS, e=2)[:, :, e, :]
                    dve.tensor_copy(o, s).then_inc(src_ready_inc, 1)

            def softmax_heads(exp_ready, exps):
                w3 = w512[:, :].rearrange("p (h j) -> p h j", h=H // 2)
                link(dve.tensor_reduce(red[:, 0:H // 2], w3, AX.X, ALU.max))
                dve.tensor_tensor(w3, w3, red[:, 0:H // 2].unsqueeze(2).to_broadcast([P, H // 2, NQ]), ALU.subtract
                                  ).then_inc(exp_ready, 1)
                dve.wait_ge(exps, 1)
                link(dve.tensor_reduce(red2[:, 0:H // 2], w3, AX.X, ALU.add))
                link(dve.reciprocal(red[:, 0:H // 2], red2[:, 0:H // 2]))
                return w3

            link(by_head(big2, w("a0_se")))
            layernorm(1).then_inc(S["ln_xn"], 1)
            take_xt(1)
            link(dve.tensor_scalar(ngb[:, :], w("a0_gb"), -1.0, None, ALU.mult))
            dve.wait_ge(T["qkv_done"], 1)
            link(dve.tensor_scalar(kT[:, :], misc[:, 128:192], w("a0_bk"), None, ALU.add))
            dve.tensor_scalar(qT[:, :], misc[:, 64:128], w("a0_bq"), None, ALU.add).then_inc(T["se_bd"], 1)
            dve.wait_ge(T["se_bd"], 1)
            link(dve.tensor_tensor(v512[:, 0:D], misc[:, 256:384], w("a0_bv"), ALU.add))
            by_head(big, kT[:, :]).then_inc(T["kbd_ready"], 1)
            dve.memset(small[:, 0:1], 1.0 / NQ).then_inc(T["qk_ready"], 1)
            link(dve.memset(vbd, 0.0))
            block_v(T["v_ready"])
            dve.wait_ge(T["v_ready"], 2)
            dve.wait_ge(T["s_done"], 1)
            dve.wait_ge(S["se_in"], 32)
            link(dve.tensor_tensor(w512[:, :], sexp[0][:, 0:512], qf[:, :], ALU.mult))
            dve.wait_ge(S["bias_in"], 32)
            link(dve.tensor_tensor(w512[:, :], w512[:, :], bias_t[:, :], ALU.add))
            w3 = softmax_heads(T["exp_ready"], T["exps"])
            link(dve.tensor_tensor(red[:, 0:H // 2], red[:, 0:H // 2], w("a0_gain"), ALU.mult))
            dve.tensor_tensor(w3, w3, red[:, 0:H // 2].unsqueeze(2).to_broadcast([P, H // 2, NQ]), ALU.mult
                              ).then_inc(T["p_ready"], 1)
            dve.wait_ge(T["gate_e"], 1)
            link(dve.tensor_scalar(gt[:, :], gt[:, :], 1.0, None, ALU.add))
            link(dve.reciprocal(gt[:, :], gt[:, :]))
            dve.wait_ge(T["pt_done"], 1)
            dve.tensor_copy(v512[:, :], sexp[0][:, 512:1024]).then_inc(T["pt_ready"], 1)
            dve.wait_ge(T["ot2_done"], 1)
            dve.tensor_tensor(ogT[:, :], misc[:, 384:448], gt[:, :], ALU.mult).then_inc(T["og_ready"], 1)
            dve.wait_ge(T["y2_done"], 1)
            link(dve.tensor_tensor(x[:, :], acc[0:NQ, D:2 * D], x[:, :], ALU.add))
            link(dve.tensor_tensor(x[:, :], x[:, :], w("a0_bo"), ALU.add))

            layernorm(2).then_inc(S["ln_xn"], 1)
            take_xt(2)
            dve.wait_ge(T["r_done"], 1)

            def first_of_max(logits, rows, n, mxcol, out):
                link(dve.tensor_reduce(mxcol, logits, AX.X, ALU.max))
                link(dve.tensor_scalar(onehot[rows, 0:n], logits, mxcol, None, ALU.is_equal))
                link(dve.tensor_tensor(onehot[rows, 0:n], onehot[rows, 0:n], tie_row(rows, n), ALU.mult))
                link(dve.tensor_reduce(small[rows, 3:4], onehot[rows, 0:n], AX.X, ALU.max))
                return dve.tensor_scalar(out, onehot[rows, 0:n], small[rows, 3:4], None, ALU.is_equal)

            def tie_row(rows, n):
                return w("tie")[rows, E0 - n:E0]

            R = slice(0, P)
            first = dve.tensor_reduce(small[R, 1:2], misc[R, 64:64 + E0], AX.X, ALU.max)
            first.then_inc(T["r_e"], 1)
            dve.wait_ge(T["r_e"], 1)
            link(first_of_max(misc[R, 64:64 + E0], R, E0, small[R, 5:6], onehot2[R, :]))
            dve.tensor_tensor(routing, onehot2[R, :].unsqueeze(2).to_broadcast([P, E0, NQ]),
                              w("ident2").unsqueeze(1).to_broadcast([P, E0, NQ]), ALU.mult
                              ).then_inc(T["route_ready"], 1)
            dve.wait_ge(T["r_e"], 2)
            link(dve.tensor_scalar(small[R, 2:3], small[R, 2:3], 1.0, None, ALU.add))
            link(dve.reciprocal(small[R, 6:7], small[R, 2:3]))
            dve.tensor_scalar(xz[:, :], xn[:, :], small[0:NQ, 6:7], None, ALU.mult).then_inc(T["route_ready"], 1)
            dve.wait_ge(T["xm_done"], 1)
            dve.tensor_copy(big2[:, :], sexp[0][:, :]).then_inc(T["xm_ready"], 1)

            def silu(v, gate, up, out):
                link(dve.tensor_scalar(v, v, 1.0, None, ALU.add))
                link(dve.reciprocal(v, v))
                link(dve.tensor_tensor(v, gate, v, ALU.mult))
                return dve.tensor_tensor(out, up, v, ALU.mult)

            dve.wait_ge(T["sh_e"], 1)
            silu(v512[0:NQ, F0:2 * F0], sexp[1][0:NQ, 2 * F0:3 * F0], sexp[1][0:NQ, 3 * F0:4 * F0],
                 w512[0:NQ, F0:2 * F0]).then_inc(T["sh_ready"], 1)
            dve.wait_ge(T["h_e"], 1)
            silu(v512[:, 0:F0], sexp[1][:, 0:F0], sexp[1][:, F0:2 * F0], w512[:, 0:F0]).then_inc(T["a_ready"], 1)
            dve.wait_ge(T["at_done"], 1)
            dve.tensor_copy(big2[:, :], sexp[0][:, :]).then_inc(T["at_ready"], 1)
            dve.wait_ge(T["yf_done"], 1)
            link(dve.tensor_copy(xz[:, :], acc[NQ:P, D:2 * D]))
            link(dve.tensor_tensor(x[:, :], acc[0:NQ, D:2 * D], x[:, :], ALU.add))
            link(dve.tensor_tensor(x[:, :], x[:, :], xz[:, :], ALU.add))

            layernorm(3).then_inc(S["ln_xn"], 1)
            take_xt(3)
            for stage in range(STAGES):
                stack_q(1, stage)
            cross(1)
            cross_out(1)

            layernorm(4).then_inc(S["ln_xn"], 1)
            take_xt(4)
            dve.wait_ge(T["b_qkv_done"], 1)
            s4 = w("a1_s")
            link(dve.tensor_scalar(kT[:, :], misc[:, 128:192], s4[:, 1:2], w("a1_bk"), ALU.mult, ALU.add))
            link(dve.tensor_scalar(qT[:, :], misc[:, 64:128], s4[:, 0:1], w("a1_bq"), ALU.mult, ALU.add))
            link(dve.tensor_scalar(qT[:, :], qT[:, :], SCALE, None, ALU.mult))
            link(dve.scalar_tensor_tensor(v512[:, 0:D], misc[:, 256:384], s4[:, 2:3], w("a1_bv"), ALU.mult, ALU.add))
            by_head(big, kT[:, :]).then_inc(T["b_kbd_ready"], 1)
            link(dve.memset(vbd, 0.0))
            block_v(T["b_v_ready"])
            dve.wait_ge(T["b_s_done"], 1)
            link(dve.tensor_copy(w512[:, :], sexp[0][:, 0:512]))
            w3 = softmax_heads(T["b_exp_ready"], T["b_exps"])
            dve.tensor_tensor(w3, w3, red[:, 0:H // 2].unsqueeze(2).to_broadcast([P, H // 2, NQ]), ALU.mult
                              ).then_inc(T["b_p_ready"], 1)
            dve.wait_ge(T["b_pt_done"], 1)
            dve.tensor_copy(v512[:, :], sexp[0][:, 512:1024]).then_inc(T["b_pt_ready"], 1)
            dve.wait_ge(T["b_ot_done"], 1)
            dve.tensor_copy(ogT[:, :], misc[:, 384:448]).then_inc(T["b_og_ready"], 1)
            dve.wait_ge(T["b_y_done"], 1)
            link(dve.scalar_tensor_tensor(x[:, :], acc[0:NQ, D:2 * D], s4[0:NQ, 3:4], x[:, :], ALU.mult, ALU.add))
            link(dve.tensor_tensor(x[:, :], x[:, :], w("a1_bo"), ALU.add))

            link(layernorm(5))
            link(layernorm(6, xn[:, :]))
            link(dve.tensor_tensor(xn[:, :], xn[:, :], w("f1_lng"), ALU.mult))
            dve.tensor_tensor(xz[:, :], xn[:, :], w("f1_lnb"), ALU.add).then_inc(T["z_ready"], 1)
            bn = w("f1_bn")
            dve.wait_ge(T["bn_rs"], 1)
            link(dve.reciprocal(bnr[:, 0:1], bnr[:, 0:1]))
            dve.wait_ge(T["zt_done"], 1)
            link(dve.tensor_scalar(red[:, 2:3], misc[:, 64:65], bn[:, 2:3], bnr[:, 0:1], ALU.subtract, ALU.mult))
            link(dve.tensor_scalar(red[:, 3:4], red[:, 2:3], bn[:, 0:1], bn[:, 1:2], ALU.mult, ALU.add))
            link(dve.memset(big2[:, 0:P], 1.0))
            dve.tensor_scalar(w512[:, 0:P], big2[:, 0:P], red[:, 3:4], None, ALU.mult).then_inc(T["zb_ready"], 1)
            dve.tensor_copy(qT[:, :], misc[:, 128:192]).then_inc(T["zt_ready"], 1)
            dve.wait_ge(T["g_done"], 1)
            A = slice(0, P)
            link(dve.tensor_tensor(red2[:, 0:E1], sexp[0][:, 0:E1], w("f1_br"), ALU.add))
            link(first_of_max(red2[:, 0:E1], A, E1, small[:, 5:6], onehot2[:, 0:E1]))
            dve.tensor_scalar(red[:, 0:E1], red2[:, 0:E1], small[:, 5:6], None, ALU.subtract).then_inc(T["g_ready"], 1)
            oh = onehot2[:, 0:E1]

            def select(name, n, rows, out):
                src = w(name).rearrange("p (n e) -> p n e", e=E1)
                link(dve.tensor_tensor(big[0:rows, 0:n * E1].rearrange("p (n e) -> p n e", e=E1), src,
                                       oh[0:rows, :].unsqueeze(1).to_broadcast([rows, n, E1]), ALU.mult))
                return dve.tensor_reduce(out, big[0:rows, 0:n * E1].rearrange("p (n e) -> p n e", e=E1), AX.X, ALU.add)

            link(select("f1_wd", F1, D, v512[:, 0:F1]))
            select("f1_wu", D, F1, v512[0:F1, 128:256]).then_inc(T["wsel_ready"], 1)
            dve.wait_ge(T["wsel_ready"], 1)
            link(dve.tensor_tensor(big[0:F1, 0:E1], w("f1_bd")[:, 0:E1], oh[0:F1, :], ALU.mult))
            link(dve.tensor_reduce(small[0:F1, 8:9], big[0:F1, 0:E1], AX.X, ALU.add))
            dve.wait_ge(T["h1_done"], 1)
            dve.tensor_scalar(kT[0:F1, :], acc[0:F1, 0:NQ], small[0:F1, 8:9], 0.0, ALU.add, ALU.max).then_inc(T["h1_ready"], 1)
            link(select("f1_bu", D, NQ, v512[0:NQ, 256:384]))
            dve.wait_ge(T["g_e"], 1)
            link(dve.reciprocal(small[:, 7:8], small[:, 4:5]))
            dve.wait_ge(T["y1_done"], 1)
            link(dve.tensor_tensor(xz[:, :], sexp[1][0:NQ, 0:D], v512[0:NQ, 256:384], ALU.add))
            dve.scalar_tensor_tensor(x[:, :], xz[:, :], small[0:NQ, 7:8], x[:, :], ALU.mult, ALU.add
                                     ).then_inc(T["out_ready"], 1)

        @block.gpsimd
        def _(pool):
            def take_mask(first, last):
                cs = slice(first * CW, last * CW)
                pool.tensor_scalar(maskadd[:, cs], mask_u8[:, cs], -MASKED, MASKED, ALU.mult, ALU.add
                                   ).then_inc(S["mask_ready"], last - first)

            def take_q(L):
                pool.wait_ge(LS[L]["qstack_ready"], 2)
                pool.tensor_copy(qmax[0:ROWS, 0, :], qstack[0:ROWS, 0, :, :].rearrange("p e n -> p (e n)")
                                 ).then_inc(LS[L]["qmax_ready"], 1)

            def split_k(L):
                q = LS[L]
                for c in range(NCH):
                    if c >= NCH // 2:
                        take_mask(c, c + 1)
                    if c == NCH - 1:
                        take_q(0)
                    cs = slice(c * CW, (c + 1) * CW)
                    pool.wait_ge(q["kmid_done"], c + 1)
                    pool.tensor_tensor(kpart[:, 2, cs], kres[:, c % 2, :], kpart[:, 1, cs], ALU.subtract
                                       ).then_inc(q["klow_done"], 1)

            def split_k_ahead():
                q = LS[1]
                for c in range(NCH + 1):
                    if c < NCH:
                        pool.wait_ge(q["kproj_taken"], c + 1)
                        pool.tensor_tensor(kres[:, c % 2, :], kres[:, c % 2, :], kpart[:, 0, c * CW:(c + 1) * CW],
                                           ALU.subtract).then_inc(q["krest_ready"], 1)
                    if c:
                        cs = slice((c - 1) * CW, c * CW)
                        pool.wait_ge(q["kmid_done"], c)
                        pool.tensor_tensor(kpart[:, 2, cs], kres[:, (c - 1) % 2, :], kpart[:, 1, cs], ALU.subtract
                                           ).then_inc(q["klow_done"], 1)

            def cross(L):
                q = LS[L]
                qflat = qstack[:, :, :, :].rearrange("p a e n -> p (a e n)")
                vflat = vones[:, :, :, :].rearrange("p t a c -> p t (a c)")

                def one(pair, b, first):
                    qs = qflat[0:ROWS, pair * P:(pair + 1) * P] if isinstance(pair, int) else \
                        qflat[0:ROWS, bass.ds(pair * P, P)]
                    vs = vflat[:, :, pair * VC:(pair + 1) * VC] if isinstance(pair, int) else \
                        vflat[:, :, bass.ds(pair * VC, VC)]
                    pool.wait_ge(q["qstack_ready"], 2)
                    if not first:
                        pool.wait_ge(q["smax_done"], (pair - 1) * NCH)
                        pool.sem_inc(q["pool_passed"], 1)
                    if L or not first or b:
                        pool.tensor_copy(qmax[0:ROWS, b, :], qs).then_inc(q["qmax_ready"], 1)
                    pool.wait_ge(q["qstack_ready"], 2)
                    if not first:
                        pool.wait_ge(q["sexp_done"], (pair - 1) * STEPS)
                        pool.sem_inc(q["pool_passed"], 1)
                    pool.tensor_copy(qexp[0:ROWS, b, :], qs).then_inc(q["qexp_ready"], 1)
                    pool.wait_ge(q["vproj_taken"], V1_GROUPS if L else STEPS)
                    if not first:
                        pool.wait_ge(q["pv_done"], (pair - 1) * STEPS + 2)
                        pool.sem_inc(q["pool_passed"], 1)
                    pool.tensor_copy(vcur[:, b, :, :], vs).then_inc(q["vcur_ready"], 1)

                pool.wait_ge(S["vones_ready"], 1)
                one(0, 0, True)
                one(1, 1, True)
                with pool.Fori(1, PAIRS // 2) as i:
                    one(i * 2, 0, False)
                    one(i * 2 + 1, 1, False)

            pool.memset(vones[:, :, :, 2 * HD:VC], 1.0).then_inc(S["vones_ready"], 1)
            pool.wait_ge(S["mask_in"], 32)
            take_mask(0, NCH // 2)
            split_k(0)
            pool.wait_ge(S["mask_ready"], NCH)
            cross(0)
            split_k_ahead()
            pool.wait_ge(T["h_done"], 1)
            cross(1)


OFFSETS = sorted(set(range(33)) | {48, 64, 96, 128, 192})


def kernel(**inputs):
    import ml_dtypes
    import numpy as np
    import concourse.bacc as bacc
    from concourse.bass_utils import run_bass_kernel_spmd

    a = {k: np.asarray(v) for k, v in inputs.items()}
    rows = lambda v, n=P: np.broadcast_to(np.asarray(v).reshape(1, -1), (n, np.asarray(v).size))
    col = lambda v: np.asarray(v).reshape(-1, 1)
    pair_rows = np.array([[(2 * p + e) * HD + d for _ in range(TERMS) for e in range(2) for d in range(HD)]
                          for p in range(PAIRS)])

    def by_pairs(m):
        return m.T[:, pair_rows.reshape(-1)]

    def out_pairs(m):
        return m.T.reshape(PAIRS, 2, HD, D).transpose(0, 2, 1, 3).reshape(NQ, 2 * D)

    sel = np.zeros((ROWS, 4), np.float32)
    for r in range(ROWS):
        sel[r, 0] = -(Q_TERM[r // 16] > 0)
        sel[r, 1] = -(Q_TERM[r // 16] > 1)
        sel[r, 2 + (r % 16) // HD] = 1
    sum4 = np.zeros((P, VC), np.float32)
    for g in range(4):
        sum4[32 * g + np.arange(VC), np.arange(VC)] = 1
    hmask = (np.arange(P)[:, None] // HD == np.arange(H)[None, :]).astype(np.float32)
    near = [o for o in OFFSETS if o < NQ]
    at = [NQ - 1 - o for o in near]
    se = np.zeros((HD, NQ), np.float32)
    se[:, at] = a["L0_attn_scale_embed"][:len(near)].T
    bias = np.full((H, P), NEG, np.float32)
    bias[:, at] = a["L0_attn_pos_bias"][:len(near)].T
    qkv, qkvb = a["L0_attn_qkv_w"], a["L0_attn_qkv_b"]
    gain = a["L0_attn_if_gain"].reshape(2, 1, H // 2)
    parts = {
        "ident": np.eye(P, dtype=np.float32), "hmask": hmask, "sel": sel, "sum4": sum4,
        "eps": np.full((P, 1), LN_EPS, np.float32), "tie": rows(np.arange(E0, 0, -1).astype(np.float32)),
        "zero": np.zeros((P, 1), np.float32), "ident2": np.tile(np.eye(NQ, dtype=np.float32), (2, 1)),
        "a0_wq": qkv[0:D].T, "a0_wk": qkv[D:2 * D].T, "a0_wv": qkv[2 * D:].T,
        "a0_bq": col(qkvb[0:D]), "a0_bk": col(qkvb[D:2 * D]), "a0_bv": rows(qkvb[2 * D:]),
        "a0_se": np.tile(se, (H, 1)), "a0_gw": a["L0_attn_gate_w"].T, "a0_gb": col(a["L0_attn_gate_b"]),
        "a0_gain": np.broadcast_to(gain, (2, NQ, H // 2)).reshape(P, H // 2),
        "a0_wo": a["L0_attn_out_w"].T, "a0_bo": rows(a["L0_attn_out_b"], NQ),
        "f0_router": a["L0_ffn_w_router"].T,
        "f0_shared": np.concatenate([a["L0_ffn_w_gate"].T, a["L0_ffn_w_up"].T], 1),
        "f0_wd": a["L0_ffn_w_down"].T.reshape(2, P, D).transpose(1, 0, 2).reshape(P, 2 * D),
        "bk1": col(a["L1_xattn_bk"]), "bq1": a["L1_xattn_bq"][pair_rows].T,
        "bv1": np.repeat(a["L1_xattn_bv"].reshape(PAIRS, 2, HD).transpose(1, 0, 2).reshape(2, NQ), NQ, 0),
        "bo1": rows(a["L1_xattn_bo"], NQ),
        "a1_wq": a["L1_attn_w_q"].T, "a1_wk": a["L1_attn_w_k"].T, "a1_wv": a["L1_attn_w_v"].T, "a1_wo": a["L1_attn_w_o"].T,
        "a1_s": rows(np.stack([a[f"L1_attn_s_{n}"] for n in "qkvo"])),
        "a1_bq": col(a["L1_attn_b_q"]), "a1_bk": col(a["L1_attn_b_k"]),
        "a1_bv": rows(a["L1_attn_b_v"]), "a1_bo": rows(a["L1_attn_b_o"], NQ),
        "f1_lng": rows(a["L1_ffn_ln_g"], NQ), "f1_lnb": rows(a["L1_ffn_ln_b"], NQ),
        "f1_bn": np.stack([a[f"L1_ffn_bn_{n}"] for n in ("g", "b", "mean", "var")], 1),
        "f1_wr": a["L1_ffn_Wr"], "f1_br": rows(a["L1_ffn_br"]),
        "f1_wd": a["L1_ffn_W_down"].transpose(1, 2, 0).reshape(D, F1 * E1), "f1_bd": a["L1_ffn_b_down"].T,
        "f1_wu": a["L1_ffn_W_up"].transpose(1, 2, 0).reshape(F1, D * E1), "f1_bu": rows(a["L1_ffn_b_up"].T, NQ),
    }
    for L in range(2):
        parts[f"wq{L}"] = by_pairs(a[f"L{L}_xattn_Wq"])
        parts[f"wk{L}"] = a[f"L{L}_xattn_Wk"].T
        parts[f"wv{L}"] = a[f"L{L}_xattn_Wv"].T
        parts[f"wo{L}"] = out_pairs(a[f"L{L}_xattn_Wo"])
    packs = []
    for cols, width in pack_layout():
        pack = np.zeros((P, width), np.float32)
        for name, (c, n, r) in cols.items():
            assert parts[name].shape == (r, n), (name, parts[name].shape, (r, n))
            pack[:r, c:c + n] = parts[name]
        packs.append(pack)
    arrays = {
        "x_in": a["x"][0], "ctx_in": np.ascontiguousarray(a["ctx_1024"][0].T),
        "mask_in": np.ascontiguousarray(a["mask_SxS2_bk0"]),
        "pack1_in": packs[0], "pack2_in": packs[1], "bias_in": np.ascontiguousarray(np.broadcast_to(bias, (NQ, H, P))),
        "gup_in": np.ascontiguousarray(a["L0_ffn_gate_up_proj"].transpose(1, 0, 2)),
        "down_in": np.ascontiguousarray(a["L0_ffn_down_proj"].reshape(E0, 2, P, D).transpose(2, 1, 0, 3)),
        "ones_in": np.ones((3, 2 * NK), ml_dtypes.bfloat16),
    }
    nc = bacc.Bacc("TRN2", target_bir_lowering=False, num_devices=1)
    aps = [nc.dram_tensor(n, v.shape, mybir.dt.from_np(v.dtype), kind="ExternalInput").ap() for n, v in arrays.items()]
    skew = nc.dram_tensor("skew", (NQ * H * NQ,), F32, kind="Internal").ap()
    out = nc.dram_tensor("x_out", (1, NQ, D), F32, kind="ExternalOutput").ap()
    perceiver(nc, *aps, skew, out[0])
    r = run_bass_kernel_spmd(nc, [arrays], core_ids=[0])
    return r.results[0]["x_out"]
```
